# Optimizing a Trainium2 kernel written in Bass

```python
import numpy as np
import jax
import jax.numpy as jnp

def _softmax(x, axis=-1):
    return jax.nn.softmax(x, axis=axis)

def _gelu(x):
    return jax.nn.gelu(x, approximate=True)

def _silu(x):
    return jax.nn.silu(x)

def _sigmoid(x):
    return jax.nn.sigmoid(x)

def _layernorm(x, axis=-1, eps=1e-05):
    m = jnp.mean(x, axis=axis, keepdims=True)
    v = jnp.var(x, axis=axis, keepdims=True)
    return (x - m) / jnp.sqrt(v + eps)

def _scatter_add(tgt, idx, src, axis=0):
    return tgt.at[idx].add(src)

def _segment_sum(src, seg, n):
    return jax.ops.segment_sum(src, seg, n)
kernel_name = 'mk_decoder_postln_d1_seqx_r8_b2810e'

def setup_inputs(seed: int=0):
    np.random.seed(seed)
    _w = jnp.asarray

    def _rec_inputs():
        import jax
        import jax.numpy as jnp
        _rk = jax.random.key(seed)
        x = 7.22e-05 + 1 * jax.random.normal(jax.random.fold_in(_rk, 1), (4, 512, 128), jnp.float32)
        _lenS = 512 - jax.random.randint(jax.random.fold_in(_rk, 7), (4,), 0, max(1, 512 // 4) + 1, jnp.int32)
        _lenS2 = 32 - jax.random.randint(jax.random.fold_in(_rk, 8), (4,), 0, max(1, 32 // 4) + 1, jnp.int32)
        _ctx_768P = jax.random.normal(jax.random.fold_in(_rk, 11), (4, 16, 96), jnp.float32)
        _ctx_768c = jax.random.dirichlet(jax.random.fold_in(_rk, 511), 0.3 * jnp.ones((16,), jnp.float32), (4, 32))
        _ctx_768t = jnp.einsum('bsk,bkd->bsd', _ctx_768c, _ctx_768P)
        _ctx_768t = _ctx_768t * jax.lax.rsqrt(jnp.mean(jnp.square(_ctx_768t)) + 1e-12) * 0.953939
        ctx_768 = 3.88148e-05 + 0.999967 * (_ctx_768t + 0.3 * jax.random.normal(jax.random.fold_in(_rk, 611), (4, 32, 96), jnp.float32))
        _validS = jnp.arange(512)[None, :] < _lenS[:, None]
        _validS2 = jnp.arange(32)[None, :] < _lenS2[:, None]
        _causal = jnp.tril(jnp.ones((512, 512), dtype=bool))
        mask_BxS_bf1 = jnp.ones((4, 512), dtype=bool)
        mask_BxS2_bf1 = jnp.ones((4, 32), dtype=bool)
        return (x, ctx_768, mask_BxS_bf1, mask_BxS2_bf1)
    x, ctx_768, mask_BxS_bf1, mask_BxS2_bf1 = _rec_inputs()

    def _L0_attn_setup():
        import jax, jax.numpy as jnp
        import numpy as np
        D_MODEL = 128
        N_HEADS = 16
        N_KV = 4
        HEAD_DIM = D_MODEL // N_HEADS
        SEQ = 256
        BATCH = 2
        CAP = 50.0
        EPS = 1e-05
        THETA = 10000.0

        def _rms_norm(x, eps=EPS):
            return x * jax.lax.rsqrt(jnp.mean(jnp.square(x), axis=-1, keepdims=True) + eps)

        def _rope_cos_sin(seq_len, head_dim, theta=THETA):
            inv_freq = 1.0 / theta ** (jnp.arange(0, head_dim, 2, dtype=jnp.float32) / head_dim)
            freqs = jnp.arange(seq_len, dtype=jnp.float32)[:, None] * inv_freq[None, :]
            return (jnp.cos(freqs)[None, :, None, :], jnp.sin(freqs)[None, :, None, :])

        def _apply_rope(x, cos, sin):
            d = x.shape[-1] // 2
            x1, x2 = (x[..., :d], x[..., d:])
            return jnp.concatenate([x1 * cos - x2 * sin, x2 * cos + x1 * sin], axis=-1).astype(x.dtype)
        key = jax.random.key(seed)
        ks = jax.random.split(key, 5)
        s = 0.02
        return {'x': jax.random.normal(ks[0], (BATCH, SEQ, D_MODEL), dtype=jnp.float32), 'w_q': jax.random.normal(ks[1], (D_MODEL, N_HEADS * HEAD_DIM), dtype=jnp.float32) * s, 'w_k': jax.random.normal(ks[2], (D_MODEL, N_KV * HEAD_DIM), dtype=jnp.float32) * s, 'w_v': jax.random.normal(ks[3], (D_MODEL, N_KV * HEAD_DIM), dtype=jnp.float32) * s, 'w_o': jax.random.normal(ks[4], (N_HEADS * HEAD_DIM, D_MODEL), dtype=jnp.float32) * s}
    _L0_attn_all = _L0_attn_setup()
    _L0_attn_in = {k: v for k, v in _L0_attn_all.items() if k in ('w_q', 'w_k', 'w_v', 'w_o')}
    del _L0_attn_all

    def _L0_xattn_setup():
        import jax, jax.numpy as jnp
        import numpy as np
        B, T, DT, G, DV = (16, 64, 128, 72, 96)
        H, DH = (4, 32)
        INNER = H * DH
        HID = 4 * DT
        N_STATE = 64
        K_TOP = 32

        def layernorm(x, g, b, eps=1e-05):
            m = x.mean(-1, keepdims=True)
            v = x.var(-1, keepdims=True)
            return (x - m) * jax.lax.rsqrt(v + eps) * g + b

        def s4d(x, log_dt, A_re, A_im, C_re, C_im, D_skip):
            Bb, L, D = x.shape
            dt = jnp.exp(log_dt)
            A = A_re + 1j * A_im
            C = C_re + 1j * C_im
            dtA = dt[:, None] * A
            dC = C * (jnp.exp(dtA) - 1.0) / A
            powers = jnp.exp(dtA[:, :, None] * jnp.arange(L))
            K = 2.0 * jnp.einsum('dn,dnl->dl', dC, powers).real
            n = 2 * L
            Kf = jnp.fft.rfft(K, n=n, axis=-1)
            xf = jnp.fft.rfft(x, n=n, axis=1)
            y = jnp.fft.irfft(xf * Kf.T[None], n=n, axis=1)[:, :L]
            return y + x * D_skip
        key = jax.random.key(seed)
        ks = jax.random.split(key, 16)
        s = 0.02
        inp = {'x_text': jax.random.normal(ks[0], (B, T, DT), jnp.float32), 'x_vision': jax.random.normal(ks[1], (B, G, DV), jnp.float32), 'text_mask': jnp.ones((B, T), bool), 'vision_mask': jnp.ones((B, G), bool), 'Wq': jax.random.normal(ks[2], (DT, INNER), jnp.float32) * s, 'Wk': jax.random.normal(ks[3], (DV, INNER), jnp.float32) * s, 'Wv': jax.random.normal(ks[4], (DV, DT), jnp.float32) * s, 'W_film_in': jax.random.normal(ks[5], (DT, 2 * DT), jnp.float32) * s, 'b_film_in': jnp.zeros((2 * DT,), jnp.float32), 'W_film_out': jax.random.normal(ks[6], (DT, 2 * DT), jnp.float32) * s, 'b_film_out': jnp.zeros((2 * DT,), jnp.float32), 'g_norm_in': jnp.ones((DT,), jnp.float32), 'b_norm_in': jnp.zeros((DT,), jnp.float32), 'g_norm_out': jnp.ones((DT,), jnp.float32), 'b_norm_out': jnp.zeros((DT,), jnp.float32), 'g_ffn': jnp.ones((DT,), jnp.float32), 'b_ffn': jnp.zeros((DT,), jnp.float32), 'W1': jax.random.normal(ks[7], (DT, HID), jnp.float32) * s, 'b1': jnp.zeros((HID,), jnp.float32), 'W2': jax.random.normal(ks[8], (HID, DT), jnp.float32) * s, 'b2': jnp.zeros((DT,), jnp.float32), 'log_dt': jnp.log(0.001) + jax.random.uniform(ks[9], (DT,), jnp.float32) * (jnp.log(0.1) - jnp.log(0.001)), 'A_re': -0.5 * jnp.ones((DT, N_STATE), jnp.float32), 'A_im': jnp.tile(jnp.pi * jnp.arange(N_STATE, dtype=jnp.float32), (DT, 1)), 'C_re': jax.random.normal(ks[10], (DT, N_STATE), jnp.float32) * 0.5 ** 0.5, 'C_im': jax.random.normal(ks[11], (DT, N_STATE), jnp.float32) * 0.5 ** 0.5, 'D_skip': jax.random.normal(ks[12], (DT,), jnp.float32), 'mod_gate': jnp.array(0.5, jnp.float32)}
        return inp
    _L0_xattn_all = _L0_xattn_setup()
    _L0_xattn_in = {k: v for k, v in _L0_xattn_all.items() if k in ('Wq', 'Wk', 'Wv', 'W_film_in', 'b_film_in', 'W_film_out', 'b_film_out', 'g_norm_in', 'b_norm_in', 'g_norm_out', 'b_norm_out', 'g_ffn', 'b_ffn', 'W1', 'b1', 'W2', 'b2', 'log_dt', 'A_re', 'A_im', 'C_re', 'C_im', 'D_skip', 'mod_gate')}
    del _L0_xattn_all

    def _L0_ffn_setup():
        import jax, jax.numpy as jnp
        import numpy as np
        D_MODEL = 128
        HIDDEN = 512
        NUM_EXPERTS = 8
        TOP_K = 2
        NUM_SHARED = 2

        def _gelu(x):
            return jax.nn.gelu(x, approximate=False)
        key = jax.random.key(seed)
        ks = jax.random.split(key, 12)
        s = 0.02
        return {'x': jax.random.normal(ks[0], (2, 256, D_MODEL), dtype=jnp.float32), 'rW': jax.random.normal(ks[1], (D_MODEL, NUM_EXPERTS), dtype=jnp.float32) * s, 'rb': jnp.zeros((NUM_EXPERTS,), dtype=jnp.float32), 'W1': jax.random.normal(ks[2], (NUM_EXPERTS, D_MODEL, HIDDEN), dtype=jnp.float32) * s, 'b1': jnp.zeros((NUM_EXPERTS, HIDDEN), dtype=jnp.float32), 'W2': jax.random.normal(ks[3], (NUM_EXPERTS, HIDDEN, D_MODEL), dtype=jnp.float32) * s, 'b2': jnp.zeros((NUM_EXPERTS, D_MODEL), dtype=jnp.float32), 'sW1': jax.random.normal(ks[4], (NUM_SHARED, D_MODEL, HIDDEN), dtype=jnp.float32) * s, 'sb1': jnp.zeros((NUM_SHARED, HIDDEN), dtype=jnp.float32), 'sW2': jax.random.normal(ks[5], (NUM_SHARED, HIDDEN, D_MODEL), dtype=jnp.float32) * s, 'sb2': jnp.zeros((NUM_SHARED, D_MODEL), dtype=jnp.float32)}
    _L0_ffn_all = _L0_ffn_setup()
    _L0_ffn_in = {k: v for k, v in _L0_ffn_all.items() if k in ('rW', 'rb', 'W1', 'b1', 'W2', 'b2', 'sW1', 'sb1', 'sW2', 'sb2')}
    del _L0_ffn_all
    return {'x': x, 'ctx_768': ctx_768, 'mask_BxS_bf1': mask_BxS_bf1, 'mask_BxS2_bf1': mask_BxS2_bf1, 'L0_attn_w_q': _L0_attn_in['w_q'], 'L0_attn_w_k': _L0_attn_in['w_k'], 'L0_attn_w_v': _L0_attn_in['w_v'], 'L0_attn_w_o': _L0_attn_in['w_o'], 'L0_xattn_Wq': _L0_xattn_in['Wq'], 'L0_xattn_Wk': _L0_xattn_in['Wk'], 'L0_xattn_Wv': _L0_xattn_in['Wv'], 'L0_xattn_W_film_in': _L0_xattn_in['W_film_in'], 'L0_xattn_b_film_in': _L0_xattn_in['b_film_in'], 'L0_xattn_W_film_out': _L0_xattn_in['W_film_out'], 'L0_xattn_b_film_out': _L0_xattn_in['b_film_out'], 'L0_xattn_g_norm_in': _L0_xattn_in['g_norm_in'], 'L0_xattn_b_norm_in': _L0_xattn_in['b_norm_in'], 'L0_xattn_g_norm_out': _L0_xattn_in['g_norm_out'], 'L0_xattn_b_norm_out': _L0_xattn_in['b_norm_out'], 'L0_xattn_g_ffn': _L0_xattn_in['g_ffn'], 'L0_xattn_b_ffn': _L0_xattn_in['b_ffn'], 'L0_xattn_W1': _L0_xattn_in['W1'], 'L0_xattn_b1': _L0_xattn_in['b1'], 'L0_xattn_W2': _L0_xattn_in['W2'], 'L0_xattn_b2': _L0_xattn_in['b2'], 'L0_xattn_log_dt': _L0_xattn_in['log_dt'], 'L0_xattn_A_re': _L0_xattn_in['A_re'], 'L0_xattn_A_im': _L0_xattn_in['A_im'], 'L0_xattn_C_re': _L0_xattn_in['C_re'], 'L0_xattn_C_im': _L0_xattn_in['C_im'], 'L0_xattn_D_skip': _L0_xattn_in['D_skip'], 'L0_xattn_mod_gate': _L0_xattn_in['mod_gate'], 'L0_ffn_rW': _L0_ffn_in['rW'], 'L0_ffn_rb': _L0_ffn_in['rb'], 'L0_ffn_W1': _L0_ffn_in['W1'], 'L0_ffn_b1': _L0_ffn_in['b1'], 'L0_ffn_W2': _L0_ffn_in['W2'], 'L0_ffn_b2': _L0_ffn_in['b2'], 'L0_ffn_sW1': _L0_ffn_in['sW1'], 'L0_ffn_sb1': _L0_ffn_in['sb1'], 'L0_ffn_sW2': _L0_ffn_in['sW2'], 'L0_ffn_sb2': _L0_ffn_in['sb2']}

def reference(x, ctx_768, mask_BxS_bf1, mask_BxS2_bf1, L0_attn_w_q, L0_attn_w_k, L0_attn_w_v, L0_attn_w_o, L0_xattn_Wq, L0_xattn_Wk, L0_xattn_Wv, L0_xattn_W_film_in, L0_xattn_b_film_in, L0_xattn_W_film_out, L0_xattn_b_film_out, L0_xattn_g_norm_in, L0_xattn_b_norm_in, L0_xattn_g_norm_out, L0_xattn_b_norm_out, L0_xattn_g_ffn, L0_xattn_b_ffn, L0_xattn_W1, L0_xattn_b1, L0_xattn_W2, L0_xattn_b2, L0_xattn_log_dt, L0_xattn_A_re, L0_xattn_A_im, L0_xattn_C_re, L0_xattn_C_im, L0_xattn_D_skip, L0_xattn_mod_gate, L0_ffn_rW, L0_ffn_rb, L0_ffn_W1, L0_ffn_b1, L0_ffn_W2, L0_ffn_b2, L0_ffn_sW1, L0_ffn_sb1, L0_ffn_sW2, L0_ffn_sb2):
    import jax
    import jax.numpy as jnp

    def _L0_attn_ref(x, w_q, w_k, w_v, w_o):
        import jax, jax.numpy as jnp
        import numpy as np
        D_MODEL = 128
        N_HEADS = 16
        N_KV = 4
        HEAD_DIM = D_MODEL // N_HEADS
        SEQ = 256
        BATCH = 2
        CAP = 50.0
        EPS = 1e-05
        THETA = 10000.0

        def _rms_norm(x, eps=EPS):
            return x * jax.lax.rsqrt(jnp.mean(jnp.square(x), axis=-1, keepdims=True) + eps)

        def _rope_cos_sin(seq_len, head_dim, theta=THETA):
            inv_freq = 1.0 / theta ** (jnp.arange(0, head_dim, 2, dtype=jnp.float32) / head_dim)
            freqs = jnp.arange(seq_len, dtype=jnp.float32)[:, None] * inv_freq[None, :]
            return (jnp.cos(freqs)[None, :, None, :], jnp.sin(freqs)[None, :, None, :])

        def _apply_rope(x, cos, sin):
            d = x.shape[-1] // 2
            x1, x2 = (x[..., :d], x[..., d:])
            return jnp.concatenate([x1 * cos - x2 * sin, x2 * cos + x1 * sin], axis=-1).astype(x.dtype)
        B, S, _ = x.shape
        q = (x @ w_q).reshape(B, S, N_HEADS, HEAD_DIM)
        k = (x @ w_k).reshape(B, S, N_KV, HEAD_DIM)
        v = (x @ w_v).reshape(B, S, N_KV, HEAD_DIM)
        q = _rms_norm(q)
        k = _rms_norm(k)
        cos, sin = _rope_cos_sin(S, HEAD_DIM)
        q = _apply_rope(q, cos, sin)
        k = _apply_rope(k, cos, sin)
        rep = N_HEADS // N_KV
        k = jnp.repeat(k, rep, axis=2)
        v = jnp.repeat(v, rep, axis=2)
        scores = jnp.einsum('bqhd,bkhd->bhqk', q, k) / np.sqrt(HEAD_DIM).astype(np.float32)
        scores = jnp.tanh(scores.astype(jnp.float32) / CAP) * CAP
        causal = jnp.tril(jnp.ones((S, S), dtype=bool))
        scores = jnp.where(causal[None, None], scores, -jnp.inf)
        probs = jax.nn.softmax(scores, axis=-1)
        y = jnp.einsum('bhqk,bkhd->bqhd', probs, v).reshape(B, S, N_HEADS * HEAD_DIM)
        return y @ w_o

    def _L0_xattn_ref(x_text, x_vision, text_mask, vision_mask, Wq, Wk, Wv, W_film_in, b_film_in, W_film_out, b_film_out, g_norm_in, b_norm_in, g_norm_out, b_norm_out, g_ffn, b_ffn, W1, b1, W2, b2, log_dt, A_re, A_im, C_re, C_im, D_skip, mod_gate):
        import jax, jax.numpy as jnp
        import numpy as np
        B, T, DT, G, DV = (16, 64, 128, 72, 96)
        H, DH = (4, 32)
        INNER = H * DH
        HID = 4 * DT
        N_STATE = 64
        K_TOP = 32

        def layernorm(x, g, b, eps=1e-05):
            m = x.mean(-1, keepdims=True)
            v = x.var(-1, keepdims=True)
            return (x - m) * jax.lax.rsqrt(v + eps) * g + b

        def s4d(x, log_dt, A_re, A_im, C_re, C_im, D_skip):
            Bb, L, D = x.shape
            dt = jnp.exp(log_dt)
            A = A_re + 1j * A_im
            C = C_re + 1j * C_im
            dtA = dt[:, None] * A
            dC = C * (jnp.exp(dtA) - 1.0) / A
            powers = jnp.exp(dtA[:, :, None] * jnp.arange(L))
            K = 2.0 * jnp.einsum('dn,dnl->dl', dC, powers).real
            n = 2 * L
            Kf = jnp.fft.rfft(K, n=n, axis=-1)
            xf = jnp.fft.rfft(x, n=n, axis=1)
            y = jnp.fft.irfft(xf * Kf.T[None], n=n, axis=1)[:, :L]
            return y + x * D_skip
        Bb, Tt, D = x_text.shape
        Gg = x_vision.shape[1]
        Q = (x_text @ Wq).reshape(Bb, Tt, H, DH)
        K = (x_vision @ Wk).reshape(Bb, Gg, H, DH)
        scores = jnp.einsum('bthd,bghd->bhtg', Q, K) / np.sqrt(DH).astype(np.float32)
        scores = jnp.where(vision_mask[:, None, None, :], scores, -jnp.inf)
        topv, topi = jax.lax.top_k(scores, K_TOP)
        probs = jax.nn.softmax(topv, axis=-1)
        bi = jnp.arange(Bb)[:, None, None, None]
        hi = jnp.arange(H)[None, :, None, None]
        ti = jnp.arange(Tt)[None, None, :, None]
        attn = jnp.zeros_like(scores).at[bi, hi, ti, topi].set(probs)
        attn_mean = attn.mean(axis=1)
        V = x_vision @ Wv
        c_t = jnp.einsum('btg,bgd->btd', attn_mean, V)
        c_t = c_t * text_mask[..., None]
        x = layernorm(x_text, g_norm_in, b_norm_in)
        scale_in, shift_in = jnp.split(c_t @ W_film_in + b_film_in, 2, axis=-1)
        x = x * (1.0 + mod_gate * scale_in) + mod_gate * shift_in
        y = s4d(x, log_dt, A_re, A_im, C_re, C_im, D_skip)
        scale_out, shift_out = jnp.split(c_t @ W_film_out + b_film_out, 2, axis=-1)
        y = y * (1.0 + mod_gate * scale_out) + mod_gate * shift_out
        xt = x_text + y
        h = layernorm(xt, g_ffn, b_ffn)
        h = jax.nn.gelu(h @ W1 + b1, approximate=False) @ W2 + b2
        xt = xt + h
        return layernorm(xt, g_norm_out, b_norm_out)

    def _L0_ffn_ref(x, rW, rb, W1, b1, W2, b2, sW1, sb1, sW2, sb2):
        import jax, jax.numpy as jnp
        import numpy as np
        D_MODEL = 128
        HIDDEN = 512
        NUM_EXPERTS = 8
        TOP_K = 2
        NUM_SHARED = 2

        def _gelu(x):
            return jax.nn.gelu(x, approximate=False)
        B, L, D = x.shape
        xf = x.reshape(-1, D)
        sh = _gelu(jnp.einsum('td,sdh->sth', xf, sW1) + sb1[:, None, :])
        shared = jnp.einsum('sth,shd->std', sh, sW2) + sb2[:, None, :]
        shared = shared.mean(axis=0)
        gates = xf @ rW + rb
        topk_vals, topk_idx = jax.lax.top_k(gates, TOP_K)
        topk_probs = jax.nn.softmax(topk_vals, axis=-1)
        onehot = topk_idx[:, :, None] == jnp.arange(NUM_EXPERTS)[None, None, :]
        w = jnp.sum(topk_probs[:, :, None] * onehot, axis=1)
        h = _gelu(jnp.einsum('td,edh->eth', xf, W1) + b1[:, None, :])
        y = jnp.einsum('eth,ehd->etd', h, W2) + b2[:, None, :]
        moe = jnp.einsum('te,etd->td', w, y)
        return (shared + moe).reshape(B, L, D)
    x = _layernorm(x + _L0_attn_ref(x, L0_attn_w_q, L0_attn_w_k, L0_attn_w_v, L0_attn_w_o), axis=-1)
    x = _layernorm(x + _L0_xattn_ref(x, ctx_768, mask_BxS_bf1, mask_BxS2_bf1, L0_xattn_Wq, L0_xattn_Wk, L0_xattn_Wv, L0_xattn_W_film_in, L0_xattn_b_film_in, L0_xattn_W_film_out, L0_xattn_b_film_out, L0_xattn_g_norm_in, L0_xattn_b_norm_in, L0_xattn_g_norm_out, L0_xattn_b_norm_out, L0_xattn_g_ffn, L0_xattn_b_ffn, L0_xattn_W1, L0_xattn_b1, L0_xattn_W2, L0_xattn_b2, L0_xattn_log_dt, L0_xattn_A_re, L0_xattn_A_im, L0_xattn_C_re, L0_xattn_C_im, L0_xattn_D_skip, L0_xattn_mod_gate), axis=-1)
    x = _layernorm(x + _L0_ffn_ref(x, L0_ffn_rW, L0_ffn_rb, L0_ffn_W1, L0_ffn_b1, L0_ffn_W2, L0_ffn_b2, L0_ffn_sW1, L0_ffn_sb1, L0_ffn_sW2, L0_ffn_sb2), axis=-1)
    return x

_drawn_inputs = setup_inputs


def setup_inputs(seed=0):
    import zlib

    import numpy as np

    out = dict(_drawn_inputs(seed))
    spreads = {'L0_xattn_b_film_in': (0.0, 0.284),
     'L0_xattn_b_film_out': (0.0, 0.355),
     'L0_xattn_g_norm_in': (1.0, 0.2),
     'L0_xattn_b_norm_in': (0.0, 0.1),
     'L0_xattn_g_norm_out': (1.0, 0.2),
     'L0_xattn_b_norm_out': (0.0, 0.1),
     'L0_xattn_g_ffn': (1.0, 0.6),
     'L0_xattn_b_ffn': (0.0, 0.8),
     'L0_xattn_b1': (0.0, 0.737),
     'L0_xattn_b2': (0.0, 0.904),
     'L0_xattn_A_re': (-0.5, 0.2),
     'L0_ffn_rb': (0.0, 0.1),
     'L0_ffn_b1': (0.0, 0.478),
     'L0_ffn_b2': (0.0, 0.1),
     'L0_ffn_sb1': (0.0, 0.485),
     'L0_ffn_sb2': (0.0, 0.1)}
    factors = {'ctx_768': 4.529,
     'L0_attn_w_q': 7.001,
     'L0_attn_w_k': 7.059,
     'L0_attn_w_v': 5.289,
     'L0_attn_w_o': 5.319,
     'L0_xattn_Wq': 8.0,
     'L0_xattn_Wk': 8.0,
     'L0_xattn_Wv': 4.12,
     'L0_xattn_W_film_in': 4.69,
     'L0_xattn_W_film_out': 6.923,
     'L0_xattn_W1': 2.957,
     'L0_xattn_W2': 2.779}
    for name, (base, spread) in spreads.items():
        noise = np.random.default_rng([zlib.crc32(name.encode()), seed]).standard_normal(out[name].shape)
        drawn = base * np.exp(spread * noise) if base else spread * noise
        out[name] = jnp.asarray(drawn.astype(out[name].dtype))
    for name, factor in factors.items():
        out[name] = (out[name] * factor).astype(out[name].dtype)
    return out
```

```python
from contextlib import ExitStack

import numpy as np
import concourse.bass as bass
from concourse import mybir

F32 = mybir.dt.float32
F32R = mybir.dt.float32r
BF16 = mybir.dt.bfloat16
I32 = mybir.dt.int32
U8 = mybir.dt.uint8
ALU = mybir.AluOpType
ACT = mybir.ActivationFunctionType
AX = mybir.AxisListType.X

P = 128
B, SEQ, D = 4, 512, 128
NT = SEQ // P
NH, NKV, HD = 16, 4, 8
QK = (NH + NKV) * HD
QKV = QK + NKV * HD
LAG = 2
CAP, EPS = 50.0, 1e-5
PARTS = 8
G, DV, XH, XD = 32, 96, 4, 32
NS = 64
HID = 512
HC = HID // P
NE, NSH = 8, 2
NM = NSH + NE
NX = 1 + NM
NPAIR = NH // 2
PW = 5 * SEQ
JM, IM = 32, SEQ // 32
MAGIC = 12582912.0
TWO_PI = 6.283185307179586
TURN = 6.283185
SIN_SCALE = TWO_PI * (1 - 2.5e-6)
LN2_HI, LN2_LO = 0.693145751953125, 1.42860682030941723212e-6

ROW_B1, ROW_B2, ROW_LDT = 0, HC * NX, (HC + 1) * NX
ROWS = ROW_LDT + 1
S_QKV, S_QT, S_SC = 0, 2, 8
U_FILM, U_DFT, U_FFN, U_FILLS = 0, 4, 6, 10
U_DVE, U_ACT = 6, 4
NORMS = 6
FILLS = [(r, tiles) for tiles in ([(0, 0)], [(1, 0), (3, 384)], [(2, 0)]) for r in range(2)]
BASE = [0, SEQ, 2 * SEQ, 3 * SEQ, 4 * SEQ, 4 * SEQ + 256]
WIDTH = [SEQ, SEQ, SEQ, SEQ, 256, 256]
NF = len(FILLS)
S_FILLS = S_SC + NF * NPAIR
COL = {(r, j): BASE[n] + c for n, (r, tiles) in enumerate(FILLS) for j, c in tiles}


def build(nc, t, out):
    ctx = ExitStack()
    with ctx:
        def sb(name, shape, dt=F32):
            return ctx.enter_context(nc.sbuf_tensor(name, shape, dt))

        def sem(name):
            return ctx.enter_context(nc.semaphore(name))

        ring_s = [ctx.enter_context(nc.psum_tensor(f"ring_s{i}", [P, 512], F32)) for i in range(2)]
        ring_u = [ctx.enter_context(nc.psum_tensor(f"ring_u{i}", [P, 512], F32)) for i in range(2)]
        bank_o = ctx.enter_context(nc.psum_tensor("bank_o", [P, 512], F32))
        bank_m = ctx.enter_context(nc.psum_tensor("bank_m", [P, 512], F32))
        bank_d = ctx.enter_context(nc.psum_tensor("bank_d", [P, 512], F32))
        bank_r = ctx.enter_context(nc.psum_tensor("bank_r", [P, 512], F32))
        down = [bank_d, bank_r]
        ring_up = [ring_s[0], ring_s[1], ring_u[0], ring_u[1]]

        wqkv = sb("wqkv", [P, QKV])
        wo = sb("wo", [P, D])
        ident = sb("ident", [P, P])
        identb = sb("identb", [P, P], BF16)
        pair_sum = sb("pair_sum", [P, 64])
        rope = sb("rope", [P, NT, 2, HD])
        wt_hi = sb("wt_hi", [P, 2 * HID], F32R)
        wt_lo = sb("wt_lo", [P, 2 * HID], F32R)
        vcols = sb("vcols", [P, ROWS])
        b2_shared = sb("b2_shared", [P, 1])
        norms = sb("norms", [P, 6, D])
        film_bias = sb("film_bias", [P, 4 * D])
        router_w = sb("router_w", [P, NE])
        router_b = sb("router_b", [P, NE])
        earlier = sb("earlier", [P, NE, NE])
        spread = sb("spread", [2 * NE, NE], F32R)
        neg_half = sb("neg_half", [P, NT * (NH + NKV)])
        cosm = sb("cosm", [P, NT, SEQ])
        sin_fwd = sb("sin_fwd", [P, NT, SEQ])
        sin_inv = sb("sin_inv", [P, NT, SEQ])
        kc = sb("kc", [P, NT, D])
        ks = sb("ks", [P, NT, D])
        kcn = sb("kcn", [P, NT, D])
        xq = sb("xq", [P, B, XH * G])
        vf = sb("vf", [P, B, 4 * D])
        ctx_bias = sb("ctx_bias", [P, B, XH, G])
        tmask = sb("tmask", [P, B * NT])
        gate = sb("gate", [P, 1])
        gate4 = sb("gate4", [P, 1])

        x2 = sb("x2", [P, B, NT * D])
        t_hi = sb("t_hi", [P, B, SEQ], F32R)
        t_lo = sb("t_lo", [P, B, SEQ], F32R)
        wT = sb("wT", [2 * NE, B, SEQ], F32R)
        g_raw = sb("g_raw", [P, 2, SEQ])
        g_hi = sb("g_hi", [P, HC, SEQ], F32R)
        g_lo = sb("g_lo", [P, HC, SEQ], F32R)
        fa = sb("fa", [P, NT, D])
        stats = sb("stats", [P, NT, 6])
        mean_var = sb("mean_var", [P, NT, 2])
        var_eps = sb("var_eps", [P, NT])
        rstd = sb("rstd", [P, NT])

        experts = ExitStack()
        with experts:
            def eb(name, shape, dt=F32):
                return experts.enter_context(nc.sbuf_tensor(name, shape, dt))
            w_hi = eb("w_hi", [P, 2, 2 * HID], F32R)
            w_lo = eb("w_lo", [P, 2, 2 * HID], F32R)
            e_raw = eb("e_raw", [P, 2, 2 * HID])
            acc = eb("acc", [P, B, SEQ])
            w_bc = eb("w_bc", [P, 2, SEQ])
            term = eb("term", [P, SEQ])
            y_out = eb("y_out", [P, B, NT, D])

        x_in = sb("x_in", [P, NT, D])
        xT = sb("xT", [P, SEQ])
        qkv = sb("qkv", [P, NT, QKV])
        qT = sb("qT", [P, NPAIR, SEQ], BF16)
        kT = sb("kT", [P, NKV, SEQ], BF16)
        vv = sb("vv", [P, NT, NKV, 32])
        probs = sb("probs", [P, 2, PW])
        oT = sb("oT", [P, 2, SEQ])
        ry = sb("ry", [P, NT, 2])
        y_att = sb("y_att", [P, NT, D])
        yT = xT
        qs = probs[:, 1, 0:NT * NH * PARTS * HD // 2].bitcast(BF16).rearrange("p (n c e) -> p n c e", c=PARTS, e=HD)
        kbd = probs[:, 0, 0:B * XH * G]
        kij = probs[0:IM, :, :].rearrange("i s c -> i (s c)")[:, 0:JM * D].rearrange("i (j d) -> i j d", j=JM)
        tmp_a = probs[:, 0, 0:640]
        tmp_b = probs[:, 0, 640:1280]
        tmp_c = probs[:, 0, 1280:1920]
        k_parts = sb("k_parts", [P, NT * NKV, 2, PARTS, HD], BF16)
        rms_in = sb("rms_in", [P, NT * (NH + NKV)])
        rms_out = sb("rms_out", [P, NT * (NH + NKV)])

        x1 = sb("x1", [P, NT, D])

        scratch = ExitStack()
        with scratch:
            def tb(name, shape, dt=F32):
                return scratch.enter_context(nc.sbuf_tensor(name, shape, dt))
            vec_rows = tb("vec_rows", [ROWS, P])
            tm_rows8 = tb("tm_rows8", [B * NT, P], U8)
            tm_rows = tb("tm_rows", [B * NT, P])
            cmask8 = tb("cmask8", [P, B * G], U8)
            cmask = tb("cmask", [P, B * G])
            dskip = tb("dskip", [1, D])
            s4 = tb("s4", [P, 4, NS])
            sm = tb("sm", [P, 12, NS])
            dtc = tb("dtc", [P, 8])
            dti = tb("dti", [P, 2], I32)
            packs = tb("packs", [P, 4, P])
            pk = tb("pk", [P, 4, P])
            pk32 = tb("pk32", [P, 3, P])
            index = tb("index", [P, JM])
            offs = tb("offs", [P, 4])
            pv = tb("pv", [P, JM, JM])
            pt = tb("pt", [P, JM, JM])
            pr = tb("pr", [P, JM, JM])
            wt_raw = pr[:, :, :].rearrange("p a b -> p (a b)")
            uf = tb("uf", [P, JM, IM])
            ug = tb("ug", [P, JM, IM])
            ut = tb("ut", [P, JM, IM])
            ue = tb("ue", [P, JM, IM])
            kld = pv[:, 0:NT * D // JM, :].rearrange("p a c -> p (a c)").rearrange("p (j d) -> p j d", j=NT)
            ctxs = tb("ctxs", [P, DV])
            ctxT = tb("ctxT", [DV, B * G])
            ctx_rep = uf[0:DV, :, :].rearrange("p a c -> p (a c)").rearrange("p (b n) -> p b n", b=B)
            wk = tb("wk", [DV, P])
            wv = tb("wv", [DV, D])
            wq = tb("wq", [P, P])
            wqT = tb("wqT", [P, P])
            wvT = tb("wvT", [P, DV])
            w_film = tb("w_film", [P, 4 * D])
            wvf = ug[0:DV, :, :].rearrange("p a c -> p (a c)")

        x1T = sb("x1T", [P, SEQ])
        sc = sb("sc", [P, NT * XH, G])
        sc_max = sb("sc_max", [P, NT * XH])
        sc_sum = sb("sc_sum", [P, NT * XH])
        attnT = sb("attnT", [P, SEQ])
        film = sb("film", [P, NT, 4 * D])
        xn = sb("xn", [P, NT, D])
        fb = sb("fb", [P, NT, D])
        spec = sb("spec", [P, 2 * NT, D])
        xt = sb("xt", [P, NT, D])
        x2T = attnT
        ffT = fa[:, :, :].rearrange("p j d -> p (j d)")
        gates = sb("gates", [P, NT, NE])
        gmax = sb("gmax", [P, NT])
        cmp_a = sb("cmp_a", [P, NT, NE, NE])
        cmp_b = sb("cmp_b", [P, NT, NE, NE])
        chosen = sb("chosen", [P, NT, NE])
        w_tok = sb("w_tok", [P, NT, NE])
        w_round = sb("w_round", [P, NT, NE], F32R)
        w_parts = sb("w_parts", [P, NT, 2 * NE])

        ld_attn = sem("ld_attn")
        ld_s4 = sem("ld_s4")
        ld_vec = sem("ld_vec")
        ld_cross = sem("ld_cross")
        ld_dft = sem("ld_dft")
        ld_rest = sem("ld_rest")
        ld_wt = sem("ld_wt")
        wt_split = sem("wt_split")
        ld_w = [sem(f"ld_w{i}") for i in range(2)]
        w_split = sem("w_split")
        x_landed = sem("x_landed")
        x_used = sem("x_used")
        out_sent = sem("out_sent")
        k_copied = sem("k_copied")
        vones_ready = sem("vones_ready")
        pro_pe = sem("pro_pe")
        pro_sb = sem("pro_sb")
        pro_arg = sem("pro_arg")
        pro_fun = sem("pro_fun")
        kij_ready = sem("kij_ready")
        kij_sent = sem("kij_sent")
        kld_landed = sem("kld_landed")
        kconst_ready = sem("kconst_ready")
        s_full = sem("s_full")
        s_free = sem("s_free")
        u_full = sem("u_full")
        u_free_dve = sem("u_free_dve")
        u_free_act = sem("u_free_act")
        xT_ps, xT_sb = sem("xT_ps"), sem("xT_sb")
        var_ready = sem("var_ready")
        rstd_ready = sem("rstd_ready")
        parts_ready = sem("parts_ready")
        v_ready = sem("v_ready")
        copies_ready = sem("copies_ready")
        exp_done = sem("exp_done")
        masked = sem("masked")
        pv_done = sem("pv_done")
        oT_ready = sem("oT_ready")
        y_ps = sem("y_ps")
        y_ready = sem("y_ready")
        yT_ps, yT_sb, proj_ps, x1_ready = sem("yT_ps"), sem("yT_sb"), sem("proj_ps"), sem("x1_ready")
        x1T_ps, x1T_sb, sc_ps = sem("x1T_ps"), sem("x1T_sb"), sem("sc_ps")
        sc_ready, sc_exp, attn_ready, attnT_ps, attnT_sb = (sem(n) for n in (
            "sc_ready", "sc_exp", "attn_ready", "attnT_ps", "attnT_sb"))
        xmod_ready, spec_ready, conv_ps, h_ready, hT_ps, hT_sb = (sem(n) for n in (
            "xmod_ready", "spec_ready", "conv_ps", "h_ready", "hT_ps", "hT_sb"))
        ffn_ps, ffT_sb, ffn_tok, x2_ready, x2T_ps, x2T_sb, x2_split = (sem(n) for n in (
            "ffn_ps", "ffT_sb", "ffn_tok", "x2_ready", "x2T_ps", "x2T_sb", "x2_split"))
        gates_ps, gates_ready, gates_exp, wtok_ready, wT_ps, wT_sb = (sem(n) for n in (
            "gates_ps", "gates_ready", "gates_exp", "wtok_ready", "wT_ps", "wT_sb"))
        split_done = sem("split_done")
        down_step = sem("down_step")
        e_up, e_gelu, e_split, e_down = sem("e_up"), sem("e_gelu"), sem("e_split"), sem("e_down")
        bc_ps, bc_sb, settled, accT_ps = sem("bc_ps"), sem("bc_sb"), sem("settled"), sem("accT_ps")
        y_out_ready = sem("y_out_ready")
        dve_step = sem("dve_step")
        pool_step = sem("pool_step")
        act_step = sem("act_step")

        x_dram = t["x"]
        kernel_dram = nc.dram_tensor("s4d_kernel", (SEQ, D), F32, kind="Internal").ap()
        block = ctx.enter_context(nc.Block())

        @block.sync
        def _(sp):
            def load(dst, src, s):
                sp.dma_start(dst, src).then_inc(s, 16)

            def load_x(b):
                if b:
                    sp.wait_ge(x_used, b)
                sp.dma_start(x_in[:, :, :], x_dram[b].rearrange("(j p) d -> p j d", p=P)).then_inc(x_landed, 16)

            load(vec_rows[ROW_B1:ROW_B1 + HC, :], t["L0_xattn_b1"].rearrange("(c p) -> c p", p=P), ld_vec)
            load(vec_rows[ROW_B1 + HC:ROW_B1 + HC * (1 + NSH), :], t["L0_ffn_sb1"].rearrange("s (c p) -> (s c) p", p=P), ld_vec)
            load(vec_rows[ROW_B1 + HC * (1 + NSH):ROW_B2, :], t["L0_ffn_b1"].rearrange("s (c p) -> (s c) p", p=P), ld_vec)
            load(vec_rows[ROW_B2:ROW_B2 + 1, :], t["L0_xattn_b2"].rearrange("(c p) -> c p", p=P), ld_vec)
            load(vec_rows[ROW_B2 + 1:ROW_B2 + 1 + NSH, :], t["L0_ffn_sb2"], ld_vec)
            load(vec_rows[ROW_B2 + 1 + NSH:ROW_LDT, :], t["L0_ffn_b2"], ld_vec)
            load(vec_rows[ROW_LDT:ROWS, :], t["L0_xattn_log_dt"].rearrange("(c p) -> c p", p=P), ld_vec)
            load(ident[:, :], t["c_ident"], ld_vec)
            for n, k in enumerate(("A_re", "A_im", "C_re", "C_im")):
                load(s4[:, n, :], t[f"L0_xattn_{k}"], ld_s4)
            load(index[:, :], t["c_index"].partition_broadcast(P), ld_s4)
            load(offs[:, :], t["c_offs"], ld_s4)
            load(dskip[:, :], t["L0_xattn_D_skip"].rearrange("(c p) -> c p", p=P), ld_s4)
            load_x(0)
            load(wqkv[:, 0:NH * HD], t["L0_attn_w_q"], ld_attn)
            load(wqkv[:, NH * HD:QK], t["L0_attn_w_k"], ld_attn)
            load(wqkv[:, QK:QKV], t["L0_attn_w_v"], ld_attn)
            load(wo[:, :], t["L0_attn_w_o"], ld_attn)
            load(rope[:, :, :, :].rearrange("p j c e -> p (j c e)"), t["c_rope"], ld_attn)
            load(pair_sum[:, :], t["c_pair_sum"], ld_attn)
            load(ctxs[:, :], t["ctx_768"].rearrange("b g d -> (b g) d"), ld_cross)
            load(wq[:, :], t["L0_xattn_Wq"], ld_cross)
            load(wk[:, :], t["L0_xattn_Wk"], ld_cross)
            load(wv[:, :], t["L0_xattn_Wv"], ld_cross)
            load(w_film[:, 0:2 * D], t["L0_xattn_W_film_in"], ld_cross)
            load(w_film[:, 2 * D:4 * D], t["L0_xattn_W_film_out"], ld_cross)
            load(gate[:, :], t["L0_xattn_mod_gate"].partition_broadcast(P), ld_cross)
            load(film_bias[:, 0:2 * D], t["L0_xattn_b_film_in"].partition_broadcast(P), ld_cross)
            load(film_bias[:, 2 * D:4 * D], t["L0_xattn_b_film_out"].partition_broadcast(P), ld_cross)
            load(tm_rows8[:, :], t["mask_BxS_bf1"].rearrange("b (j p) -> (b j) p", p=P), ld_cross)
            load(cmask8[:, :], t["mask_BxS2_bf1"].rearrange("b g -> (b g)").partition_broadcast(P), ld_cross)
            for m, k in ((cosm, "c_cos"), (sin_fwd, "c_sin_fwd"), (sin_inv, "c_sin_inv")):
                load(m[:, :, :], t[k].rearrange("(j p) f -> p j f", p=P), ld_dft)
            for n, k in enumerate(("g_norm_in", "b_norm_in", "g_ffn", "b_ffn", "g_norm_out", "b_norm_out")):
                load(norms[:, n, :], t[f"L0_xattn_{k}"].partition_broadcast(P), ld_rest)
            load(router_w[:, :], t["L0_ffn_rW"], ld_rest)
            load(router_b[:, :], t["L0_ffn_rb"].partition_broadcast(P), ld_rest)
            load(earlier[:, :, :].rearrange("p a b -> p (a b)"), t["c_earlier"].partition_broadcast(P), ld_rest)
            sp.wait_ge(kij_ready, 1)
            load(kernel_dram.rearrange("(i j) d -> i (j d)", i=IM), kij.rearrange("i j d -> i (j d)"), kij_sent)
            sp.wait_ge(kij_sent, 16)
            load(kld, kernel_dram.rearrange("(j p) d -> p j d", p=P), kld_landed)
            load(wt_raw[:, 0:HID], t["L0_xattn_W1"], ld_wt)
            load(wt_raw[:, HID:2 * HID].rearrange("p (c d) -> p c d", c=HC),
                 t["L0_xattn_W2"].rearrange("(c p) d -> p c d", p=P), ld_wt)
            for b in range(1, B):
                load_x(b)
            sp.wait_ge(x1_ready, B)
            for e in range(NM):
                if e >= 2:
                    sp.wait_ge(w_split, e - 1)
                w1, w2 = (t["L0_ffn_sW1"][e], t["L0_ffn_sW2"][e]) if e < NSH else (
                    t["L0_ffn_W1"][e - NSH], t["L0_ffn_W2"][e - NSH])
                load(e_raw[:, e % 2, 0:HID], w1, ld_w[e % 2])
                load(e_raw[:, e % 2, HID:2 * HID].rearrange("p (c d) -> p c d", c=HC),
                     w2.rearrange("(c p) d -> p c d", p=P), ld_w[e % 2])
            for b in range(B):
                sp.wait_ge(y_out_ready, b + 1)
                sp.dma_start(out[b].rearrange("(j p) d -> p j d", p=P), y_out[:, b, :, :]).then_inc(out_sent, 16)
            sp.wait_ge(out_sent, 16 * B)

        @block.tensor
        def _(pe):
            mm = nc.tensor.matmul

            def tp(dst, src):
                return nc.tensor.transpose(dst, src, ident[0:src.shape[0], 0:src.shape[0]])

            pe.wait_ge(ld_vec, 16 * 8)
            tp(bank_d[:, 0:ROWS], vec_rows[:, :]).then_inc(pro_pe, 1)
            pe.wait_ge(ld_cross, 16 * 11)
            tp(bank_r[:, 0:P], wq[:, :])
            tp(bank_r[0:DV, P:2 * P], ctxs[:, :])
            tp(bank_r[:, 2 * P:2 * P + DV], wv[:, :])
            pe.wait_ge(pro_sb, 1)
            tp(bank_r[:, 3 * P:3 * P + B * NT], tm_rows[:, :]).then_inc(pro_pe, 1)
            pe.wait_ge(pro_sb, 2)
            mm(bank_o[:, 0:B * G], wk[:, :], ctxT[:, :], start=True, stop=True).then_inc(pro_pe, 1)
            mm(bank_m[0:DV, :], wvT[:, :], w_film[:, :], start=True, stop=True).then_inc(pro_pe, 1)
            pe.wait_ge(pro_sb, 3)
            mm(ring_s[0][:, :], wqT[:, :], kbd, start=True, stop=True).then_inc(pro_pe, 1)
            pe.wait_ge(pro_sb, 4)
            for b in range(B):
                dst = (bank_r, bank_d, ring_u[0], ring_u[1])[b]
                mm(dst[:, :], ctx_rep[:, b, :], wvf, start=True, stop=True).then_inc(pro_pe, 1)
            pe.wait_ge(pro_sb, 5)
            for n in range(4):
                last = tp(bank_o[:, n * P:(n + 1) * P], packs[:, n, :])
            last.then_inc(pro_pe, 1)
            for q in range(D // JM):
                pe.wait_ge(pro_sb, 6 + q)
                for h in range(2):
                    for d in range(16):
                        last = mm(down[h][0:IM, JM * d:JM * (d + 1)], uf[:, 16 * h + d, :], pv[:, 16 * h + d, :],
                                  start=True, stop=True)
                last.then_inc(pro_pe, 1)
            pe.wait_ge(kconst_ready, 1)
            pe.wait_ge(ld_dft, 48)
            for f in range(2 * NT):
                mat, c = (cosm, f) if f < NT else (sin_fwd, f - NT)
                for j in range(NT):
                    last = mm(ring_u[f // NT][:, P * c:P * (c + 1)], mat[:, j, P * c:P * (c + 1)],
                              kld[:, j, :], start=(j == 0), stop=(j == NT - 1))
            last.then_inc(pro_pe, 1)

            def s_fill(b, n):
                if b * S_FILLS + n >= 2:
                    pe.wait_ge(s_free, b * S_FILLS + n - 1)
                return ring_s[n % 2]

            def scores(b, p):
                for n, (r, tiles) in enumerate(FILLS):
                    bank = s_fill(b, S_SC + NF * p + n)
                    for j, c in tiles:
                        w = SEQ - P * j
                        last = mm(bank[:, c:c + w], kT[64 * r:64 * r + 64, p // 2, P * j:P * (j + 1)],
                                  qT[64 * r:64 * r + 64, p, P * j:SEQ], start=True, stop=True)
                    last.then_inc(s_full, 1)

            def values(b, p):
                pe.wait_ge(masked, b * NPAIR + p + 1)
                if b * NPAIR + p >= 1:
                    pe.wait_ge(oT_ready, b * NPAIR + p)
                for first in (True, False):
                    for s in range(4):
                        r, j = s % 2, ((0, 3), (1, 2))[s // 2][0 if first else 1]
                        c = COL[(r, j)]
                        last = mm(bank_o[32 * s:32 * s + 32, P * j:SEQ], vv[:, j, p // 2, :],
                                  probs[:, p % 2, c:c + SEQ - P * j], start=first, stop=not first)
                last.then_inc(pv_done, 1)

            def token_rows(b, p):
                pe.wait_ge(oT_ready, b * NPAIR + p + 1)
                if p >= 2:
                    pe.wait_ge(y_ready, b * NPAIR + p - 1)
                for j in range(NT):
                    c = 256 * (p % 2) + 64 * j
                    last = mm(bank_m[:, c:c + 64], oT[:, p % 2, P * j:P * (j + 1)], pair_sum[:, :],
                              start=True, stop=True)
                last.then_inc(y_ps, 1)

            def attention(b):
                pe.wait_ge(x_landed, 16 * (b + 1))
                for j in range(NT):
                    last = tp(bank_m[:, P * j:P * (j + 1)], x_in[:, j, :])
                last.then_inc(xT_ps, 1)
                pe.wait_ge(xT_sb, b + 1)
                for n in range(2):
                    bank = s_fill(b, S_QKV + n)
                    for j in range(2):
                        k = 2 * n + j
                        last = mm(bank[:, QKV * j:QKV * (j + 1)], xT[:, P * k:P * (k + 1)], wqkv[:, :],
                                  start=True, stop=True)
                    last.then_inc(s_full, 1)
                pe.wait_ge(copies_ready, b + 1)
                pe.wait_ge(parts_ready, b + 1)
                for n in range(6):
                    bank = s_fill(b, S_QT + n)[:, :].bitcast(BF16).rearrange("p (a j q) -> p a j q", a=2, j=NT)
                    for a in range(2):
                        for j in range(NT):
                            if n < 4:
                                src = qs[:, j * NH + 2 * (2 * n + a):j * NH + 2 * (2 * n + a) + 2, :, :]
                                src = src.rearrange("p n c e -> p (n c e)")
                            else:
                                src = k_parts[:, j * NKV + 2 * (n - 4) + a, :, :, :].rearrange("p n c e -> p (n c e)")
                            last = nc.tensor.transpose(bank[:, a, j, :], src, identb[:, :])
                    last.then_inc(s_full, 1)
                pe.wait_ge(s_free, b * S_FILLS + S_SC)
                pe.wait_ge(v_ready, b + 1)
                scores(b, 0)
                for p in range(NPAIR):
                    if p + 1 < NPAIR:
                        scores(b, p + 1)
                    values(b, p)
                    if p >= 1:
                        token_rows(b, p - 1)
                token_rows(b, NPAIR - 1)
                pe.wait_ge(y_ready, NPAIR * (b + 1))
                for j in range(NT):
                    last = tp(bank_m[:, P * j:P * (j + 1)], y_att[:, j, :])
                last.then_inc(yT_ps, 1)
                pe.wait_ge(yT_sb, b + 1)
                for j in range(NT):
                    last = mm(bank_o[:, P * j:P * (j + 1)], yT[:, P * j:P * (j + 1)], wo[:, :], start=True, stop=True)
                last.then_inc(proj_ps, 1)

            def three(bank, hi, lo, a_hi, a_lo, start, stop):
                for k, (w, a) in enumerate(((hi, a_hi), (hi, a_lo), (lo, a_hi))):
                    last = mm(bank[:, :], w, a, start=(start and k == 0), stop=(stop and k == 2))
                return last

            def u_wait(b, u):
                if u < 2:
                    return
                if u - 2 < U_FFN:
                    pe.wait_ge(u_free_dve, b * U_DVE + u - 1)
                else:
                    pe.wait_ge(u_free_act, b * U_ACT + u - 1 - U_FFN)

            def rest(b):
                pe.wait_ge(x1_ready, b + 1)
                for j in range(NT):
                    last = tp(bank_r[:, P * j:P * (j + 1)], x1[:, j, :])
                last.then_inc(x1T_ps, 1)
                pe.wait_ge(x1T_sb, b + 1)
                for j in range(NT):
                    last = mm(bank_d[:, P * j:P * (j + 1)], x1T[:, P * j:P * (j + 1)], xq[:, b, :], start=True, stop=True)
                last.then_inc(sc_ps, 1)
                pe.wait_ge(attn_ready, b + 1)
                for j in range(NT):
                    last = tp(bank_r[:, P * j:P * (j + 1)], sc[:, XH * j:XH * (j + 1), :].rearrange("p h g -> p (h g)"))
                last.then_inc(attnT_ps, 1)
                pe.wait_ge(attnT_sb, b + 1)
                for j in range(NT):
                    u_wait(b, U_FILM + j)
                    mm(ring_u[j % 2][:, :], attnT[:, P * j:P * (j + 1)], vf[:, b, :], start=True, stop=True).then_inc(u_full, 1)
                pe.wait_ge(xmod_ready, b + 1)
                for f in range(2):
                    u_wait(b, U_DFT + f)
                    mat = (cosm, sin_fwd)[f]
                    for c in range(NT):
                        for j in range(NT):
                            last = mm(ring_u[f][:, P * c:P * (c + 1)], mat[:, j, P * c:P * (c + 1)], xn[:, j, :],
                                      start=(j == 0), stop=(j == NT - 1))
                    last.then_inc(u_full, 1)
                pe.wait_ge(spec_ready, b + 1)
                for j in range(NT):
                    for f in range(2 * NT):
                        mat = cosm if f < NT else sin_inv
                        last = mm(bank_d[:, P * j:P * (j + 1)], mat[:, f % NT, P * j:P * (j + 1)], spec[:, f, :],
                                  start=(f == 0), stop=(f == 2 * NT - 1))
                last.then_inc(conv_ps, 1)
                pe.wait_ge(h_ready, b + 1)
                for j in range(NT):
                    last = tp(bank_r[:, P * j:P * (j + 1)], fa[:, j, :])
                last.then_inc(hT_ps, 1)
                pe.wait_ge(hT_sb, b + 1)
                pe.wait_ge(wt_split, 1)
                for n in range(HC + 1):
                    if n < HC:
                        u_wait(b, U_FFN + n)
                        c = slice(P * n, P * (n + 1))
                        three(ring_u[n % 2], wt_hi[:, c], wt_lo[:, c], t_hi[:, b, :], t_lo[:, b, :], True, True).then_inc(u_full, 1)
                    if n:
                        k = n - 1
                        pe.wait_ge(split_done, b * HC + n)
                        c = slice(HID + P * k, HID + P * (k + 1))
                        three(bank_d, wt_hi[:, c], wt_lo[:, c], g_hi[:, k, :], g_lo[:, k, :], k == 0, k == HC - 1).then_inc(down_step, 1)
                pe.wait_ge(ffT_sb, b + 1)
                for j in range(NT):
                    last = tp(bank_r[:, P * j:P * (j + 1)], ffT[:, P * j:P * (j + 1)])
                last.then_inc(ffn_tok, 1)
                pe.wait_ge(x2_ready, b + 1)
                for j in range(NT):
                    last = tp(bank_r[:, P * j:P * (j + 1)], x2[:, b, P * j:P * (j + 1)])
                last.then_inc(x2T_ps, 1)
                pe.wait_ge(x2T_sb, b + 1)
                for j in range(NT):
                    last = mm(bank_d[:, NE * j:NE * (j + 1)], x2T[:, P * j:P * (j + 1)], router_w[:, :], start=True, stop=True)
                last.then_inc(gates_ps, 1)
                pe.wait_ge(wtok_ready, b + 1)
                for j in range(NT):
                    last = tp(bank_r[0:2 * NE, P * j:P * (j + 1)], w_parts[:, j, :])
                last.then_inc(wT_ps, 1)

            def moe():
                total = NM * B * HC

                def up(c):
                    (e, b), n = divmod(c // HC, B), c % HC
                    if b == 0 and n == 0:
                        pe.wait_ge(w_split, e + 1)
                    if e >= NSH and n == 0:
                        r = c // HC - NSH * B
                        if r >= 1:
                            pe.wait_ge(bc_sb, r)
                        mm(bank_m[:, :], spread[:, e - NSH:e - NSH + 1].broadcast_to([2 * NE, P]), wT[:, b, :],
                           start=True, stop=True).then_inc(bc_ps, 1)
                    if c >= HC:
                        pe.wait_ge(e_gelu, c - HC + 1)
                    w = slice(P * n, P * (n + 1))
                    three(ring_up[n], w_hi[:, e % 2, w], w_lo[:, e % 2, w], t_hi[:, b, :], t_lo[:, b, :],
                          True, True).then_inc(e_up, 1)

                def down_product(c):
                    (e, b), n = divmod(c // HC, B), c % HC
                    q = c // HC
                    if n == 0 and q >= 2:
                        pe.wait_ge(settled, q - 1)
                    pe.wait_ge(e_split, c + 1)
                    w = slice(HID + P * n, HID + P * (n + 1))
                    three(down[q % 2], w_hi[:, e % 2, w], w_lo[:, e % 2, w], g_hi[:, n, :], g_lo[:, n, :],
                          n == 0, n == HC - 1).then_inc(e_down, 1)

                pe.wait_ge(wT_sb, B)
                for c in range(total + LAG):
                    if c < total:
                        up(c)
                    if c >= LAG:
                        down_product(c - LAG)
                for b in range(B):
                    pe.wait_ge(settled, NM * B - B + b + 1)
                    if b >= 2:
                        pe.wait_ge(y_out_ready, b - 1)
                    for j in range(NT):
                        last = tp((bank_o, bank_m)[b % 2][:, P * j:P * (j + 1)], acc[:, b, P * j:P * (j + 1)])
                    last.then_inc(accT_ps, 1)

            for b in range(B):
                attention(b)
                rest(b)
            moe()

        @block.scalar
        def _(act):
            f = nc.scalar.activation
            act.wait_ge(pro_arg, 1)
            f(sm[:, 2, :], sm[:, 0, :], ACT.Tanh, scale=0.5).then_inc(pro_fun, 1)
            act.wait_ge(pro_arg, 2)
            f(sm[:, 3, :], sm[:, 4, :], ACT.Sin, scale=TURN / 2)
            f(sm[:, 5, :], sm[:, 4, :], ACT.Sin, scale=TURN).then_inc(pro_fun, 1)
            for q in range(D // JM):
                act.wait_ge(pro_arg, 3 + 3 * q)
                f(pv[:, :, :], pt[:, :, :], ACT.Sin, scale=-SIN_SCALE, bias=offs[:, 2:3]).then_inc(pro_fun, 1)
                act.wait_ge(pro_arg, 4 + 3 * q)
                f(uf[:, :, :], uf[:, :, :], ACT.Sin, scale=-SIN_SCALE, bias=offs[:, 2:3])
                f(ug[:, :, :], ug[:, :, :], ACT.Sin, scale=-SIN_SCALE, bias=offs[:, 3:4]).then_inc(pro_fun, 1)
                act.wait_ge(pro_arg, 5 + 3 * q)
                f(pr[:, :, :], pr[:, :, :], ACT.Exp)
                f(ue[:, :, :], ue[:, :, :], ACT.Exp).then_inc(pro_fun, 1)

            def attention(b):
                for n in range(2):
                    act.wait_ge(s_full, b * S_FILLS + S_QKV + n + 1)
                    f(qkv[:, 2 * n:2 * n + 2, :].rearrange("p j c -> p (j c)"), ring_s[n][:, 0:2 * QKV], ACT.Copy).then_inc(s_free, 1)
                for n in range(6):
                    act.wait_ge(s_full, b * S_FILLS + S_QT + n + 1)
                    dst = qT[:, 2 * n:2 * n + 2, :] if n < 4 else kT[:, 2 * (n - 4):2 * (n - 4) + 2, :]
                    f(dst.rearrange("p a q -> p (a q)"), ring_s[n % 2][:, :].bitcast(BF16), ACT.Copy).then_inc(s_free, 1)
                for p in range(NPAIR):
                    if b * NPAIR + p >= 2:
                        act.wait_ge(pv_done, b * NPAIR + p - 1)
                    for n in range(NF):
                        act.wait_ge(s_full, b * S_FILLS + S_SC + NF * p + n + 1)
                        f(probs[:, p % 2, BASE[n]:BASE[n] + WIDTH[n]], ring_s[n % 2][:, 0:WIDTH[n]], ACT.Tanh,
                          scale=1.0 / (CAP * float(np.sqrt(np.float32(HD))))).then_inc(s_free, 1)
                    act.wait_ge(s_free, b * S_FILLS + S_SC + NF * (p + 1))
                    f(probs[:, p % 2, :], probs[:, p % 2, :], ACT.Exp, scale=CAP).then_inc(exp_done, 1)

            def rest(b):
                act.wait_ge(x1T_ps, b + 1)
                f(x1T[:, :], bank_r[:, :], ACT.Copy).then_inc(x1T_sb, 1)
                act.wait_ge(sc_ready, b + 1)
                f(sc[:, :, :], sc[:, :, :], ACT.Exp).then_inc(sc_exp, 1)
                act.wait_ge(attnT_ps, b + 1)
                f(attnT[:, :], bank_r[:, :], ACT.Copy).then_inc(attnT_sb, 1)
                for n in range(HC):
                    act.wait_ge(u_full, b * U_FILLS + U_FFN + n + 1)
                    if b * HC + n >= 2:
                        act.wait_ge(split_done, b * HC + n - 1)
                    f(g_raw[:, n % 2, :], ring_u[n % 2][:, :], ACT.Gelu, bias=vcols[:, ROW_B1 + n:ROW_B1 + n + 1]).then_inc(u_free_act, 1)
                act.wait_ge(down_step, HC * (b + 1))
                f(ffT, bank_d[:, :], ACT.Identity, bias=vcols[:, ROW_B2:ROW_B2 + 1]).then_inc(ffT_sb, 1)
                act.wait_ge(x2T_ps, b + 1)
                f(x2T[:, :], bank_r[:, :], ACT.Copy).then_inc(x2T_sb, 1)
                act.wait_ge(gates_ready, b + 1)
                f(w_tok[:, :, :], w_tok[:, :, :], ACT.Exp).then_inc(gates_exp, 1)

            def moe():
                for q in range(NM * B):
                    e, b = divmod(q, B)
                    if e >= NSH:
                        r = q - NSH * B
                        act.wait_ge(bc_ps, r + 1)
                        if r >= 2:
                            act.wait_ge(settled, q - 1)
                        f(w_bc[:, r % 2, :], bank_m[:, :], ACT.Copy).then_inc(bc_sb, 1)
                    for n in range(HC):
                        c = q * HC + n
                        act.wait_ge(e_up, c + 1)
                        if c >= 2:
                            act.wait_ge(e_split, c - 1)
                        k = ROW_B1 + HC * (1 + e) + n
                        f(g_raw[:, n % 2, :], ring_up[n][:, :], ACT.Gelu, bias=vcols[:, k:k + 1]).then_inc(e_gelu, 1)

            for b in range(B):
                attention(b)
                rest(b)
            moe()

        @block.gpsimd
        def _(pool):
            def step(k, ins):
                ins.then_inc(pool_step, 1)
                pool.wait_ge(pool_step, k)

            g = nc.gpsimd
            g.memset(neg_half[:, :], -0.5)
            step(1, g.memset(vv[:, :, :, :], 0.0))
            g.memset(vv[:, :, :, HD:HD + 1], 1.0)
            pool.wait_ge(ld_vec, 16 * 8)
            g.tensor_copy(identb[:, :], ident[:, :]).then_inc(vones_ready, 1)

            def power(k, b):
                pool.wait_ge(var_ready, NORMS * b + k + 1)
                if k == 0:
                    g.tensor_tensor(rms_out[:, :], rms_in[:, :], neg_half[:, :], ALU.pow).then_inc(rstd_ready, 1)
                else:
                    g.tensor_tensor(rstd[:, :], var_eps[:, :], neg_half[:, 0:NT], ALU.pow).then_inc(rstd_ready, 1)

            def copies(b):
                pool.wait_ge(parts_ready, b + 1)
                last = None
                for src, dsts in ((0, (1, 2)), (3, (4, 5)), (6, (7,))):
                    g.tensor_copy(qs[:, :, dsts[0]:dsts[-1] + 1, :],
                                  qs[:, :, src:src + 1, :].broadcast_to([P, NT * NH, len(dsts), HD]))
                for src, dsts in ((0, (3, 6)), (1, (4, 7)), (2, (5,))):
                    for d in dsts:
                        g.tensor_copy(k_parts[:, :, 0, d, :], k_parts[:, :, 0, src, :]).then_inc(k_copied, 1)
                pool.wait_ge(k_copied, 5 * (b + 1))
                g.tensor_copy(k_parts[:, :, 1, :, :].rearrange("p n c e -> p n (c e)"),
                              k_parts[:, :, 0, :, :].rearrange("p n c e -> p n (c e)")).then_inc(copies_ready, 1)

            def mask(b, p):
                pool.wait_ge(exp_done, b * NPAIR + p + 1)
                pr = probs[:, p % 2, :]
                for v in (pr[:, 0:4 * SEQ].rearrange("p (n w) -> p n w", w=SEQ)[:, :, 0:P],
                          pr[:, 2 * SEQ:4 * SEQ].rearrange("p (n w) -> p n w", w=SEQ)[:, :, 384:SEQ],
                          pr[:, 4 * SEQ:5 * SEQ].rearrange("p (n w) -> p n w", w=256)[:, :, 0:P]):
                    last = g.affine_select(out=v, in_=v, compare_op=ALU.is_ge, fill=0.0, base=0,
                                           pattern=[[0, v.shape[1]], [1, P]], channel_multiplier=-1)
                last.then_inc(masked, 1)

            for b in range(B):
                power(0, b)
                copies(b)
                for p in range(NPAIR):
                    mask(b, p)
                for k in range(1, NORMS):
                    power(k, b)
            for b in range(B):
                power(NORMS + b, B - 1)

        @block.vector
        def _(dve):
            v = nc.vector
            count = [0]

            def op(ins):
                count[0] += 1
                ins.then_inc(dve_step, 1)

            def then():
                dve.wait_ge(dve_step, count[0])

            def one(ins):
                op(ins)
                then()

            def s(k):
                return sm[:, k, :]

            tt, ts, stt = v.tensor_tensor, v.tensor_scalar, v.scalar_tensor_tensor
            op(v.memset(oT[64:P, :, 0:P], 0.0))
            dve.wait_ge(ld_cross, 16 * 11)
            v.tensor_copy(tm_rows[:, :], tm_rows8[:, :]).then_inc(pro_sb, 1)
            op(v.tensor_copy(cmask[:, :], cmask8[:, :]))
            op(ts(gate4[:, :], gate[:, :], 0.25, None, ALU.mult))
            one(ts(film_bias[:, :], film_bias[:, :], gate[:, 0:1], None, ALU.mult))
            op(ts(cmask[:, :], cmask[:, :], 1.0, 3e38, ALU.subtract, ALU.mult))
            for n in range(2):
                op(ts(film_bias[:, 2 * D * n:2 * D * n + D], film_bias[:, 2 * D * n:2 * D * n + D], 1.0, None, ALU.add))
            then()
            for h in range(XH):
                op(ts(ctx_bias[:, :, h, :], cmask[:, :].rearrange("p (b g) -> p b g", b=B), 10.0, None, ALU.mult))
            dve.wait_ge(pro_pe, 1)
            one(v.tensor_copy(vcols[:, :], bank_d[:, 0:ROWS]))
            one(tt(b2_shared[:, :], vcols[:, ROW_B2 + 1:ROW_B2 + 2], vcols[:, ROW_B2 + 2:ROW_B2 + 3], ALU.add))
            op(ts(b2_shared[:, :], b2_shared[:, :], 0.5, None, ALU.mult))
            one(v.memset(kbd, 0.0))
            dve.wait_ge(pro_pe, 2)
            op(v.tensor_copy(wqT[:, :], bank_r[:, 0:P]))
            op(v.tensor_copy(tmask[:, :], bank_r[:, 3 * P:3 * P + B * NT]))
            one(v.tensor_copy(ctxT[:, :], bank_r[0:DV, P:2 * P]))
            v.tensor_copy(wvT[:, :], bank_r[:, 2 * P:2 * P + DV]).then_inc(pro_sb, 1)
            for h in range(XH):
                op(v.tensor_copy(ctx_rep.rearrange("p b (h g) -> p b h g", h=XH)[:, :, h, :],
                                 ctxT[:, :].rearrange("p (b g) -> p b g", b=B)))
            dve.wait_ge(pro_pe, 3)
            for h in range(XH):
                last = v.tensor_copy(kbd.rearrange("p (b h g) -> p b h g", b=B, h=XH)[32 * h:32 * h + 32, :, h, :],
                                     bank_o[32 * h:32 * h + 32, 0:B * G].rearrange("p (b g) -> p b g", b=B))
            last.then_inc(pro_sb, 1)
            then()
            dve.wait_ge(pro_pe, 4)
            v.tensor_copy(wvf, bank_m[0:DV, :]).then_inc(pro_sb, 1)
            dve.wait_ge(pro_pe, 5)
            op(v.tensor_copy(xq[:, :, :].rearrange("p b g -> p (b g)"), ring_s[0][:, :]))
            for b in range(B):
                dve.wait_ge(pro_pe, 6 + b)
                op(ts(vf[:, b, :], (bank_r, bank_d, ring_u[0], ring_u[1])[b][:, :], gate4[:, 0:1], None, ALU.mult))
            ldt = vcols[:, ROW_LDT:ROW_LDT + 1]
            c = lambda k: dtc[:, k:k + 1]
            dve.wait_ge(ld_s4, 16 * 7)
            one(ts(c(0), ldt, 1.4426950408889634, MAGIC, ALU.mult, ALU.add))
            one(ts(c(0), c(0), MAGIC, None, ALU.subtract))
            op(ts(c(4), c(0), 127.0, None, ALU.add))
            one(stt(out=c(1), in0=c(0), scalar=-LN2_HI, in1=ldt, op0=ALU.mult, op1=ALU.add))
            op(v.tensor_copy(dti[:, 0:1], c(4)))
            one(stt(out=c(2), in0=c(0), scalar=-LN2_LO, in1=c(1), op0=ALU.mult, op1=ALU.add))
            one(ts(dti[:, 1:2], dti[:, 0:1], 23, None, ALU.logical_shift_left))
            one(ts(c(3), c(2), 1.0 / 5040, 1.0 / 720, ALU.mult, ALU.add))
            for k in (1.0 / 120, 1.0 / 24, 1.0 / 6, 0.5, 1.0, 1.0):
                one(ts(c(3), c(3), c(2), k, ALU.mult, ALU.add))
            one(tt(c(5), c(3), dti[:, 1:2].bitcast(F32), ALU.mult))
            op(ts(s(0), s4[:, 0, :], c(5), None, ALU.mult))
            one(ts(s(1), s4[:, 1, :], c(5), 1.0 / TWO_PI, ALU.mult, ALU.mult))
            one(ts(s(4), s(1), MAGIC, MAGIC, ALU.add, ALU.subtract))
            v.tensor_copy(packs[:, 0, 0:NS], s(0)).then_inc(pro_arg, 1)
            tt(s(4), s(1), s(4), ALU.subtract).then_inc(pro_arg, 1)
            dve.wait_ge(pro_arg, 2)
            op(v.tensor_copy(packs[:, 0, NS:P], s(0)))
            op(v.tensor_copy(packs[:, 1, 0:NS], s(4)))
            op(v.tensor_copy(packs[:, 1, NS:P], s(4)))
            op(tt(s(9), s4[:, 0, :], s4[:, 0, :], ALU.mult))
            op(tt(s(10), s4[:, 1, :], s4[:, 1, :], ALU.mult))
            dve.wait_ge(pro_fun, 1)
            one(ts(s(6), s(2), -1.0, 1.0, ALU.mult, ALU.add))
            op(tt(s(9), s(9), s(10), ALU.add))
            one(v.reciprocal(s(6), s(6)))
            op(v.reciprocal(s(9), s(9)))
            one(tt(s(6), s(6), s(2), ALU.mult))
            one(ts(s(6), s(6), 2.0, None, ALU.mult))
            dve.wait_ge(pro_fun, 2)
            one(tt(s(3), s(3), s(3), ALU.mult))
            one(ts(s(3), s(3), -2.0, None, ALU.mult))
            op(ts(s(7), s(3), 1.0, None, ALU.add))
            one(ts(s(8), s(6), 1.0, None, ALU.add))
            op(tt(s(7), s(7), s(6), ALU.mult))
            one(tt(s(8), s(8), s(5), ALU.mult))
            one(tt(s(7), s(7), s(3), ALU.add))
            op(tt(s(0), s4[:, 2, :], s(7), ALU.mult))
            op(tt(s(1), s4[:, 3, :], s(8), ALU.mult))
            op(tt(s(2), s4[:, 2, :], s(8), ALU.mult))
            one(tt(s(3), s4[:, 3, :], s(7), ALU.mult))
            op(tt(s(0), s(0), s(1), ALU.subtract))
            one(tt(s(2), s(2), s(3), ALU.add))
            op(tt(s(5), s(0), s4[:, 0, :], ALU.mult))
            op(tt(s(6), s(2), s4[:, 1, :], ALU.mult))
            op(tt(s(7), s(2), s4[:, 0, :], ALU.mult))
            one(tt(s(8), s(0), s4[:, 1, :], ALU.mult))
            op(tt(s(5), s(5), s(6), ALU.add))
            one(tt(s(7), s(8), s(7), ALU.subtract))
            op(tt(packs[:, 2, 0:NS], s(5), s(9), ALU.mult))
            one(tt(packs[:, 3, 0:NS], s(7), s(9), ALU.mult))
            op(ts(packs[:, 2, NS:P], packs[:, 2, 0:NS], -1.0, None, ALU.mult))
            v.tensor_copy(packs[:, 3, NS:P], packs[:, 3, 0:NS]).then_inc(pro_sb, 1)
            dve.wait_ge(pro_pe, 10)
            one(v.tensor_copy(pk[:, :, :].rearrange("p n d -> p (n d)"), bank_o[:, :]))
            op(ts(pk32[:, 0, :], pk[:, 0, :], float(JM), None, ALU.mult))
            one(ts(pk32[:, 1, :], pk[:, 1, :], float(JM), None, ALU.mult))
            one(ts(pk32[:, 2, :], pk32[:, 1, :], MAGIC, MAGIC, ALU.add, ALU.subtract))
            one(tt(pk32[:, 1, :], pk32[:, 1, :], pk32[:, 2, :], ALU.subtract))

            def fl(x):
                return x[:, :, :].rearrange("p d m -> p (d m)")

            def bc(x, q, m):
                return x[:, JM * q:JM * (q + 1)].unsqueeze(2).broadcast_to([P, JM, m])

            def ix(m):
                return index[:, 0:m].unsqueeze(1).broadcast_to([P, JM, m])

            def evacuate(q, h):
                d0 = JM * q + 16 * h
                return ts(kij[:, :, d0:d0 + 16].rearrange("i j d -> i d j"),
                          down[h][0:IM, :].rearrange("i (d j) -> i d j", j=JM), 2.0, None, ALU.mult)

            for q in range(D // JM):
                if q:
                    dve.wait_ge(pro_pe, 10 + q)
                    op(evacuate(q - 1, 0))
                    op(evacuate(q - 1, 1))
                one(tt(pr[:, :, :], bc(pk[:, 1, :], q, JM), ix(JM), ALU.mult))
                one(ts(fl(pt), fl(pr), offs[:, 0:1], MAGIC, ALU.add, ALU.add))
                stt(out=fl(pt), in0=fl(pt), scalar=MAGIC, in1=fl(pr), op0=ALU.subtract, op1=ALU.subtract).then_inc(pro_arg, 1)
                one(tt(ue[:, :, :], bc(pk32[:, 1, :], q, IM), ix(IM), ALU.mult))
                op(ts(fl(uf), fl(ue), offs[:, 0:1], MAGIC, ALU.add, ALU.add))
                one(ts(fl(ug), fl(ue), offs[:, 1:2], MAGIC, ALU.add, ALU.add))
                op(stt(out=fl(uf), in0=fl(uf), scalar=MAGIC, in1=fl(ue), op0=ALU.subtract, op1=ALU.subtract))
                stt(out=fl(ug), in0=fl(ug), scalar=MAGIC, in1=fl(ue), op0=ALU.subtract, op1=ALU.subtract).then_inc(pro_arg, 1)
                dve.wait_ge(pro_arg, 4 + 3 * q)
                op(tt(pr[:, :, :], bc(pk[:, 0, :], q, JM), ix(JM), ALU.mult))
                tt(ue[:, :, :], bc(pk32[:, 0, :], q, IM), ix(IM), ALU.mult).then_inc(pro_arg, 1)
                dve.wait_ge(pro_fun, 4 + 3 * q)
                op(tt(uf[:, :, :], uf[:, :, :], bc(pk[:, 2, :], q, IM), ALU.mult))
                one(tt(ug[:, :, :], ug[:, :, :], bc(pk[:, 3, :], q, IM), ALU.mult))
                one(tt(fl(uf), fl(uf), fl(ug), ALU.add))
                dve.wait_ge(pro_fun, 5 + 3 * q)
                op(tt(fl(pv), fl(pv), fl(pr), ALU.mult))
                tt(fl(uf), fl(uf), fl(ue), ALU.mult).then_inc(pro_sb, 1)
            dve.wait_ge(pro_pe, 14)
            op(evacuate(D // JM - 1, 0))
            evacuate(D // JM - 1, 1).then_inc(kij_ready, 1)
            dve.wait_ge(kld_landed, 16)
            tt(kld[0:1, 0, :], kld[0:1, 0, :], dskip[:, :], ALU.add).then_inc(kconst_ready, 1)
            dve.wait_ge(pro_pe, 15)
            op(ts(fl(kc), ring_u[0][:, :], 2.0 / (2 * SEQ), None, ALU.mult))
            op(ts(fl(ks), ring_u[1][:, :], 2.0 / (2 * SEQ), None, ALU.mult))
            one(ts(fl(kcn), ring_u[0][:, :], 2.0 / (2 * SEQ), None, ALU.mult))
            op(ts(kc[0:1, 0, :], kc[0:1, 0, :], 0.5, None, ALU.mult))
            one(ts(kcn[0:1, 0, :], ks[0:1, 0, :], 0.5, None, ALU.mult))
            one(v.memset(ks[0:1, 0, :], 0.0))
            dve.wait_ge(ld_vec, 16 * 8)
            op(tt(spread[:, :], ident[0:2 * NE, 0:NE], ident[0:2 * NE, NE:2 * NE], ALU.add))

            def norm(b, k, src, dst):
                for j in range(NT):
                    op(v.bn_stats(stats[:, j, :], src[:, j, :]))
                then()
                for j in range(NT):
                    op(v.bn_aggr(mean_var[:, j, :], stats[:, j, :]))
                then()
                ts(var_eps[:, :], mean_var[:, :, 1], EPS, None, ALU.add).then_inc(var_ready, 1)
                dve.wait_ge(rstd_ready, NORMS * b + k + 1)
                for j in range(NT):
                    last = ts(dst[:, j, :], src[:, j, :], mean_var[:, j, 0:1], rstd[:, j:j + 1], ALU.subtract, ALU.mult)
                    if j < NT - 1:
                        op(last)
                return last

            def affine(src, n):
                one(tt(src[:, :, :], src[:, :, :], norms[:, n:n + 1, :].broadcast_to([P, NT, D]), ALU.mult))
                return tt(src[:, :, :], src[:, :, :], norms[:, n + 1:n + 2, :].broadcast_to([P, NT, D]), ALU.add)

            def halves(hi, lo, src):
                one(v.tensor_copy(hi, src))
                return tt(lo, src, hi.bitcast(F32), ALU.subtract)

            def attention(b):
                dve.wait_ge(xT_ps, b + 1)
                v.tensor_copy(xT[:, :], bank_m[:, :]).then_inc(xT_sb, 1)
                dve.wait_ge(s_free, b * S_FILLS + 2)
                dve.wait_ge(vones_ready, 1)
                v.tensor_copy(vv[:, :, :, 0:HD], qkv[:, :, QK:QKV].rearrange("p j (g e) -> p j g e", g=NKV)).then_inc(v_ready, 1)
                heads = NH + NKV
                r4 = lambda x: x.rearrange("p (j h e) -> p j h e", j=NT, h=heads)
                r3 = lambda x: x.rearrange("p (n e) -> p n e", e=HD)
                qk = qkv[:, :, 0:QK]
                a3 = tmp_a.rearrange("p (j c) -> p j c", j=NT)
                one(tt(a3, qk, qk, ALU.mult))
                one(v.tensor_reduce(rms_in[:, :], r3(tmp_a), AX, ALU.add))
                ts(rms_in[:, :], rms_in[:, :], 1.0 / HD, EPS, ALU.mult, ALU.add).then_inc(var_ready, 1)
                dve.wait_ge(rstd_ready, NORMS * b + 1)
                for j in range(NT):
                    op(tt(r4(tmp_a)[:, j], qkv[:, j, 0:QK].rearrange("p (h e) -> p h e", e=HD),
                          rms_out[:, heads * j:heads * (j + 1)].unsqueeze(2).broadcast_to([P, heads, HD]), ALU.mult))
                then()
                half = HD // 2
                rp = lambda c, lo: rope[:, :, c:c + 1, lo:lo + half]
                op(tt(r4(tmp_b), r4(tmp_a), rope[:, :, 0:1, :].broadcast_to([P, NT, heads, HD]), ALU.mult))
                op(tt(r4(tmp_c)[:, :, :, 0:half], r4(tmp_a)[:, :, :, half:HD], rp(1, 0).broadcast_to([P, NT, heads, half]), ALU.mult))
                one(tt(r4(tmp_c)[:, :, :, half:HD], r4(tmp_a)[:, :, :, 0:half], rp(1, half).broadcast_to([P, NT, heads, half]), ALU.mult))
                one(tt(tmp_b, tmp_b, tmp_c, ALU.add))
                q4 = r4(tmp_b)[:, :, 0:NH, :]
                k4 = r4(tmp_b)[:, :, NH:heads, :]
                qp = lambda c: qs[:, :, c, :].rearrange("p (j h) e -> p j h e", j=NT)
                kp = lambda c: k_parts[:, :, 0, c, :].rearrange("p (j h) e -> p j h e", j=NT)
                op(v.tensor_copy(qp(0), q4))
                one(v.tensor_copy(kp(0), k4))
                op(tt(q4, q4, qp(0), ALU.subtract))
                one(tt(k4, k4, kp(0), ALU.subtract))
                op(v.tensor_copy(qp(3), q4))
                one(v.tensor_copy(kp(1), k4))
                op(tt(qp(6), q4, qp(3), ALU.subtract))
                tt(kp(2), k4, kp(1), ALU.subtract).then_inc(parts_ready, 1)
                for p in range(NPAIR):
                    dve.wait_ge(pv_done, b * NPAIR + p + 1)
                    if b * NPAIR + p >= 2:
                        dve.wait_ge(y_ps, b * NPAIR + p - 1)
                    op(v.tensor_copy(oT[0:64, p % 2, :], bank_o[0:64, :]))
                    v.tensor_copy(oT[64:P, p % 2, P:SEQ], bank_o[64:P, P:SEQ]).then_inc(oT_ready, 1)
                    dve.wait_ge(y_ps, b * NPAIR + p + 1)
                    ys = bank_m[:, 256 * (p % 2):256 * (p % 2 + 1)].rearrange("p (j h e) -> p j h e", j=NT, h=2)
                    one(v.reciprocal(ry[:, :, :], ys[:, :, :, HD]))
                    tt(y_att[:, :, 2 * HD * p:2 * HD * (p + 1)].rearrange("p j (h e) -> p j h e", h=2), ys[:, :, :, 0:HD],
                       ry[:, :, :].unsqueeze(3).broadcast_to([P, NT, 2, HD]), ALU.mult).then_inc(y_ready, 1)
                if b == 0:
                    dve.wait_ge(ld_wt, 32)
                    halves(wt_hi[:, :], wt_lo[:, :], wt_raw).then_inc(wt_split, 1)
                dve.wait_ge(yT_ps, b + 1)
                v.tensor_copy(yT[:, :], bank_m[:, :]).then_inc(yT_sb, 1)
                dve.wait_ge(proj_ps, b + 1)
                tt(fl(y_att), bank_o[:, :], fl(x_in), ALU.add).then_inc(x_used, 1)
                dve.wait_ge(x_used, b + 1)
                norm(b, 1, y_att, x1).then_inc(x1_ready, 1)

            def rest(b):
                dve.wait_ge(sc_ps, b + 1)
                d4 = bank_d[:, :].rearrange("p (j c) -> p j c", j=NT)
                s4v = fl(sc).rearrange("p (j c) -> p j c", j=NT)
                one(stt(out=s4v, in0=d4, scalar=1.0 / float(np.sqrt(np.float32(XD))),
                        in1=ctx_bias[:, b:b + 1].rearrange("p b h g -> p b (h g)").broadcast_to([P, NT, XH * G]),
                        op0=ALU.mult, op1=ALU.add))
                one(v.tensor_reduce(sc_max[:, :], sc[:, :, :], AX, ALU.max))
                tt(sc[:, :, :], sc[:, :, :], sc_max[:, :].unsqueeze(2).broadcast_to([P, NT * XH, G]), ALU.subtract).then_inc(sc_ready, 1)
                dve.wait_ge(x1_ready, b + 1)
                one(norm(b, 2, x1, xn))
                one(affine(xn, 0))
                dve.wait_ge(sc_exp, b + 1)
                one(v.tensor_reduce(sc_sum[:, :], sc[:, :, :], AX, ALU.add))
                one(v.reciprocal(sc_sum[:, :], sc_sum[:, :]))
                one(tt(sc_sum[:, :].rearrange("p (j h) -> p j h", j=NT), sc_sum[:, :].rearrange("p (j h) -> p j h", j=NT),
                       tmask[:, NT * b:NT * (b + 1)].unsqueeze(2).broadcast_to([P, NT, XH]), ALU.mult))
                tt(sc[:, :, :], sc[:, :, :], sc_sum[:, :].unsqueeze(2).broadcast_to([P, NT * XH, G]), ALU.mult).then_inc(attn_ready, 1)
                for j in range(NT):
                    dve.wait_ge(u_full, b * U_FILLS + U_FILM + j + 1)
                    tt(film[:, j, :], ring_u[j % 2][:, :], film_bias[:, :], ALU.add).then_inc(u_free_dve, 1)
                dve.wait_ge(u_free_dve, b * U_DVE + NT)
                one(tt(xn[:, :, :], xn[:, :, :], film[:, :, 0:D], ALU.mult))
                tt(xn[:, :, :], xn[:, :, :], film[:, :, D:2 * D], ALU.add).then_inc(xmod_ready, 1)
                dve.wait_ge(u_full, b * U_FILLS + U_DFT + 2)
                re, im = ring_u[0][:, :], ring_u[1][:, :]
                lo = spec[:, 0:NT, :].rearrange("p n d -> p (n d)")
                hi = spec[:, NT:2 * NT, :].rearrange("p n d -> p (n d)")
                op(tt(lo, re, fl(kc), ALU.mult))
                op(tt(fl(fa), im, fl(ks), ALU.mult))
                tt(hi, re, fl(ks), ALU.mult).then_inc(u_free_dve, 1)
                tt(fl(fb), im, fl(kcn), ALU.mult).then_inc(u_free_dve, 1)
                then()
                dve.wait_ge(u_free_dve, U_DVE * (b + 1))
                one(tt(lo, lo, fl(fa), ALU.subtract))
                tt(hi, hi, fl(fb), ALU.add).then_inc(spec_ready, 1)
                dve.wait_ge(conv_ps, b + 1)
                one(tt(fa[:, :, :], bank_d[:, :].rearrange("p (j d) -> p j d", j=NT), film[:, :, 2 * D:3 * D], ALU.mult))
                one(tt(fa[:, :, :], fa[:, :, :], film[:, :, 3 * D:4 * D], ALU.add))
                one(tt(fl(xt), fl(fa), fl(x1), ALU.add))
                one(norm(b, 3, xt, fa))
                affine(fa, 2).then_inc(h_ready, 1)
                dve.wait_ge(hT_ps, b + 1)
                halves(t_hi[:, b, :], t_lo[:, b, :], bank_r[:, :]).then_inc(hT_sb, 1)
                for n in range(HC):
                    dve.wait_ge(u_free_act, b * U_ACT + n + 1)
                    halves(g_hi[:, n, :], g_lo[:, n, :], g_raw[:, n % 2, :]).then_inc(split_done, 1)
                dve.wait_ge(ffn_tok, b + 1)
                one(tt(fl(xt), bank_r[:, :], fl(xt), ALU.add))
                one(norm(b, 4, xt, fa))
                one(affine(fa, 4))
                one(tt(fl(fa), fl(fa), fl(x1), ALU.add))
                norm(b, 5, fa, x2[:, b, :].rearrange("p (j d) -> p j d", j=NT)).then_inc(x2_ready, 1)
                dve.wait_ge(x2T_sb, b + 1)
                halves(t_hi[:, b, :], t_lo[:, b, :], x2T[:, :]).then_inc(x2_split, 1)
                dve.wait_ge(gates_ps, b + 1)
                one(tt(gates[:, :, :], bank_d[:, 0:NT * NE].rearrange("p (j e) -> p j e", j=NT),
                       router_b[:, :].unsqueeze(1).broadcast_to([P, NT, NE]), ALU.add))
                one(v.tensor_reduce(gmax[:, :], gates[:, :, :], AX, ALU.max))
                tt(w_tok[:, :, :], gates[:, :, :], gmax[:, :].unsqueeze(2).broadcast_to([P, NT, NE]), ALU.subtract).then_inc(gates_ready, 1)
                other = gates[:, :, :].unsqueeze(2).broadcast_to([P, NT, NE, NE])
                own = gates[:, :, :].unsqueeze(3).broadcast_to([P, NT, NE, NE])
                op(tt(cmp_a[:, :, :, :], other, own, ALU.is_gt))
                one(tt(cmp_b[:, :, :, :], other, own, ALU.is_equal))
                one(tt(cmp_b[:, :, :, :], cmp_b[:, :, :, :], earlier[:, :, :].unsqueeze(1).broadcast_to([P, NT, NE, NE]), ALU.mult))
                one(tt(cmp_a[:, :, :, :], cmp_a[:, :, :, :], cmp_b[:, :, :, :], ALU.add))
                one(v.tensor_reduce(chosen[:, :, :], cmp_a[:, :, :, :], AX, ALU.add))
                one(ts(chosen[:, :, :], chosen[:, :, :], 2.0, None, ALU.is_lt))
                dve.wait_ge(gates_exp, b + 1)
                one(tt(w_tok[:, :, :], w_tok[:, :, :], chosen[:, :, :], ALU.mult))
                one(v.tensor_reduce(gmax[:, :], w_tok[:, :, :], AX, ALU.add))
                one(v.reciprocal(gmax[:, :], gmax[:, :]))
                one(tt(w_tok[:, :, :], w_tok[:, :, :], gmax[:, :].unsqueeze(2).broadcast_to([P, NT, NE]), ALU.mult))
                one(v.tensor_copy(w_round[:, :, :], w_tok[:, :, :]))
                op(v.tensor_copy(w_parts[:, :, 0:NE], w_round[:, :, :].bitcast(F32)))
                tt(w_parts[:, :, NE:2 * NE], w_tok[:, :, :], w_round[:, :, :].bitcast(F32), ALU.subtract).then_inc(wtok_ready, 1)
                dve.wait_ge(wT_ps, b + 1)
                v.tensor_copy(wT[:, b, :], bank_r[0:2 * NE, :]).then_inc(wT_sb, 1)

            def settle(q):
                e, b = divmod(q, B)
                dve.wait_ge(e_down, HC * (q + 1))
                bank = down[q % 2][:, :]
                if e == 0:
                    ts(acc[:, b, :], bank, 1.0 / NSH, b2_shared[:, 0:1], ALU.mult, ALU.add).then_inc(settled, 1)
                elif e < NSH:
                    stt(out=acc[:, b, :], in0=bank, scalar=1.0 / NSH, in1=acc[:, b, :], op0=ALU.mult, op1=ALU.add).then_inc(settled, 1)
                else:
                    r, k = q - NSH * B, ROW_B2 + 1 + e
                    dve.wait_ge(bc_sb, r + 1)
                    one(stt(out=term[:, :], in0=bank, scalar=vcols[:, k:k + 1], in1=w_bc[:, r % 2, :], op0=ALU.add, op1=ALU.mult))
                    tt(acc[:, b, :], acc[:, b, :], term[:, :], ALU.add).then_inc(settled, 1)

            def split_weights(e):
                dve.wait_ge(ld_w[e % 2], 32 * (e // 2 + 1))
                halves(w_hi[:, e % 2, :], w_lo[:, e % 2, :], e_raw[:, e % 2, :]).then_inc(w_split, 1)

            def moe():
                split_weights(0)
                for q in range(NM * B):
                    e, b = divmod(q, B)
                    for n in range(HC):
                        c = q * HC + n
                        dve.wait_ge(e_gelu, c + 1)
                        if c >= HC:
                            dve.wait_ge(e_down, c - HC + 1)
                        halves(g_hi[:, n, :], g_lo[:, n, :], g_raw[:, n % 2, :]).then_inc(e_split, 1)
                        if n == LAG and q:
                            if e >= 1:
                                dve.wait_ge(settled, q - 1)
                            settle(q - 1)
                    if b == 0 and e + 1 < NM:
                        split_weights(e + 1)
                settle(NM * B - 1)
                for b in range(B):
                    dve.wait_ge(accT_ps, b + 1)
                    if b:
                        dve.wait_ge(y_out_ready, b)
                    one(tt(fl(fa), (bank_o, bank_m)[b % 2][:, :], x2[:, b, :], ALU.add))
                    norm(B - 1, NORMS + b, fa, y_out[:, b, :, :]).then_inc(y_out_ready, 1)

            for b in range(B):
                attention(b)
                rest(b)
            moe()


_INS = ["x", "ctx_768", "mask_BxS_bf1", "mask_BxS2_bf1", "L0_attn_w_q", "L0_attn_w_k", "L0_attn_w_v", "L0_attn_w_o",
        "L0_xattn_Wq", "L0_xattn_Wk", "L0_xattn_Wv", "L0_xattn_W_film_in", "L0_xattn_b_film_in", "L0_xattn_W_film_out",
        "L0_xattn_b_film_out", "L0_xattn_g_norm_in", "L0_xattn_b_norm_in", "L0_xattn_g_norm_out",
        "L0_xattn_b_norm_out", "L0_xattn_g_ffn", "L0_xattn_b_ffn", "L0_xattn_W1", "L0_xattn_b1", "L0_xattn_W2",
        "L0_xattn_b2", "L0_xattn_log_dt", "L0_xattn_A_re", "L0_xattn_A_im", "L0_xattn_C_re", "L0_xattn_C_im",
        "L0_xattn_D_skip", "L0_xattn_mod_gate", "L0_ffn_rW", "L0_ffn_rb", "L0_ffn_W1", "L0_ffn_b1", "L0_ffn_W2",
        "L0_ffn_b2", "L0_ffn_sW1", "L0_ffn_sb1", "L0_ffn_sW2", "L0_ffn_sb2"]


def constants():
    n = np.arange(SEQ)
    turn = 2 * np.pi * np.outer(n, n) / (2 * SEQ)
    alternate = (-1.0) ** n
    sin_fwd, sin_inv = np.sin(turn), np.sin(turn)
    sin_fwd[:, 0] = alternate
    sin_inv[0, :] = alternate
    freq = 1.0 / 10000.0 ** (np.arange(0, HD, 2, dtype=np.float32) / np.float32(HD))
    angle = (n.astype(np.float32)[:, None] * freq.astype(np.float32)[None, :]).astype(np.float64)
    c, s = np.cos(angle), np.sin(angle)
    rope = np.stack([np.concatenate([c, c], 1), np.concatenate([-s, s], 1)], 1)
    rope = rope.reshape(NT, P, 2, HD).transpose(1, 0, 2, 3).reshape(P, -1)
    offs = np.zeros((P, 4))
    offs[:NS, 0], offs[NS:, 1] = 0.25, 0.25
    offs[:, 2:4] = offs[:, 0:2] * SIN_SCALE
    pair_sum = np.tile(np.eye(64), (2, 1))
    earlier = (np.arange(NE)[None, :] < np.arange(NE)[:, None]).astype(np.float32).reshape(-1)
    tables = dict(c_cos=np.cos(turn), c_sin_fwd=sin_fwd, c_sin_inv=sin_inv, c_rope=rope, c_offs=offs,
                  c_pair_sum=pair_sum, c_earlier=earlier, c_ident=np.eye(P), c_index=np.arange(JM))
    return {k: np.ascontiguousarray(v, dtype=np.float32) for k, v in tables.items()}


def kernel(**inputs):
    import numpy as _np
    import concourse.bacc as _bacc
    from concourse import mybir as _mybir
    from concourse.bass_utils import run_bass_kernel_spmd as _run

    nc = _bacc.Bacc("TRN2", target_bir_lowering=False, num_devices=1)
    arrays, args = {}, {}
    for name in _INS:
        a = _np.ascontiguousarray(inputs[name])
        if a.ndim == 0:
            a = a.reshape(1)
        arrays[f"in_{name}"] = a
    for name, a in constants().items():
        arrays[f"in_{name}"] = a
    for name, a in arrays.items():
        args[name[3:]] = nc.dram_tensor(name, a.shape, _mybir.dt.from_np(a.dtype), kind="ExternalInput").ap()
    out = nc.dram_tensor("out_0", (B, SEQ, D), F32, kind="ExternalOutput").ap()
    build(nc, args, out)
    r = _run(nc, [arrays], core_ids=[0])
    return r.results[0]["out_0"]
```

```python
from contextlib import ExitStack

import numpy as np
import concourse.bass as bass
from concourse import mybir

F32 = mybir.dt.float32
F32R = mybir.dt.float32r
BF16 = mybir.dt.bfloat16
I32 = mybir.dt.int32
U8 = mybir.dt.uint8
ALU = mybir.AluOpType
ACT = mybir.ActivationFunctionType
AX = mybir.AxisListType.X

P = 128
B, SEQ, D = 4, 512, 128
NT = SEQ // P
NH, NKV, HD = 16, 4, 8
QK = (NH + NKV) * HD
QKV = QK + NKV * HD
LAG = 3
CAP, EPS = 50.0, 1e-5
PARTS = 8
G, DV, XH, XD = 32, 96, 4, 32
NS = 64
HID = 512
HC = HID // P
NE, NSH = 8, 2
NM = NSH + NE
NX = 1 + NM
NPAIR = NH // 2
PW = 5 * SEQ
JM, IM = 32, SEQ // 32
MAGIC = 12582912.0
TWO_PI = 6.283185307179586
TURN = 6.283185
SIN_SCALE = TWO_PI * (1 - 2.5e-6)
LN2_HI, LN2_LO = 0.693145751953125, 1.42860682030941723212e-6

ROW_B1, ROW_B2, ROW_LDT = 0, HC * NX, (HC + 1) * NX
ROWS = ROW_LDT + 1
S_QT, S_SC = 0, 6
U_FILM, U_DFT, U_FILLS = 0, 4, 6
S_PREP = 4
FILLS = [(r, tiles) for tiles in ([(0, 0)], [(1, 0), (3, 384)], [(2, 0)]) for r in range(2)]
BASE = [0, SEQ, 2 * SEQ, 3 * SEQ, 4 * SEQ, 4 * SEQ + 256]
WIDTH = [SEQ, SEQ, SEQ, SEQ, 256, 256]
NF = len(FILLS)
S_FILLS = S_SC + NF * NPAIR + S_PREP
COL = {(r, j): BASE[n] + c for n, (r, tiles) in enumerate(FILLS) for j, c in tiles}

XT_AT, QKV_AT = (4, 1), (5, 1)
STEPS = [
    (-1, *XT_AT, "xT"), (-1, *QKV_AT, "qkv"), (-1, 5, 4, "rms"), (-1, 6, 0, "rope"), (-1, 7, 1, "parts"),
    (3, 0, 3, "x2T"), (3, 1, 0, "gates"), (3, 1, 2, "gates_exp"), (3, 1, 3, "route"), (3, 2, 0, "wT"),
    (2, 0, 0, "dft", 4), (2, 0, 1, "dft", 5), (2, 0, 2, "dft", 6), (2, 0, 2, "dft", 7), (2, 0, 5, "spectrum"),
    *[(2, 1 + (1 + n) // NF, (1 + n) % NF, "conv", n) for n in range(8)],
    (1, 2, 2, "yT"), (2, 2, 3, "shape_out"), (1, 2, 5, "proj"), (2, 3, 4, "hT"), (1, 3, 5, "x1T"),
    *[(2, 4, n, "up", n) for n in range(HC)], (1, 4, 1, "scores"), (1, 4, 2, "x_norm"),
    (2, 4, 4, "gelu"), (1, 4, 5, "cross_exp"), (1, 5, 0, "soften"),
    *[(2, 5, 2 + n, "down", n) for n in range(HC)], (1, 5, 3, "attnT"), (2, 6, 0, "ff_out"),
    *[(1, 6, 1 + n, "film", n) for n in range(NT)], (2, 6, 2, "ffT"), (2, 6, 3, "ff_norm"), (1, 6, 5, "modulate"),
    *[(1, 7, 2 + n, "dft", n) for n in range(4)], (2, 7, 3, "x2"),
]
ONCE = [
    (0, 0, 1, "vectors"), (0, 0, 3, "fold1"), (0, 1, 1, "fold2"), (0, 1, 3, "fold3"), (0, 2, 1, "fold4"),
    (0, 2, 3, "states"), (0, 3, 1, "pack"), (0, 3, 2, "args", 0),
    *[(0, 4 + q, n, name, q + (name == "args")) for q in range(D // JM)
      for n, name in ((0, "powers"), (3, "taps"), (5, "args"))],
    (1, 1, 1, "first_tap"), *[(1, 1 + (2 + n) // NF, (2 + n) % NF, "kernel", n) for n in range(2 * NT)],
    (1, 3, 1, "spectra"), (1, 3, 3, "text_weights"),
]
LOOK = 2
PRODUCTS = [(e, b) for rows in ((0, 1), (2,), (3,)) for e in range(NSH) for b in rows]
PRODUCTS += [(e, b) for e in range(NSH, NM) for b in range(B)]
CHUNKS = HC * len(PRODUCTS)
EARLY_AT = [(B, p, n) for p in range(4, NPAIR) for n in range(NF)][:4 * HC]
EARLY_AT += [(B + 1, p, n) for p in range(2, 6) for n in range(0, NF, 2)][:2 * HC]
EARLY_AT += [(B + 2, p, n) for p in range(2) for n in range(NF)][7:]
EARLY = len(EARLY_AT)
EARLY_CHUNKS = [(*at, c) for c, at in enumerate(EARLY_AT)]
FINAL_AT = [CHUNKS - HC * (B - 1 - b) + HC for b in range(B - 1)]


def fill_index(b, what, p=0, n=0):
    if what in ("xT", "qkv"):
        own = n + (2 if what == "qkv" else 0)
        if b == 0:
            return own
        at = XT_AT if what == "xT" else QKV_AT
        return S_PREP + (b - 1) * S_FILLS + S_SC + NF * at[0] + at[1] + 1 + own
    k = S_PREP + b * S_FILLS
    if what == "qT":
        return k + S_QT + n
    extra = 2 * ((p, n) > XT_AT) + 2 * ((p, n) > QKV_AT) if b + 1 < B else 0
    return k + S_SC + NF * p + n + extra


def run(parts, i, p, n):
    for at, q, m, name, *part in ONCE:
        if (at, q, m) == (i, p, n) and name in parts:
            parts[name](*part)
    for after, q, m, name, *part in STEPS:
        b = i - after
        if (q, m) == (p, n) and 0 <= b < B and name in parts:
            parts[name](b, *part)
    for at, q, m, c in EARLY_CHUNKS:
        if (at, q, m) == (i, p, n) and "chunk" in parts:
            parts["chunk"](c)


def iterate(parts, first, fill, close, late=False):
    for name in ("xT", "qkv", "rms", "rope", "parts"):
        if name in parts:
            parts[name](0)
    for i in range(B + 3):
        if i < B:
            first(i)
        for p in range(NPAIR):
            for n in range(NF):
                if i < B:
                    fill(i, p, n)
                slot = NPAIR * i + p - 1
                if late and n == LOOK - 1 and 0 <= slot < NPAIR * (B + 1):
                    close(*divmod(slot, NPAIR))
                run(parts, i, p, n)
            if i <= B and not late:
                close(i, p)


def build(nc, t, out):
    ctx = ExitStack()
    with ctx:
        def sb(name, shape, dt=F32):
            return ctx.enter_context(nc.sbuf_tensor(name, shape, dt))

        def sem(name):
            return ctx.enter_context(nc.semaphore(name))

        ring_s = [ctx.enter_context(nc.psum_tensor(f"ring_s{i}", [P, 512], F32)) for i in range(2)]
        ring_u = [ctx.enter_context(nc.psum_tensor(f"ring_u{i}", [P, 512], F32)) for i in range(2)]
        bank_o = ctx.enter_context(nc.psum_tensor("bank_o", [P, 512], F32))
        bank_m = ctx.enter_context(nc.psum_tensor("bank_m", [P, 512], F32))
        bank_d = ctx.enter_context(nc.psum_tensor("bank_d", [P, 512], F32))
        bank_r = ctx.enter_context(nc.psum_tensor("bank_r", [P, 512], F32))
        taps_ps = [bank_d, bank_r]
        experts_up = [ring_s[0], ring_s[1], ring_u[0], ring_u[1]]
        down = [bank_o, bank_m]
        text_up = [ring_u[0], ring_u[1], bank_d, bank_r]

        wqkv = sb("wqkv", [P, QKV])
        wo = sb("wo", [P, D])
        ident = sb("ident", [P, P])
        identb = sb("identb", [P, P], BF16)
        pair_sum = sb("pair_sum", [P, 64])
        rope = sb("rope", [P, NT, 2, HD])
        wt_hi = sb("wt_hi", [P, 2 * HID], F32R)
        wt_lo = sb("wt_lo", [P, 2 * HID], F32R)
        vcols = sb("vcols", [P, ROWS])
        b2_shared = sb("b2_shared", [P, 1])
        norms = sb("norms", [P, 6, D])
        film_bias = sb("film_bias", [P, 4 * D])
        router_w = sb("router_w", [P, NE])
        router_b = sb("router_b", [P, NE])
        earlier = sb("earlier", [P, NE, NE])
        spread = sb("spread", [2 * NE, NE], F32R)
        neg_half = sb("neg_half", [P, NT])
        cosm = sb("cosm", [P, NT, SEQ])
        sin_fwd = sb("sin_fwd", [P, NT, SEQ])
        sin_inv = sb("sin_inv", [P, NT, SEQ])
        kc = sb("kc", [P, NT, D])
        ks = sb("ks", [P, NT, D])
        kcn = sb("kcn", [P, NT, D])
        xq = sb("xq", [P, B, XH * G])
        vf = sb("vf", [P, B, 4 * D])
        ctx_bias = sb("ctx_bias", [P, B, XH, G])
        tmask = sb("tmask", [P, B * NT])
        gate = sb("gate", [P, 1])
        gate4 = sb("gate4", [P, 1])

        scratch = ExitStack()
        with scratch:
            def tb(name, shape, dt=F32):
                return scratch.enter_context(nc.sbuf_tensor(name, shape, dt))
            vec_rows = tb("vec_rows", [ROWS, P])
            tm_rows8 = tb("tm_rows8", [B * NT, P], U8)
            tm_rows = tb("tm_rows", [B * NT, P])
            cmask8 = tb("cmask8", [P, B * G], U8)
            cmask = tb("cmask", [P, B * G])
            dskip = tb("dskip", [1, D])
            s4 = tb("s4", [P, 4, NS])
            sm = tb("sm", [P, 12, NS])
            dtc = tb("dtc", [P, 8])
            dti = tb("dti", [P, 2], I32)
            packs = tb("packs", [P, 4, P])
            pk = tb("pk", [P, 4, P])
            pk32 = tb("pk32", [P, 3, P])
            index = tb("index", [P, JM])
            offs = tb("offs", [P, 4])
            pv = tb("pv", [P, JM, JM])
            pt = tb("pt", [P, JM, JM])
            pr = tb("pr", [P, JM, JM])
            wt_raw = pr[:, :, :].rearrange("p a b -> p (a b)")
            uf = tb("uf", [P, JM, IM])
            ug = tb("ug", [P, JM, IM])
            ue = tb("ue", [P, JM, IM])
            kld = pv[:, 0:NT * D // JM, :].rearrange("p a c -> p (a c)").rearrange("p (j d) -> p j d", j=NT)
            ctxs = tb("ctxs", [P, DV])
            ctxT = tb("ctxT", [DV, B * G])
            ctx_rep = uf[0:DV, :, :].rearrange("p a c -> p (a c)").rearrange("p (b n) -> p b n", b=B)
            wk = tb("wk", [DV, P])
            wv = tb("wv", [DV, D])
            wq = tb("wq", [P, P])
            wqT = tb("wqT", [P, P])
            wvT = tb("wvT", [P, DV])
            w_film = tb("w_film", [P, 4 * D])
            kbd = tb("kbd", [P, B * XH * G])
            kij = tb("kij", [IM, JM, D])
            wvf = ug[0:DV, :, :].rearrange("p a c -> p (a c)")

        x2 = sb("x2", [P, B, NT * D])
        t_hi = sb("t_hi", [P, B, SEQ], F32R)
        t_lo = sb("t_lo", [P, B, SEQ], F32R)
        wT = sb("wT", [2 * NE, B, SEQ], F32R)
        g_raw = sb("g_raw", [P, HC, SEQ])
        g_hi = sb("g_hi", [P, HC, SEQ], F32R)
        g_lo = sb("g_lo", [P, HC, SEQ], F32R)
        fa = sb("fa", [P, NT, D])
        ffT = fa[:, :, :].rearrange("p j d -> p (j d)")
        stats = sb("stats", [P, NT, 6])
        mean_var = sb("mean_var", [P, NT, 2])
        var_eps = sb("var_eps", [P, NT])
        rstd = sb("rstd", [P, NT])

        experts = ExitStack()
        with experts:
            def eb(name, shape, dt=F32):
                return experts.enter_context(nc.sbuf_tensor(name, shape, dt))
            w_hi = eb("w_hi", [P, 2, 2 * HID], F32R)
            w_lo = eb("w_lo", [P, 2, 2 * HID], F32R)
            e_raw = eb("e_raw", [P, 2, 2 * HID])
            acc = eb("acc", [P, B, SEQ])
            w_bc = eb("w_bc", [P, 2, SEQ])
            term = eb("term", [P, SEQ])
            eg_raw = eb("eg_raw", [P, HC, SEQ])
            eg_hi = eb("eg_hi", [P, HC, SEQ], F32R)
            eg_lo = eb("eg_lo", [P, HC, SEQ], F32R)

        x_in = sb("x_in", [P, 2, NT, D])
        xT = sb("xT", [P, SEQ])
        qkv = sb("qkv", [P, NT, QKV])
        qT = sb("qT", [P, NPAIR, SEQ], BF16)
        kT = sb("kT", [P, NKV, SEQ], BF16)
        vv = sb("vv", [P, NT, NKV, 32])
        probs = sb("probs", [P, 2, PW])
        oT = sb("oT", [P, 2, SEQ])
        ry = sb("ry", [P, NT, 2])
        y_att = sb("y_att", [P, NT, D])
        yT = xT
        qs = sb("qs", [P, NT * NH, PARTS, HD], BF16)
        tmp_c = sb("tmp_c", [P, NT * QK])[:, :]
        k_parts = sb("k_parts", [P, NT * NKV, 2, PARTS, HD], BF16)
        rms_in = sb("rms_in", [P, NT * (NH + NKV)])
        rms_out = sb("rms_out", [P, NT * (NH + NKV)])
        rms_tmp = sb("rms_tmp", [P, NT * (NH + NKV)])
        rms_bits = rms_out[:, :].bitcast(I32)

        x1 = sb("x1", [P, 2, NT, D])

        x1T = sb("x1T", [P, SEQ])
        sc = sb("sc", [P, NT * XH, G])
        sc_max = sb("sc_max", [P, NT * XH])
        sc_sum = sb("sc_sum", [P, NT * XH])
        attnT = x1T
        film = sb("film", [P, NT, 4 * D])
        xn = sb("xn", [P, NT, D])
        fb = sb("fb", [P, NT, D])
        spec = sb("spec", [P, 2 * NT, D])
        tmp_b = spec[:, 0:NT * QK // D, :].rearrange("p n d -> p (n d)")
        xt = sb("xt", [P, NT, D])
        x2T = attnT
        gates = sb("gates", [P, NT, NE])
        gmax = sb("gmax", [P, NT])
        cmp_a, cmp_b = (fb[:, 2 * k:2 * k + 2, :].rearrange("p a (j e f) -> p (a j) e f", j=2, e=NE) for k in range(2))
        chosen = sb("chosen", [P, NT, NE])
        w_tok = sb("w_tok", [P, NT, NE])
        w_round = sb("w_round", [P, NT, NE], F32R)
        w_parts = sb("w_parts", [P, NT, 2 * NE])

        ld_attn, ld_s4, ld_vec, ld_cross, ld_dft, ld_rest, ld_wt = (
            sem(n) for n in ("ld_attn", "ld_s4", "ld_vec", "ld_cross", "ld_dft", "ld_rest", "ld_wt"))
        ld_w = [sem(f"ld_w{i}") for i in range(2)]
        w_split = sem("w_split")
        x_landed = sem("x_landed")
        x_used = sem("x_used")
        out_sent = sem("out_sent")
        consts_ready = sem("consts_ready")
        pro_pe = sem("pro_pe")
        pro_sb = sem("pro_sb")
        pro_arg = sem("pro_arg")
        pro_fun = sem("pro_fun")
        kij_ready = sem("kij_ready")
        kij_sent = sem("kij_sent")
        kld_landed = sem("kld_landed")
        kconst_ready = sem("kconst_ready")
        wt_split = sem("wt_split")
        s_full = sem("s_full")
        s_free = sem("s_free")
        u_full = sem("u_full")
        u_free = sem("u_free")
        var_ready = sem("var_ready")
        rstd_ready = sem("rstd_ready")
        rms_ready, roped, parts_ready, v_ready = (sem(n) for n in ("rms_ready", "roped", "parts_ready", "v_ready"))
        exp_done = sem("exp_done")
        masked = sem("masked")
        pv_done = sem("pv_done")
        oT_ready = sem("oT_ready")
        y_ps = sem("y_ps")
        y_ready = sem("y_ready")
        yT_ps, yT_sb, proj_ps, x1_ready = (sem(n) for n in ("yT_ps", "yT_sb", "proj_ps", "x1_ready"))
        x1T_ps, x1T_sb, sc_ps = (sem(n) for n in ("x1T_ps", "x1T_sb", "sc_ps"))
        sc_ready, sc_exp, attn_ready, attnT_ps, attnT_sb = (sem(n) for n in (
            "sc_ready", "sc_exp", "attn_ready", "attnT_ps", "attnT_sb"))
        xn_scaled, xn_ready, xmod_ready, spec_ready, conv_ps = (sem(n) for n in (
            "xn_scaled", "xn_ready", "xmod_ready", "spec_ready", "conv_ps"))
        h_scaled, h_ready, hT_ps, hT_sb = (sem(n) for n in ("h_scaled", "h_ready", "hT_ps", "hT_sb"))
        up_ps = sem("up_ps")
        gelu_done = sem("gelu_done")
        split_done = sem("split_done")
        down_ps, ffT_sb, ffn_tok, tok_used = (sem(n) for n in ("down_ps", "ffT_sb", "ffn_tok", "tok_used"))
        ff_scaled, sum_ready, x2_ready, x2T_ps, x2T_sb, x2_split = (sem(n) for n in (
            "ff_scaled", "sum_ready", "x2_ready", "x2T_ps", "x2T_sb", "x2_split"))
        gates_ps, gates_ready, gates_exp, wtok_ready, wT_ps, wT_sb = (sem(n) for n in (
            "gates_ps", "gates_ready", "gates_exp", "wtok_ready", "wT_ps", "wT_sb"))
        e_up, e_gelu, e_split, e_down = (sem(n) for n in ("e_up", "e_gelu", "e_split", "e_down"))
        bc_ps, bc_sb, settled, accT_ps = (sem(n) for n in ("bc_ps", "bc_sb", "settled", "accT_ps"))
        y_out_ready = sem("y_out_ready")
        acc_used = sem("acc_used")
        dve_step = sem("dve_step")
        pool_step = sem("pool_step")

        x_dram = t["x"]
        kernel_dram = nc.dram_tensor("s4d_kernel", (SEQ, D), F32, kind="Internal").ap()
        block = ctx.enter_context(nc.Block())

        @block.sync
        def _(sp):
            def load(dst, src, s):
                sp.dma_start(dst, src).then_inc(s, 16)

            def load_x(b):
                if b >= 2:
                    sp.wait_ge(x_used, b - 1)
                load(x_in[:, b % 2, :, :], x_dram[b].rearrange("(j p) d -> p j d", p=P), x_landed)

            load_x(0)
            load(ident[:, :], t["c_ident"], ld_attn)
            load(wqkv[:, 0:NH * HD], t["L0_attn_w_q"], ld_attn)
            load(wqkv[:, NH * HD:QK], t["L0_attn_w_k"], ld_attn)
            load(wqkv[:, QK:QKV], t["L0_attn_w_v"], ld_attn)
            load(rope[:, :, :, :].rearrange("p j c e -> p (j c e)"), t["c_rope"], ld_attn)
            load(wo[:, :], t["L0_attn_w_o"], ld_attn)
            load(pair_sum[:, :], t["c_pair_sum"], ld_attn)
            for n, k in enumerate(("A_re", "A_im", "C_re", "C_im")):
                load(s4[:, n, :], t[f"L0_xattn_{k}"], ld_s4)
            load(index[:, :], t["c_index"].partition_broadcast(P), ld_s4)
            load(offs[:, :], t["c_offs"], ld_s4)
            load(dskip[:, :], t["L0_xattn_D_skip"].rearrange("(c p) -> c p", p=P), ld_s4)
            load_x(1)
            for m, k in ((cosm, "c_cos"), (sin_fwd, "c_sin_fwd"), (sin_inv, "c_sin_inv")):
                load(m[:, :, :], t[k].rearrange("(j p) f -> p j f", p=P), ld_dft)
            for n, k in enumerate(("g_norm_in", "b_norm_in", "g_ffn", "b_ffn", "g_norm_out", "b_norm_out")):
                load(norms[:, n, :], t[f"L0_xattn_{k}"].partition_broadcast(P), ld_rest)
            load(router_w[:, :], t["L0_ffn_rW"], ld_rest)
            load(router_b[:, :], t["L0_ffn_rb"].partition_broadcast(P), ld_rest)
            load(earlier[:, :, :].rearrange("p a b -> p (a b)"), t["c_earlier"].partition_broadcast(P), ld_rest)
            sp.wait_ge(kij_ready, 1)
            load(kernel_dram.rearrange("(i j) d -> i (j d)", i=IM), kij.rearrange("i j d -> i (j d)"), kij_sent)
            sp.wait_ge(kij_sent, 16)
            load(kld, kernel_dram.rearrange("(j p) d -> p j d", p=P), kld_landed)
            load(wt_raw[:, 0:HID], t["L0_xattn_W1"], ld_wt)
            load(wt_raw[:, HID:2 * HID].rearrange("p (c d) -> p c d", c=HC),
                 t["L0_xattn_W2"].rearrange("(c p) d -> p c d", p=P), ld_wt)
            for b in range(2, B):
                load_x(b)
            sp.wait_ge(x1_ready, B)
            for e in range(NM):
                if e >= 2:
                    sp.wait_ge(w_split, e - 1)
                w1, w2 = (t["L0_ffn_sW1"][e], t["L0_ffn_sW2"][e]) if e < NSH else (
                    t["L0_ffn_W1"][e - NSH], t["L0_ffn_W2"][e - NSH])
                load(e_raw[:, e % 2, 0:HID], w1, ld_w[e % 2])
                load(e_raw[:, e % 2, HID:2 * HID].rearrange("p (c d) -> p c d", c=HC),
                     w2.rearrange("(c p) d -> p c d", p=P), ld_w[e % 2])
            for b in range(B):
                sp.wait_ge(y_out_ready, b + 1)
                sp.dma_start(out[b].rearrange("(j p) d -> p j d", p=P), x2[:, b, :].rearrange("p (j d) -> p j d", j=NT)).then_inc(out_sent, 16)
            sp.wait_ge(out_sent, 16 * B)

        @block.tensor
        def _(pe):
            mm = nc.tensor.matmul

            def tp(dst, src):
                return nc.tensor.transpose(dst, src, ident[0:src.shape[0], 0:src.shape[0]])

            def s_fill(k):
                if k >= 2:
                    pe.wait_ge(s_free, k - 1)
                return ring_s[k % 2]

            def vectors():
                pe.wait_ge(ld_vec, 16 * 7)
                tp(bank_d[:, 0:ROWS], vec_rows[:, :]).then_inc(pro_pe, 1)

            def fold1():
                pe.wait_ge(ld_cross, 16 * 11)
                tp(bank_r[:, 0:P], wq[:, :])
                tp(bank_r[0:DV, P:2 * P], ctxs[:, :])
                tp(bank_r[:, 2 * P:2 * P + DV], wv[:, :])
                pe.wait_ge(pro_sb, 1)
                tp(bank_r[:, 3 * P:3 * P + B * NT], tm_rows[:, :]).then_inc(pro_pe, 1)

            def fold2():
                pe.wait_ge(pro_sb, 2)
                mm(ring_u[0][:, 0:B * G], wk[:, :], ctxT[:, :], start=True, stop=True).then_inc(pro_pe, 1)
                mm(ring_u[1][0:DV, :], wvT[:, :], w_film[:, :], start=True, stop=True).then_inc(pro_pe, 1)

            def fold3():
                pe.wait_ge(pro_sb, 3)
                mm(bank_d[:, :], wqT[:, :], kbd[:, :], start=True, stop=True).then_inc(pro_pe, 1)

            def fold4():
                pe.wait_ge(pro_sb, 5)
                for b in range(B):
                    dst = (bank_r, ring_u[0], ring_u[1], bank_d)[b]
                    mm(dst[:, :], ctx_rep[:, b, :], wvf, start=True, stop=True).then_inc(pro_pe, 1)

            def pack():
                pe.wait_ge(pro_sb, 6)
                for n in range(4):
                    last = tp(ring_u[0][:, n * P:(n + 1) * P], packs[:, n, :])
                last.then_inc(pro_pe, 1)

            def taps(q):
                pe.wait_ge(pro_sb, 7 + q)
                for h in range(2):
                    for d in range(16):
                        last = mm(taps_ps[h][0:IM, JM * d:JM * (d + 1)], uf[:, 16 * h + d, :], pv[:, 16 * h + d, :],
                                  start=True, stop=True)
                last.then_inc(pro_pe, 1)

            def kernel_dft(f):
                if f == 0:
                    pe.wait_ge(kconst_ready, 1)
                    pe.wait_ge(ld_dft, 48)
                mat, c = (cosm, f) if f < NT else (sin_fwd, f - NT)
                for j in range(NT):
                    last = mm(ring_u[f // NT][:, P * c:P * (c + 1)], mat[:, j, P * c:P * (c + 1)],
                              kld[:, j, :], start=(j == 0), stop=(j == NT - 1))
                if f == 2 * NT - 1:
                    last.then_inc(pro_pe, 1)

            def xT_step(b):
                pe.wait_ge(x_landed, 16 * (b + 1))
                if b == 0:
                    pe.wait_ge(ld_attn, 16 * 7)
                for n in range(2):
                    bank = s_fill(fill_index(b, "xT", n=n))
                    for j in range(2):
                        last = tp(bank[:, P * j:P * (j + 1)], x_in[:, b % 2, 2 * n + j, :])
                    last.then_inc(s_full, 1)

            def qkv_step(b):
                pe.wait_ge(s_free, fill_index(b, "xT", n=1) + 1)
                for n in range(2):
                    bank = s_fill(fill_index(b, "qkv", n=n))
                    for j in range(2):
                        k = 2 * n + j
                        last = mm(bank[:, QKV * j:QKV * (j + 1)], xT[:, P * k:P * (k + 1)], wqkv[:, :],
                                  start=True, stop=True)
                    last.then_inc(s_full, 1)

            def first(b):
                if b == 0:
                    pe.wait_ge(consts_ready, 1)
                pe.wait_ge(parts_ready, b + 1)
                for n in range(6):
                    bank = s_fill(fill_index(b, "qT", n=n))[:, :].bitcast(BF16).rearrange("p (a j q) -> p a j q", a=2, j=NT)
                    for a in range(2):
                        for j in range(NT):
                            if n < 4:
                                src = qs[:, j * NH + 2 * (2 * n + a):j * NH + 2 * (2 * n + a) + 2, :, :]
                                src = src.rearrange("p n c e -> p (n c e)")
                            else:
                                src = k_parts[:, j * NKV + 2 * (n - 4) + a, :, :, :].rearrange("p n c e -> p (n c e)")
                            last = nc.tensor.transpose(bank[:, a, j, :], src, identb[:, :])
                    last.then_inc(s_full, 1)
                pe.wait_ge(s_free, fill_index(b, "qT", n=5) + 1)

            def fill(b, p, n):
                r, tiles = FILLS[n]
                bank = s_fill(fill_index(b, "sc", p, n))
                for j, c in tiles:
                    w = SEQ - P * j
                    last = mm(bank[:, c:c + w], kT[64 * r:64 * r + 64, p // 2, P * j:P * (j + 1)],
                              qT[64 * r:64 * r + 64, p, P * j:SEQ], start=True, stop=True)
                last.then_inc(s_full, 1)

            def values(pair):
                b, p = divmod(pair, NPAIR)
                pe.wait_ge(masked, pair + 1)
                if pair >= 1:
                    pe.wait_ge(oT_ready, pair)
                if p == 0:
                    pe.wait_ge(v_ready, b + 1)
                if p == 1 and b:
                    pe.wait_ge(x_used, b)
                for start in (True, False):
                    for s in range(4):
                        r, j = s % 2, ((0, 3), (1, 2))[s // 2][0 if start else 1]
                        c = COL[(r, j)]
                        last = mm(bank_o[32 * s:32 * s + 32, P * j:SEQ], vv[:, j, p // 2, :],
                                  probs[:, p % 2, c:c + SEQ - P * j], start=start, stop=not start)
                last.then_inc(pv_done, 1)

            def token_rows(pair):
                b, p = divmod(pair, NPAIR)
                pe.wait_ge(oT_ready, pair + 1)
                if pair >= 1:
                    pe.wait_ge(y_ready, pair)
                if p == 0 and b:
                    pe.wait_ge(yT_sb, b)
                for j in range(NT):
                    c = 256 * (p % 2) + 64 * j
                    last = mm(bank_m[:, c:c + 64], oT[:, p % 2, P * j:P * (j + 1)], pair_sum[:, :],
                              start=True, stop=True)
                last.then_inc(y_ps, 1)

            def close(i, p):
                pair = i * NPAIR + p - 1
                if 0 <= pair < B * NPAIR:
                    values(pair)
                if 0 <= pair - 1 < B * NPAIR:
                    token_rows(pair - 1)

            def yT_step(b):
                pe.wait_ge(y_ready, NPAIR * (b + 1))
                for j in range(NT):
                    last = tp(bank_m[:, P * j:P * (j + 1)], y_att[:, j, :])
                last.then_inc(yT_ps, 1)

            def proj(b):
                pe.wait_ge(yT_sb, b + 1)
                pe.wait_ge(oT_ready, NPAIR * (b + 1) + (b + 1 < B))
                for j in range(NT):
                    last = mm(bank_o[:, P * j:P * (j + 1)], yT[:, P * j:P * (j + 1)], wo[:, :], start=True, stop=True)
                last.then_inc(proj_ps, 1)

            def three(bank, hi, lo, a_hi, a_lo, start, stop):
                for k, (w, a) in enumerate(((hi, a_hi), (hi, a_lo), (lo, a_hi))):
                    last = mm(bank[:, :], w, a, start=(start and k == 0), stop=(stop and k == 2))
                return last

            def x1T_step(b):
                pe.wait_ge(x1_ready, b + 1)
                if b:
                    pe.wait_ge(hT_sb, b)
                for j in range(NT):
                    last = tp(bank_r[:, P * j:P * (j + 1)], x1[:, b % 2, j, :])
                last.then_inc(x1T_ps, 1)

            def scores(b):
                pe.wait_ge(x1T_sb, b + 1)
                if b:
                    pe.wait_ge(h_scaled, b)
                for j in range(NT):
                    last = mm(bank_d[:, P * j:P * (j + 1)], x1T[:, P * j:P * (j + 1)], xq[:, b, :], start=True, stop=True)
                last.then_inc(sc_ps, 1)

            def attnT_step(b):
                pe.wait_ge(attn_ready, b + 1)
                if b:
                    pe.wait_ge(gelu_done, HC * b)
                for j in range(NT):
                    last = tp(bank_r[:, P * j:P * (j + 1)], sc[:, XH * j:XH * (j + 1), :].rearrange("p h g -> p (h g)"))
                last.then_inc(attnT_ps, 1)

            def film_step(b, j):
                if j == 0:
                    pe.wait_ge(attnT_sb, b + 1)
                    if b:
                        pe.wait_ge(ffT_sb, b)
                if j >= 2:
                    pe.wait_ge(u_free, b * U_FILLS + j - 1)
                mm(ring_u[j % 2][:, :], attnT[:, P * j:P * (j + 1)], vf[:, b, :], start=True, stop=True).then_inc(u_full, 1)

            def dft(b, n):
                f, c = divmod(n, NT)
                if n == 0:
                    pe.wait_ge(xmod_ready, b + 1)
                mat = (cosm, sin_fwd)[f]
                for j in range(NT):
                    last = mm(ring_u[f][:, P * c:P * (c + 1)], mat[:, j, P * c:P * (c + 1)], xn[:, j, :],
                              start=(j == 0), stop=(j == NT - 1))
                if c == NT - 1:
                    last.then_inc(u_full, 1)

            def conv(b, n):
                if n == 0:
                    pe.wait_ge(spec_ready, b + 1)
                j, half = divmod(n, 2)
                for f in range(NT * half, NT * (half + 1)):
                    mat = cosm if f < NT else sin_inv
                    last = mm(bank_d[:, P * j:P * (j + 1)], mat[:, f % NT, P * j:P * (j + 1)], spec[:, f, :],
                              start=(f == 0), stop=(f == 2 * NT - 1))
                if n == 2 * NT - 1:
                    last.then_inc(conv_ps, 1)

            def hT_step(b):
                pe.wait_ge(h_ready, b + 1)
                if b:
                    pe.wait_ge(wT_sb, b)
                for j in range(NT):
                    last = tp(bank_r[:, P * j:P * (j + 1)], fa[:, j, :])
                last.then_inc(hT_ps, 1)

            def up_step(b, n):
                if n == 0:
                    pe.wait_ge(wt_split, 1)
                    pe.wait_ge(hT_sb, b + 1)
                if n == 2 and b + 1 < B:
                    pe.wait_ge(sc_ready, b + 2)
                if n == 3 and b + 1 < B:
                    pe.wait_ge(x1T_sb, b + 2)
                c = slice(P * n, P * (n + 1))
                three(text_up[n], wt_hi[:, c], wt_lo[:, c], t_hi[:, b, :], t_lo[:, b, :], True, True).then_inc(up_ps, 1)

            def down_step(b, n):
                if n == 0:
                    pe.wait_ge(gelu_done, b * HC + 1)
                pe.wait_ge(split_done, b * HC + n + 1)
                c = slice(HID + P * n, HID + P * (n + 1))
                last = three(ring_u[0], wt_hi[:, c], wt_lo[:, c], g_hi[:, n, :], g_lo[:, n, :], n == 0, n == HC - 1)
                if n == HC - 1:
                    last.then_inc(down_ps, 1)

            def ffT_step(b):
                pe.wait_ge(ffT_sb, b + 1)
                if b + 1 < B:
                    pe.wait_ge(attnT_sb, b + 2)
                for j in range(NT):
                    last = tp(bank_r[:, P * j:P * (j + 1)], ffT[:, P * j:P * (j + 1)])
                last.then_inc(ffn_tok, 1)

            def x2T_step(b):
                pe.wait_ge(x2_ready, b + 1)
                for j in range(NT):
                    last = tp(bank_r[:, P * j:P * (j + 1)], x2[:, b, P * j:P * (j + 1)])
                last.then_inc(x2T_ps, 1)

            def gates_step(b):
                pe.wait_ge(x2T_sb, b + 1)
                for j in range(NT):
                    last = mm(bank_r[:, NE * j:NE * (j + 1)], x2T[:, P * j:P * (j + 1)], router_w[:, :], start=True, stop=True)
                last.then_inc(gates_ps, 1)

            def wT_step(b):
                pe.wait_ge(wtok_ready, b + 1)
                for j in range(NT):
                    last = tp(bank_r[0:2 * NE, P * j:P * (j + 1)], w_parts[:, j, :])
                last.then_inc(wT_ps, 1)

            def up_ps_of(c):
                return experts_up[c % (2 if c < EARLY else HC)]

            def up(c):
                (e, b), n = PRODUCTS[c // HC], c % HC
                if c == 0:
                    pe.wait_ge(s_free, fill_index(B - 1, "sc", NPAIR - 1, NF - 1) + 1)
                if n == 0:
                    pe.wait_ge(w_split, e + 1)
                    pe.wait_ge(x2_split, b + 1)
                if e >= NSH and n == 1:
                    r = c // HC - NSH * B
                    if r == 0:
                        pe.wait_ge(wT_sb, B)
                    if r >= 1:
                        pe.wait_ge(bc_sb, r)
                    mm(bank_r[:, :], spread[:, e - NSH:e - NSH + 1].broadcast_to([2 * NE, P]), wT[:, b, :],
                       start=True, stop=True).then_inc(bc_ps, 1)
                if 2 <= c < EARLY + HC:
                    pe.wait_ge(e_gelu, min(c, EARLY + 2) - 1)
                if c >= EARLY + HC:
                    pe.wait_ge(e_gelu, c - HC + 1)
                w = slice(P * n, P * (n + 1))
                three(up_ps_of(c), w_hi[:, e % 2, w], w_lo[:, e % 2, w], t_hi[:, b, :], t_lo[:, b, :],
                      True, True).then_inc(e_up, 1)

            def down_product(c):
                (e, b), n = PRODUCTS[c // HC], c % HC
                q = c // HC
                if n == 0 and q >= 2:
                    pe.wait_ge(settled, q - 1)
                pe.wait_ge(e_split, c + 1)
                w = slice(HID + P * n, HID + P * (n + 1))
                three(down[q % 2], w_hi[:, e % 2, w], w_lo[:, e % 2, w], eg_hi[:, n, :], eg_lo[:, n, :],
                      n == 0, n == HC - 1).then_inc(e_down, 1)

            def chunk(c):
                if c < CHUNKS:
                    up(c)
                if c >= LAG:
                    down_product(c - LAG)

            def final(b):
                pe.wait_ge(settled, NM * B - B + b + 1)
                if b:
                    pe.wait_ge(acc_used, b)
                for j in range(NT):
                    last = tp(bank_d[:, P * j:P * (j + 1)], acc[:, b, P * j:P * (j + 1)])
                last.then_inc(accT_ps, 1)

            def moe():
                for c in range(EARLY, CHUNKS + LAG):
                    chunk(c)
                    for b in range(B - 1):
                        if c == FINAL_AT[b]:
                            final(b)
                final(B - 1)

            iterate({"vectors": vectors, "fold1": fold1, "fold2": fold2, "fold3": fold3, "fold4": fold4, "pack": pack,
                     "taps": taps, "kernel": kernel_dft, "xT": xT_step, "qkv": qkv_step, "yT": yT_step, "proj": proj,
                     "x1T": x1T_step, "scores": scores, "attnT": attnT_step, "film": film_step, "dft": dft, "conv": conv,
                     "hT": hT_step, "up": up_step, "down": down_step, "ffT": ffT_step, "x2T": x2T_step,
                     "gates": gates_step, "wT": wT_step, "chunk": chunk}, first, fill, close, late=True)
            moe()

        @block.scalar
        def _(act):
            f = nc.scalar.activation

            def load(dst, src, s):
                act.dma_start(dst, src).then_inc(s, 16)

            load(vec_rows[ROW_B1:ROW_B1 + HC, :], t["L0_xattn_b1"].rearrange("(c p) -> c p", p=P), ld_vec)
            load(vec_rows[ROW_B1 + HC:ROW_B1 + HC * (1 + NSH), :], t["L0_ffn_sb1"].rearrange("s (c p) -> (s c) p", p=P), ld_vec)
            load(vec_rows[ROW_B1 + HC * (1 + NSH):ROW_B2, :], t["L0_ffn_b1"].rearrange("s (c p) -> (s c) p", p=P), ld_vec)
            load(vec_rows[ROW_B2:ROW_B2 + 1, :], t["L0_xattn_b2"].rearrange("(c p) -> c p", p=P), ld_vec)
            load(vec_rows[ROW_B2 + 1:ROW_B2 + 1 + NSH, :], t["L0_ffn_sb2"], ld_vec)
            load(vec_rows[ROW_B2 + 1 + NSH:ROW_LDT, :], t["L0_ffn_b2"], ld_vec)
            load(vec_rows[ROW_LDT:ROWS, :], t["L0_xattn_log_dt"].rearrange("(c p) -> c p", p=P), ld_vec)
            load(ctxs[:, :], t["ctx_768"].rearrange("b g d -> (b g) d"), ld_cross)
            load(wq[:, :], t["L0_xattn_Wq"], ld_cross)
            load(wk[:, :], t["L0_xattn_Wk"], ld_cross)
            load(wv[:, :], t["L0_xattn_Wv"], ld_cross)
            load(w_film[:, 0:2 * D], t["L0_xattn_W_film_in"], ld_cross)
            load(w_film[:, 2 * D:4 * D], t["L0_xattn_W_film_out"], ld_cross)
            load(gate[:, :], t["L0_xattn_mod_gate"].partition_broadcast(P), ld_cross)
            load(film_bias[:, 0:2 * D], t["L0_xattn_b_film_in"].partition_broadcast(P), ld_cross)
            load(film_bias[:, 2 * D:4 * D], t["L0_xattn_b_film_out"].partition_broadcast(P), ld_cross)
            load(tm_rows8[:, :], t["mask_BxS_bf1"].rearrange("b (j p) -> (b j) p", p=P), ld_cross)
            load(cmask8[:, :], t["mask_BxS2_bf1"].rearrange("b g -> (b g)").partition_broadcast(P), ld_cross)

            def states():
                act.wait_ge(pro_arg, 1)
                f(sm[:, 2, :], sm[:, 0, :], ACT.Tanh, scale=0.5).then_inc(pro_fun, 1)
                act.wait_ge(pro_arg, 2)
                f(sm[:, 3, :], sm[:, 4, :], ACT.Sin, scale=TURN / 2)
                f(sm[:, 5, :], sm[:, 4, :], ACT.Sin, scale=TURN).then_inc(pro_fun, 1)

            def powers(q):
                act.wait_ge(pro_arg, 3 + 3 * q)
                f(pv[:, :, :], pt[:, :, :], ACT.Sin, scale=-SIN_SCALE, bias=offs[:, 2:3]).then_inc(pro_fun, 1)
                act.wait_ge(pro_arg, 4 + 3 * q)
                f(uf[:, :, :], uf[:, :, :], ACT.Sin, scale=-SIN_SCALE, bias=offs[:, 2:3])
                f(ug[:, :, :], ug[:, :, :], ACT.Sin, scale=-SIN_SCALE, bias=offs[:, 3:4]).then_inc(pro_fun, 1)
                act.wait_ge(pro_arg, 5 + 3 * q)
                f(pr[:, :, :], pr[:, :, :], ACT.Exp)
                f(ue[:, :, :], ue[:, :, :], ACT.Exp).then_inc(pro_fun, 1)

            def xT_step(b):
                for n in range(2):
                    k = fill_index(b, "xT", n=n)
                    act.wait_ge(s_full, k + 1)
                    if b >= 2:
                        act.wait_ge(proj_ps, b - 1)
                    f(xT[:, 2 * P * n:2 * P * (n + 1)], ring_s[k % 2][:, 0:2 * P], ACT.Copy).then_inc(s_free, 1)

            def qkv_step(b):
                for n in range(2):
                    k = fill_index(b, "qkv", n=n)
                    act.wait_ge(s_full, k + 1)
                    if b:
                        act.wait_ge(v_ready, b)
                    f(qkv[:, 2 * n:2 * n + 2, :].rearrange("p j c -> p (j c)"), ring_s[k % 2][:, 0:2 * QKV], ACT.Copy).then_inc(s_free, 1)

            def first(b):
                for n in range(6):
                    k = fill_index(b, "qT", n=n)
                    act.wait_ge(s_full, k + 1)
                    dst = qT[:, 2 * n:2 * n + 2, :] if n < 4 else kT[:, 2 * (n - 4):2 * (n - 4) + 2, :]
                    f(dst.rearrange("p a q -> p (a q)"), ring_s[k % 2][:, :].bitcast(BF16), ACT.Copy).then_inc(s_free, 1)

            def fill(b, p, n):
                k = fill_index(b, "sc", p, n)
                if b * NPAIR + p >= 2 and n == 0:
                    act.wait_ge(pv_done, b * NPAIR + p - 1)
                act.wait_ge(s_full, k + 1)
                f(probs[:, p % 2, BASE[n]:BASE[n] + WIDTH[n]], ring_s[k % 2][:, 0:WIDTH[n]], ACT.Tanh,
                  scale=1.0 / (CAP * float(np.sqrt(np.float32(HD))))).then_inc(s_free, 1)

            def close(i, p):
                if i < B:
                    act.wait_ge(s_free, fill_index(i, "sc", p, NF - 1) + 1)
                    f(probs[:, p % 2, :], probs[:, p % 2, :], ACT.Exp, scale=CAP).then_inc(exp_done, 1)

            def x1T_step(b):
                act.wait_ge(x1T_ps, b + 1)
                f(x1T[:, :], bank_r[:, :], ACT.Copy).then_inc(x1T_sb, 1)

            def cross_exp(b):
                act.wait_ge(sc_ready, b + 1)
                f(sc[:, :, :], sc[:, :, :], ACT.Exp).then_inc(sc_exp, 1)

            def attnT_step(b):
                act.wait_ge(attnT_ps, b + 1)
                f(attnT[:, :], bank_r[:, :], ACT.Copy).then_inc(attnT_sb, 1)

            def gelu(b):
                for n in range(HC):
                    act.wait_ge(up_ps, b * HC + n + 1)
                    if b:
                        act.wait_ge(split_done, HC * (b - 1) + n + 1)
                    f(g_raw[:, n, :], text_up[n][:, :], ACT.Gelu, bias=vcols[:, ROW_B1 + n:ROW_B1 + n + 1]).then_inc(gelu_done, 1)

            def ff_out(b):
                act.wait_ge(down_ps, b + 1)
                f(ffT, ring_u[0][:, :], ACT.Identity, bias=vcols[:, ROW_B2:ROW_B2 + 1]).then_inc(ffT_sb, 1)

            def x2T_step(b):
                act.wait_ge(x2T_ps, b + 1)
                f(x2T[:, :], bank_r[:, :], ACT.Copy).then_inc(x2T_sb, 1)

            def gates_exp_step(b):
                act.wait_ge(gates_ready, b + 1)
                f(w_tok[:, :, :], w_tok[:, :, :], ACT.Exp).then_inc(gates_exp, 1)

            def chunk(c):
                if c >= CHUNKS:
                    return
                (e, b), n = PRODUCTS[c // HC], c % HC
                if e >= NSH and n == 2:
                    q = c // HC
                    r = q - NSH * B
                    act.wait_ge(bc_ps, r + 1)
                    if r >= 2:
                        act.wait_ge(settled, q - 1)
                    f(w_bc[:, r % 2, :], bank_r[:, :], ACT.Copy).then_inc(bc_sb, 1)
                act.wait_ge(e_up, c + 1)
                k = ROW_B1 + HC * (1 + e) + n
                if c >= HC:
                    act.wait_ge(e_split, c - HC + 1)
                bank = experts_up[c % (2 if c < EARLY else HC)]
                if n == HC - 1:
                    f(eg_raw[:, n, :], bank[:, :], ACT.Gelu, bias=vcols[:, k:k + 1]).then_inc(e_gelu, 1)
                    return
                f(eg_raw[:, n, :], bank[:, :], ACT.Gelu, bias=vcols[:, k:k + 1])
                if c >= HC:
                    act.wait_ge(e_down, c - HC + 1)
                f(eg_hi[:, n, :], bank[:, :], ACT.Gelu, bias=vcols[:, k:k + 1]).then_inc(e_gelu, 1)

            def moe():
                for c in range(EARLY, CHUNKS):
                    chunk(c)

            iterate({"states": states, "powers": powers, "xT": xT_step, "qkv": qkv_step, "x1T": x1T_step,
                     "cross_exp": cross_exp, "attnT": attnT_step, "gelu": gelu, "ff_out": ff_out, "x2T": x2T_step,
                     "gates_exp": gates_exp_step, "chunk": chunk}, first, fill, close)
            moe()

        @block.gpsimd
        def _(pool):
            g = nc.gpsimd
            count = [0]
            roots = [0]

            def op(ins):
                count[0] += 1
                ins.then_inc(pool_step, 1)

            def then():
                pool.wait_ge(pool_step, count[0])

            g.memset(neg_half[:, :], -0.5)
            op(g.memset(vv[:, :, :, :], 0.0))
            then()
            g.memset(vv[:, :, :, HD:HD + 1], 1.0)
            pool.wait_ge(ld_attn, 16 * 7)
            g.tensor_copy(identb[:, :], ident[:, :]).then_inc(consts_ready, 1)

            def power(_=None):
                roots[0] += 1
                pool.wait_ge(var_ready, roots[0])
                g.tensor_tensor(rstd[:, :], var_eps[:, :], neg_half[:, :], ALU.pow).then_inc(rstd_ready, 1)

            def rope_step(b):
                heads, half = NH + NKV, HD // 2
                r4 = lambda x: x.rearrange("p (j h e) -> p j h e", j=NT, h=heads)
                rp = lambda c, lo: rope[:, :, c:c + 1, lo:lo + half]
                pool.wait_ge(rms_ready, b + 1)
                for j in range(NT):
                    qk = qkv[:, j, 0:QK].rearrange("p (h e) -> p h e", e=HD)
                    op(g.tensor_tensor(qk, qk, rms_out[:, heads * j:heads * (j + 1)].unsqueeze(2).broadcast_to([P, heads, HD]), ALU.mult))
                then()
                x4 = qkv[:, :, 0:QK].rearrange("p j (h e) -> p j h e", h=heads)
                op(g.tensor_tensor(r4(tmp_b), x4, rope[:, :, 0:1, :].broadcast_to([P, NT, heads, HD]), ALU.mult))
                op(g.tensor_tensor(r4(tmp_c)[:, :, :, 0:half], x4[:, :, :, half:HD], rp(1, 0).broadcast_to([P, NT, heads, half]), ALU.mult))
                op(g.tensor_tensor(r4(tmp_c)[:, :, :, half:HD], x4[:, :, :, 0:half], rp(1, half).broadcast_to([P, NT, heads, half]), ALU.mult))
                then()
                g.tensor_tensor(tmp_b, tmp_b, tmp_c, ALU.add).then_inc(roped, 1)

            def close(i, p):
                if i == B:
                    return
                pool.wait_ge(exp_done, i * NPAIR + p + 1)
                pr = probs[:, p % 2, :]
                for v in (pr[:, 0:4 * SEQ].rearrange("p (n w) -> p n w", w=SEQ)[:, :, 0:P],
                          pr[:, 2 * SEQ:4 * SEQ].rearrange("p (n w) -> p n w", w=SEQ)[:, :, 384:SEQ],
                          pr[:, 4 * SEQ:5 * SEQ].rearrange("p (n w) -> p n w", w=256)[:, :, 0:P]):
                    last = g.affine_select(out=v, in_=v, compare_op=ALU.is_ge, fill=0.0, base=0,
                                           pattern=[[0, v.shape[1]], [1, P]], channel_multiplier=-1)
                last.then_inc(masked, 1)

            def affine(x, n, after=None):
                op(g.tensor_tensor(x[:, :, :], x[:, :, :], norms[:, n:n + 1, :].broadcast_to([P, NT, D]), ALU.mult))
                then()
                return g.tensor_tensor(x[:, :, :], x[:, :, :], norms[:, n + 1:n + 2, :].broadcast_to([P, NT, D]), ALU.add)

            def x_norm(b):
                power()
                if b == 0:
                    pool.wait_ge(ld_rest, 16 * 9)
                pool.wait_ge(xn_scaled, b + 1)
                affine(xn, 0).then_inc(xn_ready, 1)

            def shape_out(b):
                power()
                pool.wait_ge(h_scaled, b + 1)
                affine(fa, 2).then_inc(h_ready, 1)

            def ff_norm(b):
                power()
                pool.wait_ge(ff_scaled, b + 1)
                op(affine(fa, 4))
                then()
                g.tensor_tensor(fa[:, :, :], fa[:, :, :], x1[:, b % 2, :, :], ALU.add).then_inc(sum_ready, 1)

            def nothing(*_):
                pass

            iterate({"rope": rope_step, "proj": power, "x_norm": x_norm, "shape_out": shape_out, "ff_norm": ff_norm,
                     "x2": power}, nothing, nothing, close)
            for b in range(B):
                power()

        @block.vector
        def _(dve):
            v = nc.vector
            count = [0]
            roots = [0]

            def op(ins):
                count[0] += 1
                ins.then_inc(dve_step, 1)

            def then():
                dve.wait_ge(dve_step, count[0])

            def one(ins):
                op(ins)
                then()

            def s(k):
                return sm[:, k, :]

            tt, ts, stt = v.tensor_tensor, v.tensor_scalar, v.scalar_tensor_tensor

            def fl(x):
                return x[:, :, :].rearrange("p d m -> p (d m)")

            def vectors():
                dve.wait_ge(ld_cross, 16 * 11)
                v.tensor_copy(tm_rows[:, :], tm_rows8[:, :]).then_inc(pro_sb, 1)
                op(v.tensor_copy(cmask[:, :], cmask8[:, :]))
                op(ts(gate4[:, :], gate[:, :], 0.25, None, ALU.mult))
                one(ts(film_bias[:, :], film_bias[:, :], gate[:, 0:1], None, ALU.mult))
                op(ts(cmask[:, :], cmask[:, :], 1.0, 3e38, ALU.subtract, ALU.mult))
                for n in range(2):
                    op(ts(film_bias[:, 2 * D * n:2 * D * n + D], film_bias[:, 2 * D * n:2 * D * n + D], 1.0, None, ALU.add))
                then()
                for h in range(XH):
                    op(ts(ctx_bias[:, :, h, :], cmask[:, :].rearrange("p (b g) -> p b g", b=B), 10.0, None, ALU.mult))
                op(tt(spread[:, :], ident[0:2 * NE, 0:NE], ident[0:2 * NE, NE:2 * NE], ALU.add))
                dve.wait_ge(pro_pe, 1)
                one(v.tensor_copy(vcols[:, :], bank_d[:, 0:ROWS]))
                one(tt(b2_shared[:, :], vcols[:, ROW_B2 + 1:ROW_B2 + 2], vcols[:, ROW_B2 + 2:ROW_B2 + 3], ALU.add))
                op(ts(b2_shared[:, :], b2_shared[:, :], 0.5, None, ALU.mult))
                one(v.memset(kbd[:, :], 0.0))

            def fold1():
                dve.wait_ge(pro_pe, 2)
                op(v.tensor_copy(wqT[:, :], bank_r[:, 0:P]))
                op(v.tensor_copy(tmask[:, :], bank_r[:, 3 * P:3 * P + B * NT]))
                one(v.tensor_copy(ctxT[:, :], bank_r[0:DV, P:2 * P]))
                v.tensor_copy(wvT[:, :], bank_r[:, 2 * P:2 * P + DV]).then_inc(pro_sb, 1)
                for h in range(XH):
                    op(v.tensor_copy(ctx_rep.rearrange("p b (h g) -> p b h g", h=XH)[:, :, h, :],
                                     ctxT[:, :].rearrange("p (b g) -> p b g", b=B)))

            def fold2():
                dve.wait_ge(pro_pe, 3)
                for h in range(XH):
                    last = v.tensor_copy(kbd[:, :].rearrange("p (b h g) -> p b h g", b=B, h=XH)[32 * h:32 * h + 32, :, h, :],
                                         ring_u[0][32 * h:32 * h + 32, 0:B * G].rearrange("p (b g) -> p b g", b=B))
                last.then_inc(pro_sb, 1)
                then()
                dve.wait_ge(pro_pe, 4)
                v.tensor_copy(wvf, ring_u[1][0:DV, :]).then_inc(pro_sb, 1)

            def fold3():
                dve.wait_ge(pro_pe, 5)
                v.tensor_copy(xq[:, :, :].rearrange("p b g -> p (b g)"), bank_d[:, :]).then_inc(pro_sb, 1)

            def fold4():
                for b in range(B):
                    dve.wait_ge(pro_pe, 6 + b)
                    op(ts(vf[:, b, :], (bank_r, ring_u[0], ring_u[1], bank_d)[b][:, :], gate4[:, 0:1], None, ALU.mult))

            def states():
                ldt = vcols[:, ROW_LDT:ROW_LDT + 1]
                c = lambda k: dtc[:, k:k + 1]
                dve.wait_ge(ld_s4, 16 * 7)
                one(ts(c(0), ldt, 1.4426950408889634, MAGIC, ALU.mult, ALU.add))
                one(ts(c(0), c(0), MAGIC, None, ALU.subtract))
                op(ts(c(4), c(0), 127.0, None, ALU.add))
                one(stt(out=c(1), in0=c(0), scalar=-LN2_HI, in1=ldt, op0=ALU.mult, op1=ALU.add))
                op(v.tensor_copy(dti[:, 0:1], c(4)))
                one(stt(out=c(2), in0=c(0), scalar=-LN2_LO, in1=c(1), op0=ALU.mult, op1=ALU.add))
                one(ts(dti[:, 1:2], dti[:, 0:1], 23, None, ALU.logical_shift_left))
                one(ts(c(3), c(2), 1.0 / 5040, 1.0 / 720, ALU.mult, ALU.add))
                for k in (1.0 / 120, 1.0 / 24, 1.0 / 6, 0.5, 1.0, 1.0):
                    one(ts(c(3), c(3), c(2), k, ALU.mult, ALU.add))
                one(tt(c(5), c(3), dti[:, 1:2].bitcast(F32), ALU.mult))
                op(ts(s(0), s4[:, 0, :], c(5), None, ALU.mult))
                one(ts(s(1), s4[:, 1, :], c(5), 1.0 / TWO_PI, ALU.mult, ALU.mult))
                one(ts(s(4), s(1), MAGIC, MAGIC, ALU.add, ALU.subtract))
                v.tensor_copy(packs[:, 0, 0:NS], s(0)).then_inc(pro_arg, 1)
                tt(s(4), s(1), s(4), ALU.subtract).then_inc(pro_arg, 1)
                dve.wait_ge(pro_arg, 2)
                op(v.tensor_copy(packs[:, 0, NS:P], s(0)))
                op(v.tensor_copy(packs[:, 1, 0:NS], s(4)))
                op(v.tensor_copy(packs[:, 1, NS:P], s(4)))
                op(tt(s(9), s4[:, 0, :], s4[:, 0, :], ALU.mult))
                op(tt(s(10), s4[:, 1, :], s4[:, 1, :], ALU.mult))
                dve.wait_ge(pro_fun, 1)
                one(ts(s(6), s(2), -1.0, 1.0, ALU.mult, ALU.add))
                op(tt(s(9), s(9), s(10), ALU.add))
                one(v.reciprocal(s(6), s(6)))
                op(v.reciprocal(s(9), s(9)))
                one(tt(s(6), s(6), s(2), ALU.mult))
                one(ts(s(6), s(6), 2.0, None, ALU.mult))
                dve.wait_ge(pro_fun, 2)
                one(tt(s(3), s(3), s(3), ALU.mult))
                one(ts(s(3), s(3), -2.0, None, ALU.mult))
                op(ts(s(7), s(3), 1.0, None, ALU.add))
                one(ts(s(8), s(6), 1.0, None, ALU.add))
                op(tt(s(7), s(7), s(6), ALU.mult))
                one(tt(s(8), s(8), s(5), ALU.mult))
                one(tt(s(7), s(7), s(3), ALU.add))
                op(tt(s(0), s4[:, 2, :], s(7), ALU.mult))
                op(tt(s(1), s4[:, 3, :], s(8), ALU.mult))
                op(tt(s(2), s4[:, 2, :], s(8), ALU.mult))
                one(tt(s(3), s4[:, 3, :], s(7), ALU.mult))
                op(tt(s(0), s(0), s(1), ALU.subtract))
                one(tt(s(2), s(2), s(3), ALU.add))
                op(tt(s(5), s(0), s4[:, 0, :], ALU.mult))
                op(tt(s(6), s(2), s4[:, 1, :], ALU.mult))
                op(tt(s(7), s(2), s4[:, 0, :], ALU.mult))
                one(tt(s(8), s(0), s4[:, 1, :], ALU.mult))
                op(tt(s(5), s(5), s(6), ALU.add))
                one(tt(s(7), s(8), s(7), ALU.subtract))
                op(tt(packs[:, 2, 0:NS], s(5), s(9), ALU.mult))
                one(tt(packs[:, 3, 0:NS], s(7), s(9), ALU.mult))
                op(ts(packs[:, 2, NS:P], packs[:, 2, 0:NS], -1.0, None, ALU.mult))
                v.tensor_copy(packs[:, 3, NS:P], packs[:, 3, 0:NS]).then_inc(pro_sb, 1)

            def pack():
                dve.wait_ge(pro_pe, 10)
                one(v.tensor_copy(pk[:, :, :].rearrange("p n d -> p (n d)"), ring_u[0][:, :]))
                op(ts(pk32[:, 0, :], pk[:, 0, :], float(JM), None, ALU.mult))
                one(ts(pk32[:, 1, :], pk[:, 1, :], float(JM), None, ALU.mult))
                one(ts(pk32[:, 2, :], pk32[:, 1, :], MAGIC, MAGIC, ALU.add, ALU.subtract))
                one(tt(pk32[:, 1, :], pk32[:, 1, :], pk32[:, 2, :], ALU.subtract))

            def bc(x, q, m):
                return x[:, JM * q:JM * (q + 1)].unsqueeze(2).broadcast_to([P, JM, m])

            def ix(m):
                return index[:, 0:m].unsqueeze(1).broadcast_to([P, JM, m])

            def evacuate(q, h):
                d0 = JM * q + 16 * h
                return ts(kij[:, :, d0:d0 + 16].rearrange("i j d -> i d j"),
                          taps_ps[h][0:IM, :].rearrange("i (d j) -> i d j", j=JM), 2.0, None, ALU.mult)

            def args(q):
                if q:
                    dve.wait_ge(pro_pe, 10 + q)
                    op(evacuate(q - 1, 0))
                    last = evacuate(q - 1, 1)
                    if q == D // JM:
                        last.then_inc(kij_ready, 1)
                        return
                    op(last)
                one(tt(pr[:, :, :], bc(pk[:, 1, :], q, JM), ix(JM), ALU.mult))
                one(ts(fl(pt), fl(pr), offs[:, 0:1], MAGIC, ALU.add, ALU.add))
                stt(out=fl(pt), in0=fl(pt), scalar=MAGIC, in1=fl(pr), op0=ALU.subtract, op1=ALU.subtract).then_inc(pro_arg, 1)
                one(tt(ue[:, :, :], bc(pk32[:, 1, :], q, IM), ix(IM), ALU.mult))
                op(ts(fl(uf), fl(ue), offs[:, 0:1], MAGIC, ALU.add, ALU.add))
                one(ts(fl(ug), fl(ue), offs[:, 1:2], MAGIC, ALU.add, ALU.add))
                op(stt(out=fl(uf), in0=fl(uf), scalar=MAGIC, in1=fl(ue), op0=ALU.subtract, op1=ALU.subtract))
                stt(out=fl(ug), in0=fl(ug), scalar=MAGIC, in1=fl(ue), op0=ALU.subtract, op1=ALU.subtract).then_inc(pro_arg, 1)
                dve.wait_ge(pro_arg, 4 + 3 * q)
                op(tt(pr[:, :, :], bc(pk[:, 0, :], q, JM), ix(JM), ALU.mult))
                tt(ue[:, :, :], bc(pk32[:, 0, :], q, IM), ix(IM), ALU.mult).then_inc(pro_arg, 1)

            def powers(q):
                dve.wait_ge(pro_fun, 4 + 3 * q)
                op(tt(uf[:, :, :], uf[:, :, :], bc(pk[:, 2, :], q, IM), ALU.mult))
                one(tt(ug[:, :, :], ug[:, :, :], bc(pk[:, 3, :], q, IM), ALU.mult))
                one(tt(fl(uf), fl(uf), fl(ug), ALU.add))
                dve.wait_ge(pro_fun, 5 + 3 * q)
                op(tt(fl(pv), fl(pv), fl(pr), ALU.mult))
                tt(fl(uf), fl(uf), fl(ue), ALU.mult).then_inc(pro_sb, 1)

            def first_tap():
                dve.wait_ge(kld_landed, 16)
                tt(kld[0:1, 0, :], kld[0:1, 0, :], dskip[:, :], ALU.add).then_inc(kconst_ready, 1)

            def spectra():
                dve.wait_ge(pro_pe, 15)
                op(ts(fl(kc), ring_u[0][:, :], 2.0 / (2 * SEQ), None, ALU.mult))
                op(ts(fl(ks), ring_u[1][:, :], 2.0 / (2 * SEQ), None, ALU.mult))
                one(ts(fl(kcn), ring_u[0][:, :], 2.0 / (2 * SEQ), None, ALU.mult))
                op(ts(kc[0:1, 0, :], kc[0:1, 0, :], 0.5, None, ALU.mult))
                one(ts(kcn[0:1, 0, :], ks[0:1, 0, :], 0.5, None, ALU.mult))
                one(v.memset(ks[0:1, 0, :], 0.0))

            def text_weights():
                dve.wait_ge(ld_wt, 32)
                halves(wt_hi[:, :], wt_lo[:, :], wt_raw).then_inc(wt_split, 1)

            def norm(src, dst):
                for j in range(NT):
                    op(v.bn_stats(stats[:, j, :], src[:, j, :]))
                then()
                for j in range(NT):
                    op(v.bn_aggr(mean_var[:, j, :], stats[:, j, :]))
                then()
                ts(var_eps[:, :], mean_var[:, :, 1], EPS, None, ALU.add).then_inc(var_ready, 1)
                roots[0] += 1
                dve.wait_ge(rstd_ready, roots[0])
                for j in range(NT):
                    last = ts(dst[:, j, :], src[:, j, :], mean_var[:, j, 0:1], rstd[:, j:j + 1], ALU.subtract, ALU.mult)
                    if j < NT - 1:
                        op(last)
                return last

            def halves(hi, lo, src):
                one(v.tensor_copy(hi, src))
                return tt(lo, src, hi.bitcast(F32), ALU.subtract)

            def rms(b):
                dve.wait_ge(s_free, fill_index(b, "qkv", n=1) + 1)
                qk = qkv[:, :, 0:QK]
                one(tt(tmp_b.rearrange("p (j c) -> p j c", j=NT), qk, qk, ALU.mult))
                one(v.tensor_reduce(rms_in[:, :], tmp_b.rearrange("p (n e) -> p n e", e=HD), AX, ALU.add))
                one(ts(rms_in[:, :], rms_in[:, :], 1.0 / HD, EPS, ALU.mult, ALU.add))
                one(ts(rms_bits, rms_in[:, :].bitcast(I32), 1, None, ALU.logical_shift_right))
                op(ts(rms_in[:, :], rms_in[:, :], -0.5, None, ALU.mult))
                one(v.tensor_copy(rms_tmp[:, :], rms_bits))
                one(ts(rms_tmp[:, :], rms_tmp[:, :], -1.0, float(0x5F3759DF), ALU.mult, ALU.add))
                one(v.tensor_copy(rms_bits, rms_tmp[:, :]))
                y = rms_out[:, :]
                for k in range(4):
                    one(tt(rms_tmp[:, :], y, y, ALU.mult))
                    one(tt(rms_tmp[:, :], rms_tmp[:, :], rms_in[:, :], ALU.mult))
                    last = stt(out=rms_out[:, :], in0=rms_tmp[:, :], scalar=1.5, in1=y, op0=ALU.add, op1=ALU.mult)
                    if k < 3:
                        one(last)
                last.then_inc(rms_ready, 1)

            def parts_step(b):
                heads = NH + NKV
                r4 = lambda x: x.rearrange("p (j h e) -> p j h e", j=NT, h=heads)
                dve.wait_ge(roped, b + 1)
                if b:
                    dve.wait_ge(s_full, fill_index(b - 1, "qT", n=5) + 1)
                q4 = r4(tmp_b)[:, :, 0:NH, :]
                k4 = r4(tmp_b)[:, :, NH:heads, :]
                qp = lambda c: qs[:, :, c, :].rearrange("p (j h) e -> p j h e", j=NT)
                kp = lambda c: k_parts[:, :, 0, c, :].rearrange("p (j h) e -> p j h e", j=NT)
                op(v.tensor_copy(qp(0), q4))
                one(v.tensor_copy(kp(0), k4))
                op(tt(q4, q4, qp(0), ALU.subtract))
                one(tt(k4, k4, kp(0), ALU.subtract))
                op(v.tensor_copy(qp(3), q4))
                one(v.tensor_copy(kp(1), k4))
                op(tt(qp(6), q4, qp(3), ALU.subtract))
                one(tt(kp(2), k4, kp(1), ALU.subtract))
                for src, dsts in ((0, (1, 2)), (3, (4, 5)), (6, (7,))):
                    op(v.tensor_copy(qs[:, :, dsts[0]:dsts[-1] + 1, :],
                                     qs[:, :, src:src + 1, :].broadcast_to([P, NT * NH, len(dsts), HD])))
                for src, dsts in ((0, (3, 6)), (1, (4, 7)), (2, (5,))):
                    for d in dsts:
                        op(v.tensor_copy(k_parts[:, :, 0, d, :], k_parts[:, :, 0, src, :]))
                then()
                v.tensor_copy(k_parts[:, :, 1, :, :].rearrange("p n c e -> p n (c e)"),
                              k_parts[:, :, 0, :, :].rearrange("p n c e -> p n (c e)")).then_inc(parts_ready, 1)

            def close(i, p):
                pair = i * NPAIR + p - 1
                if 0 <= pair < B * NPAIR:
                    dve.wait_ge(pv_done, pair + 1)
                    if pair >= 2:
                        dve.wait_ge(y_ps, pair - 1)
                    op(v.tensor_copy(oT[0:64, pair % 2, :], bank_o[0:64, :]))
                    v.tensor_copy(oT[64:P, pair % 2, P:SEQ], bank_o[64:P, P:SEQ]).then_inc(oT_ready, 1)
                if p == 0 and i < B:
                    dve.wait_ge(consts_ready, 1)
                    v.tensor_copy(vv[:, :, :, 0:HD], qkv[:, :, QK:QKV].rearrange("p j (g e) -> p j g e", g=NKV)).then_inc(v_ready, 1)
                if 0 <= pair - 1 < B * NPAIR:
                    pair -= 1
                    q = pair % NPAIR
                    dve.wait_ge(y_ps, pair + 1)
                    ys = bank_m[:, 256 * (q % 2):256 * (q % 2 + 1)].rearrange("p (j h e) -> p j h e", j=NT, h=2)
                    one(v.reciprocal(ry[:, :, :], ys[:, :, :, HD]))
                    tt(y_att[:, :, 2 * HD * q:2 * HD * (q + 1)].rearrange("p j (h e) -> p j h e", h=2), ys[:, :, :, 0:HD],
                       ry[:, :, :].unsqueeze(3).broadcast_to([P, NT, 2, HD]), ALU.mult).then_inc(y_ready, 1)

            def yT_step(b):
                dve.wait_ge(yT_ps, b + 1)
                v.tensor_copy(yT[:, :], bank_m[:, :]).then_inc(yT_sb, 1)

            def proj(b):
                dve.wait_ge(proj_ps, b + 1)
                tt(fl(y_att), bank_o[:, :], x_in[:, b % 2, :, :].rearrange("p j d -> p (j d)"), ALU.add).then_inc(x_used, 1)
                dve.wait_ge(x_used, b + 1)
                norm(y_att, x1[:, b % 2, :, :]).then_inc(x1_ready, 1)

            def scores(b):
                dve.wait_ge(sc_ps, b + 1)
                d4 = bank_d[:, :].rearrange("p (j c) -> p j c", j=NT)
                s4v = fl(sc).rearrange("p (j c) -> p j c", j=NT)
                one(stt(out=s4v, in0=d4, scalar=1.0 / float(np.sqrt(np.float32(XD))),
                        in1=ctx_bias[:, b:b + 1].rearrange("p b h g -> p b (h g)").broadcast_to([P, NT, XH * G]),
                        op0=ALU.mult, op1=ALU.add))
                one(v.tensor_reduce(sc_max[:, :], sc[:, :, :], AX, ALU.max))
                tt(sc[:, :, :], sc[:, :, :], sc_max[:, :].unsqueeze(2).broadcast_to([P, NT * XH, G]), ALU.subtract).then_inc(sc_ready, 1)

            def x_norm(b):
                dve.wait_ge(x1_ready, b + 1)
                norm(x1[:, b % 2, :, :], xn).then_inc(xn_scaled, 1)

            def soften(b):
                dve.wait_ge(sc_exp, b + 1)
                one(v.tensor_reduce(sc_sum[:, :], sc[:, :, :], AX, ALU.add))
                one(v.reciprocal(sc_sum[:, :], sc_sum[:, :]))
                one(tt(sc_sum[:, :].rearrange("p (j h) -> p j h", j=NT), sc_sum[:, :].rearrange("p (j h) -> p j h", j=NT),
                       tmask[:, NT * b:NT * (b + 1)].unsqueeze(2).broadcast_to([P, NT, XH]), ALU.mult))
                tt(sc[:, :, :], sc[:, :, :], sc_sum[:, :].unsqueeze(2).broadcast_to([P, NT * XH, G]), ALU.mult).then_inc(attn_ready, 1)

            def film_step(b, j):
                dve.wait_ge(u_full, b * U_FILLS + U_FILM + j + 1)
                tt(film[:, j, :], ring_u[j % 2][:, :], film_bias[:, :], ALU.add).then_inc(u_free, 1)

            def modulate(b):
                dve.wait_ge(u_free, b * U_FILLS + NT)
                dve.wait_ge(xn_ready, b + 1)
                one(tt(xn[:, :, :], xn[:, :, :], film[:, :, 0:D], ALU.mult))
                tt(xn[:, :, :], xn[:, :, :], film[:, :, D:2 * D], ALU.add).then_inc(xmod_ready, 1)

            def spectrum(b):
                dve.wait_ge(u_full, b * U_FILLS + U_DFT + 2)
                if b:
                    dve.wait_ge(x2_ready, b)
                re, im = ring_u[0][:, :], ring_u[1][:, :]
                lo = spec[:, 0:NT, :].rearrange("p n d -> p (n d)")
                hi = spec[:, NT:2 * NT, :].rearrange("p n d -> p (n d)")
                op(tt(lo, re, fl(kc), ALU.mult))
                op(tt(fl(fa), im, fl(ks), ALU.mult))
                tt(hi, re, fl(ks), ALU.mult).then_inc(u_free, 1)
                tt(fl(fb), im, fl(kcn), ALU.mult).then_inc(u_free, 1)
                then()
                dve.wait_ge(u_free, U_FILLS * (b + 1))
                one(tt(lo, lo, fl(fa), ALU.subtract))
                tt(hi, hi, fl(fb), ALU.add).then_inc(spec_ready, 1)

            def shape_out(b):
                dve.wait_ge(conv_ps, b + 1)
                one(tt(fa[:, :, :], bank_d[:, :].rearrange("p (j d) -> p j d", j=NT), film[:, :, 2 * D:3 * D], ALU.mult))
                one(tt(fa[:, :, :], fa[:, :, :], film[:, :, 3 * D:4 * D], ALU.add))
                one(tt(xt[:, :, :], fa[:, :, :], x1[:, b % 2, :, :], ALU.add))
                norm(xt, fa).then_inc(h_scaled, 1)

            def hT_step(b):
                dve.wait_ge(hT_ps, b + 1)
                halves(t_hi[:, b, :], t_lo[:, b, :], bank_r[:, :]).then_inc(hT_sb, 1)

            def split_hidden(b):
                for n in range(HC):
                    dve.wait_ge(gelu_done, b * HC + n + 1)
                    halves(g_hi[:, n, :], g_lo[:, n, :], g_raw[:, n, :]).then_inc(split_done, 1)

            def ffT_step(b):
                dve.wait_ge(ffn_tok, b + 1)
                tt(fl(xt), bank_r[:, :], fl(xt), ALU.add).then_inc(tok_used, 1)

            def ff_norm(b):
                dve.wait_ge(tok_used, b + 1)
                norm(xt, fa).then_inc(ff_scaled, 1)

            def x2_step(b):
                dve.wait_ge(sum_ready, b + 1)
                norm(fa, x2[:, b, :].rearrange("p (j d) -> p j d", j=NT)).then_inc(x2_ready, 1)

            def gates_step(b):
                dve.wait_ge(x2T_sb, b + 1)
                halves(t_hi[:, b, :], t_lo[:, b, :], x2T[:, :]).then_inc(x2_split, 1)
                dve.wait_ge(gates_ps, b + 1)
                one(tt(gates[:, :, :], bank_r[:, 0:NT * NE].rearrange("p (j e) -> p j e", j=NT),
                       router_b[:, :].unsqueeze(1).broadcast_to([P, NT, NE]), ALU.add))
                one(v.tensor_reduce(gmax[:, :], gates[:, :, :], AX, ALU.max))
                tt(w_tok[:, :, :], gates[:, :, :], gmax[:, :].unsqueeze(2).broadcast_to([P, NT, NE]), ALU.subtract).then_inc(gates_ready, 1)

            def route(b):
                other = gates[:, :, :].unsqueeze(2).broadcast_to([P, NT, NE, NE])
                own = gates[:, :, :].unsqueeze(3).broadcast_to([P, NT, NE, NE])
                op(tt(cmp_a[:, :, :, :], other, own, ALU.is_gt))
                one(tt(cmp_b[:, :, :, :], other, own, ALU.is_equal))
                one(tt(cmp_b[:, :, :, :], cmp_b[:, :, :, :], earlier[:, :, :].unsqueeze(1).broadcast_to([P, NT, NE, NE]), ALU.mult))
                one(tt(cmp_a[:, :, :, :], cmp_a[:, :, :, :], cmp_b[:, :, :, :], ALU.add))
                one(v.tensor_reduce(chosen[:, :, :], cmp_a[:, :, :, :], AX, ALU.add))
                one(ts(chosen[:, :, :], chosen[:, :, :], 2.0, None, ALU.is_lt))
                dve.wait_ge(gates_exp, b + 1)
                one(tt(w_tok[:, :, :], w_tok[:, :, :], chosen[:, :, :], ALU.mult))
                one(v.tensor_reduce(gmax[:, :], w_tok[:, :, :], AX, ALU.add))
                one(v.reciprocal(gmax[:, :], gmax[:, :]))
                one(tt(w_tok[:, :, :], w_tok[:, :, :], gmax[:, :].unsqueeze(2).broadcast_to([P, NT, NE]), ALU.mult))
                one(v.tensor_copy(w_round[:, :, :], w_tok[:, :, :]))
                op(v.tensor_copy(w_parts[:, :, 0:NE], w_round[:, :, :].bitcast(F32)))
                tt(w_parts[:, :, NE:2 * NE], w_tok[:, :, :], w_round[:, :, :].bitcast(F32), ALU.subtract).then_inc(wtok_ready, 1)

            def wT_step(b):
                dve.wait_ge(wT_ps, b + 1)
                v.tensor_copy(wT[:, b, :], bank_r[0:2 * NE, :]).then_inc(wT_sb, 1)

            def settle(q):
                e, b = PRODUCTS[q]
                dve.wait_ge(e_down, HC * (q + 1))
                if q >= 1:
                    dve.wait_ge(settled, q)
                bank = down[q % 2][:, :]
                if e == 0:
                    ts(acc[:, b, :], bank, 1.0 / NSH, b2_shared[:, 0:1], ALU.mult, ALU.add).then_inc(settled, 1)
                elif e < NSH:
                    stt(out=acc[:, b, :], in0=bank, scalar=1.0 / NSH, in1=acc[:, b, :], op0=ALU.mult, op1=ALU.add).then_inc(settled, 1)
                else:
                    r, k = q - NSH * B, ROW_B2 + 1 + e
                    dve.wait_ge(bc_sb, r + 1)
                    one(stt(out=term[:, :], in0=bank, scalar=vcols[:, k:k + 1], in1=w_bc[:, r % 2, :], op0=ALU.add, op1=ALU.mult))
                    tt(acc[:, b, :], acc[:, b, :], term[:, :], ALU.add).then_inc(settled, 1)

            def split_weights(e):
                dve.wait_ge(ld_w[e % 2], 32 * (e // 2 + 1))
                halves(w_hi[:, e % 2, :], w_lo[:, e % 2, :], e_raw[:, e % 2, :]).then_inc(w_split, 1)

            def chunk(c):
                if c >= CHUNKS:
                    return
                (e, b), n = PRODUCTS[c // HC], c % HC
                q = c // HC
                if c == 0:
                    for k in range(NSH):
                        split_weights(k)
                dve.wait_ge(e_gelu, c + 1)
                if c >= HC:
                    dve.wait_ge(e_down, c - HC + 1)
                if n == HC - 1:
                    one(v.tensor_copy(eg_hi[:, n, :], eg_raw[:, n, :]))
                tt(eg_lo[:, n, :], eg_raw[:, n, :], eg_hi[:, n, :].bitcast(F32), ALU.subtract).then_inc(e_split, 1)
                if n == LAG and q:
                    settle(q - 1)
                if n == HC - 1 and (e, b) == (NSH - 1, B - 1):
                    split_weights(NSH)
                elif n == HC - 1 and b == 0 and e >= NSH and e + 1 < NM:
                    split_weights(e + 1)

            def final(b):
                dve.wait_ge(accT_ps, b + 1)
                tt(fl(fa), bank_d[:, :], x2[:, b, :], ALU.add).then_inc(acc_used, 1)
                dve.wait_ge(acc_used, b + 1)
                norm(fa, x2[:, b, :].rearrange("p (j d) -> p j d", j=NT)).then_inc(y_out_ready, 1)

            def moe():
                for c in range(EARLY, CHUNKS + 1):
                    chunk(c)
                    for b in range(B - 1):
                        if c == FINAL_AT[b]:
                            final(b)
                settle(NM * B - 1)
                final(B - 1)

            def nothing(*_):
                pass

            op(v.memset(oT[64:P, :, 0:P], 0.0))
            iterate({"vectors": vectors, "fold1": fold1, "fold2": fold2, "fold3": fold3, "fold4": fold4,
                     "states": states, "pack": pack, "args": args, "powers": powers, "first_tap": first_tap,
                     "spectra": spectra, "text_weights": text_weights, "rms": rms, "parts": parts_step, "yT": yT_step,
                     "proj": proj, "scores": scores, "x_norm": x_norm, "soften": soften, "film": film_step,
                     "modulate": modulate, "spectrum": spectrum, "shape_out": shape_out, "hT": hT_step,
                     "gelu": split_hidden, "ffT": ffT_step, "ff_norm": ff_norm, "x2": x2_step, "gates": gates_step,
                     "route": route, "wT": wT_step, "chunk": chunk}, nothing, nothing, close, late=True)
            moe()


_INS = ["x", "ctx_768", "mask_BxS_bf1", "mask_BxS2_bf1", "L0_attn_w_q", "L0_attn_w_k", "L0_attn_w_v", "L0_attn_w_o",
        "L0_xattn_Wq", "L0_xattn_Wk", "L0_xattn_Wv", "L0_xattn_W_film_in", "L0_xattn_b_film_in", "L0_xattn_W_film_out",
        "L0_xattn_b_film_out", "L0_xattn_g_norm_in", "L0_xattn_b_norm_in", "L0_xattn_g_norm_out",
        "L0_xattn_b_norm_out", "L0_xattn_g_ffn", "L0_xattn_b_ffn", "L0_xattn_W1", "L0_xattn_b1", "L0_xattn_W2",
        "L0_xattn_b2", "L0_xattn_log_dt", "L0_xattn_A_re", "L0_xattn_A_im", "L0_xattn_C_re", "L0_xattn_C_im",
        "L0_xattn_D_skip", "L0_xattn_mod_gate", "L0_ffn_rW", "L0_ffn_rb", "L0_ffn_W1", "L0_ffn_b1", "L0_ffn_W2",
        "L0_ffn_b2", "L0_ffn_sW1", "L0_ffn_sb1", "L0_ffn_sW2", "L0_ffn_sb2"]


def constants():
    n = np.arange(SEQ)
    turn = 2 * np.pi * np.outer(n, n) / (2 * SEQ)
    alternate = (-1.0) ** n
    sin_fwd, sin_inv = np.sin(turn), np.sin(turn)
    sin_fwd[:, 0] = alternate
    sin_inv[0, :] = alternate
    freq = 1.0 / 10000.0 ** (np.arange(0, HD, 2, dtype=np.float32) / np.float32(HD))
    angle = (n.astype(np.float32)[:, None] * freq.astype(np.float32)[None, :]).astype(np.float64)
    c, s = np.cos(angle), np.sin(angle)
    rope = np.stack([np.concatenate([c, c], 1), np.concatenate([-s, s], 1)], 1)
    rope = rope.reshape(NT, P, 2, HD).transpose(1, 0, 2, 3).reshape(P, -1)
    offs = np.zeros((P, 4))
    offs[:NS, 0], offs[NS:, 1] = 0.25, 0.25
    offs[:, 2:4] = offs[:, 0:2] * SIN_SCALE
    pair_sum = np.tile(np.eye(64), (2, 1))
    earlier = (np.arange(NE)[None, :] < np.arange(NE)[:, None]).astype(np.float32).reshape(-1)
    tables = dict(c_cos=np.cos(turn), c_sin_fwd=sin_fwd, c_sin_inv=sin_inv, c_rope=rope, c_offs=offs,
                  c_pair_sum=pair_sum, c_earlier=earlier, c_ident=np.eye(P), c_index=np.arange(JM))
    return {k: np.ascontiguousarray(v, dtype=np.float32) for k, v in tables.items()}


def kernel(**inputs):
    import numpy as _np
    import concourse.bacc as _bacc
    from concourse import mybir as _mybir
    from concourse.bass_utils import run_bass_kernel_spmd as _run

    nc = _bacc.Bacc("TRN2", target_bir_lowering=False, num_devices=1)
    arrays, args = {}, {}
    for name in _INS:
        a = _np.ascontiguousarray(inputs[name])
        if a.ndim == 0:
            a = a.reshape(1)
        arrays[f"in_{name}"] = a
    for name, a in constants().items():
        arrays[f"in_{name}"] = a
    for name, a in arrays.items():
        args[name[3:]] = nc.dram_tensor(name, a.shape, _mybir.dt.from_np(a.dtype), kind="ExternalInput").ap()
    out = nc.dram_tensor("out_0", (B, SEQ, D), F32, kind="ExternalOutput").ap()
    build(nc, args, out)
    r = _run(nc, [arrays], core_ids=[0])
    return r.results[0]["out_0"]
```

```python
from contextlib import ExitStack

import numpy as np
import concourse.bass as bass
from concourse import mybir

F32 = mybir.dt.float32
F32R = mybir.dt.float32r
BF16 = mybir.dt.bfloat16
I32 = mybir.dt.int32
U8 = mybir.dt.uint8
ALU = mybir.AluOpType
ACT = mybir.ActivationFunctionType
AX = mybir.AxisListType.X

P = 128
B, SEQ, D = 4, 512, 128
NT = SEQ // P
NH, NKV, HD = 16, 4, 8
QK = (NH + NKV) * HD
QKV = QK + NKV * HD
LAG = 3
CAP, EPS = 50.0, 1e-5
PARTS = 8
G, DV, XH, XD = 32, 96, 4, 32
NS = 64
HID = 512
HC = HID // P
NE, NSH = 8, 2
NM = NSH + NE
NX = 1 + NM
NPAIR = NH // 2
PW = 5 * SEQ
JM, IM = 32, SEQ // 32
MAGIC = 12582912.0
TWO_PI = 6.283185307179586
TURN = 6.283185
SIN_SCALE = TWO_PI * (1 - 2.5e-6)
LN2_HI, LN2_LO = 0.693145751953125, 1.42860682030941723212e-6

ROW_B1, ROW_B2, ROW_LDT = 0, HC * NX, (HC + 1) * NX
ROWS = ROW_LDT + 1
S_QT, S_SC = 0, 6
U_FILM, U_DFT, U_FILLS = 0, 4, 6
S_PREP = 4
FILLS = [(r, tiles) for tiles in ([(0, 0)], [(1, 0), (3, 384)], [(2, 0)]) for r in range(2)]
BASE = [0, SEQ, 2 * SEQ, 3 * SEQ, 4 * SEQ, 4 * SEQ + 256]
WIDTH = [SEQ, SEQ, SEQ, SEQ, 256, 256]
NF = len(FILLS)
S_FILLS = S_SC + NF * NPAIR + S_PREP
COL = {(r, j): BASE[n] + c for n, (r, tiles) in enumerate(FILLS) for j, c in tiles}

TOKENS_AT = 2
XT_AT, QKV_AT = (3, 3), (3, 5)
STEPS = [
    (2, 0, 0, "dft", 7), (2, 0, 1, "spectrum"), (3, 0, 5, "x2_norm"), (3, 1, 0, "x2"), (2, 1, 0, "conv", 0),
    (2, 1, 1, "conv", 1), (2, 1, 2, "conv", 2), (2, 1, 3, "conv", 3), (2, 1, 4, "conv", 4), (2, 1, 5, "conv", 5),
    (2, 2, 0, "conv", 6), (2, 2, 1, "conv", 7), (3, 1, 1, "x2T"), (3, 1, 3, "gates"), (1, 1, 4, "yT"),
    (3, 2, 1, "gates_exp"), (1, 2, 0, "proj"), (3, 2, 1, "route"), (1, 2, 3, "x1"), (2, 2, 4, "shape_out"),
    (3, 2, 5, "wT"), (1, 3, 1, "x1T"), (1, 3, 3, "x_norm"), (1, 3, 2, "scores"), (1, 3, 3, "xn"),
    (-1, *XT_AT, "xT"), (2, 3, 4, "h_norm"), (1, 3, 3, "cross_exp"), (-1, *QKV_AT, "qkv"), (2, 4, 1, "h"),
    (1, 4, 1, "soften"), (1, 4, 3, "attnT"), (2, 4, 4, "hT"), (-1, 5, 2, "rms"), (2, 5, 0, "up", 0),
    (2, 5, 1, "up", 1), (2, 5, 2, "up", 2), (2, 5, 3, "up", 3), (-1, 5, 2, "rope"), (2, 5, 1, "gelu"),
    (1, 5, 5, "film", 0), (1, 6, 0, "film", 1), (1, 6, 1, "film", 2), (1, 6, 2, "film", 3), (1, 6, 3, "modulate"),
    (2, 5, 5, "down", 0), (2, 6, 0, "down", 1), (2, 6, 1, "down", 2), (2, 6, 2, "down", 3), (-1, 6, 4, "parts"),
    (1, 6, 5, "dft", 0), (1, 7, 0, "dft", 1), (1, 7, 1, "dft", 2), (1, 7, 2, "dft", 3), (1, 7, 3, "dft", 4),
    (1, 7, 4, "dft", 5), (1, 7, 5, "dft", 6), (2, 7, 0, "ff_out"), (2, 7, 1, "ffT"), (2, 7, 5, "ff_norm"),
]
ONCE = [
    (0, 0, 0, "functions"), (0, 0, 1, "vf"), (0, 0, 3, "states"), (0, 1, 2, "pack"), (0, 1, 3, "args", 0),
    *[(0, *divmod(n + 8 * q, NF), name, q + (name == "args")) for q in range(D // JM)
      for n, name in ((13, "powers"), (15, "taps"), (17, "args"))],
    (1, 1, 1, "first_tap"), *[(1, 1 + (2 + n) // NF, (2 + n) % NF, "kernel", n) for n in range(2 * NT)],
    (1, 3, 1, "spectra"), (1, 3, 3, "text_weights"),
]
SLOTS = 3
PRODUCTS = [(e, b) for rows in ((0, 1), (2,), (3,)) for e in range(SLOTS) for b in rows]
PRODUCTS += [(e, b) for e in range(SLOTS, NM) for b in range(B)]
ROUTED = [q for q, (e, b) in enumerate(PRODUCTS) if e >= NSH]
CHUNKS = HC * len(PRODUCTS)
EARLY_AT = [(B, p, n) for p in range(2, NPAIR) for n in range(NF)][2:2 + 6 * HC]
EARLY_AT += [(B + 1, 2, 3), (B + 1, 2, 5), *[(B + 1, 3, n) for n in range(NF)], (B + 1, 7, 2), (B + 1, 7, 5)]
EARLY_AT += [(B + 2, 0, 0), (B + 2, 0, 1)]
EARLY_AT += [(B + 2, p, n) for p in range(3) for n in range(NF)][10:17]
SPLIT_BEHIND = {1: HC - 1, 2: 3 * HC - 1, 3: 11 * HC - 1}
SPLIT_BEHIND.update({e + 1: HC * (PRODUCTS.index((e, 0)) + 1) - 1 for e in range(SLOTS, NM - 1)})
EARLY = len(EARLY_AT)
EARLY_CHUNKS = [(*at, c) for c, at in enumerate(EARLY_AT)]
FINAL_AT = [CHUNKS - HC * (B - 1 - b) + HC for b in range(B - 1)]


def fill_index(b, what, p=0, n=0):
    if what in ("xT", "qkv"):
        own = n + (2 if what == "qkv" else 0)
        if b == 0:
            return own
        at = XT_AT if what == "xT" else QKV_AT
        return S_PREP + (b - 1) * S_FILLS + S_SC + NF * at[0] + at[1] + 1 + own
    k = S_PREP + b * S_FILLS
    if what == "qT":
        return k + S_QT + n
    extra = 2 * ((p, n) > XT_AT) + 2 * ((p, n) > QKV_AT) if b + 1 < B else 0
    return k + S_SC + NF * p + n + extra


def run(parts, i, p, n):
    for at, q, m, name, *part in ONCE:
        if (at, q, m) == (i, p, n) and name in parts:
            parts[name](*part)
    for after, q, m, name, *part in STEPS:
        b = i - after
        if (q, m) == (p, n) and 0 <= b < B and name in parts:
            parts[name](b, *part)
    for at, q, m, c in EARLY_CHUNKS:
        if (at, q, m) == (i, p, n) and "chunk" in parts:
            parts["chunk"](c)


def iterate(parts, first, fill, close, tokens):
    for name, *row in (("xT", 0), ("qkv", 0), ("rms", 0), ("vectors",), ("fold1",), ("fold2",),
                       ("fold3",), ("fold4",), ("rope", 0), ("parts", 0), ("steps",)):
        if name in parts:
            parts[name](*row)
    for i in range(B + 3):
        if i < B:
            first(i)
        for p in range(NPAIR):
            for n in range(NF):
                if i < B:
                    fill(i, p, n)
                if n == TOKENS_AT and i <= B:
                    tokens(i, p)
                run(parts, i, p, n)
            if i <= B:
                close(i, p)


def build(nc, t, out):
    ctx = ExitStack()
    with ctx:
        def sb(name, shape, dt=F32):
            return ctx.enter_context(nc.sbuf_tensor(name, shape, dt))

        def sem(name):
            return ctx.enter_context(nc.semaphore(name))

        ring_s = [ctx.enter_context(nc.psum_tensor(f"ring_s{i}", [P, 512], F32)) for i in range(2)]
        ring_u = [ctx.enter_context(nc.psum_tensor(f"ring_u{i}", [P, 512], F32)) for i in range(2)]
        bank_o = ctx.enter_context(nc.psum_tensor("bank_o", [P, 512], F32))
        bank_m = ctx.enter_context(nc.psum_tensor("bank_m", [P, 512], F32))
        bank_d = ctx.enter_context(nc.psum_tensor("bank_d", [P, 512], F32))
        bank_r = ctx.enter_context(nc.psum_tensor("bank_r", [P, 512], F32))
        taps_ps = [bank_d, bank_r]
        experts_up = [ring_s[0], ring_s[1], ring_u[0], ring_u[1]]
        down = [bank_o, bank_m]
        text_up = [ring_u[0], ring_u[1], bank_d, bank_r]

        wqkv = sb("wqkv", [P, QKV])
        wo = sb("wo", [P, D])
        ident = sb("ident", [P, P])
        identb = sb("identb", [P, P], BF16)
        pair_sum = sb("pair_sum", [P, 64])
        rope = sb("rope", [P, NT, 2, HD])
        wt_hi = sb("wt_hi", [P, 2 * HID], F32R)
        wt_lo = sb("wt_lo", [P, 2 * HID], F32R)
        vcols = sb("vcols", [P, ROWS])
        b2_shared = sb("b2_shared", [P, 1])
        norms = sb("norms", [P, 6, D])
        film_bias = sb("film_bias", [P, 4 * D])
        router_w = sb("router_w", [P, NE])
        router_b = sb("router_b", [P, NE])
        earlier = sb("earlier", [P, NE, NE])
        spread = sb("spread", [2 * NE, NE], F32R)
        neg_half = sb("neg_half", [P, NT])
        cosm = sb("cosm", [P, NT, SEQ])
        sin_fwd = sb("sin_fwd", [P, NT, SEQ])
        sin_inv = sb("sin_inv", [P, NT, SEQ])
        kc = sb("kc", [P, NT, D])
        ks = sb("ks", [P, NT, D])
        kcn = sb("kcn", [P, NT, D])
        xq = sb("xq", [P, B, XH * G])
        vf = sb("vf", [P, B, 4 * D])
        ctx_bias = sb("ctx_bias", [P, B, XH, G])
        tmask = sb("tmask", [P, B * NT])
        gate = sb("gate", [P, 1])
        gate4 = sb("gate4", [P, 1])

        scratch = ExitStack()
        with scratch:
            def tb(name, shape, dt=F32):
                return scratch.enter_context(nc.sbuf_tensor(name, shape, dt))
            vec_rows = tb("vec_rows", [ROWS, P])
            tm_rows8 = tb("tm_rows8", [B * NT, P], U8)
            tm_rows = tb("tm_rows", [B * NT, P])
            cmask8 = tb("cmask8", [P, B * G], U8)
            cmask = tb("cmask", [P, B * G])
            dskip = tb("dskip", [1, D])
            s4 = tb("s4", [P, 4, NS])
            sm = tb("sm", [P, 12, NS])
            dtc = tb("dtc", [P, 8])
            dti = tb("dti", [P, 2], I32)
            packs = tb("packs", [P, 4, P])
            pk = tb("pk", [P, 4, P])
            pk32 = tb("pk32", [P, 3, P])
            index = tb("index", [P, JM])
            offs = tb("offs", [P, 4])
            pv = tb("pv", [P, JM, JM])
            pt = tb("pt", [P, JM, JM])
            pr = tb("pr", [P, JM, JM])
            wt_raw = pr[:, :, :].rearrange("p a b -> p (a b)")
            uf = tb("uf", [P, JM, IM])
            ug = tb("ug", [P, JM, IM])
            ue = tb("ue", [P, JM, IM])
            kld = pv[:, 0:NT * D // JM, :].rearrange("p a c -> p (a c)").rearrange("p (j d) -> p j d", j=NT)
            ctxs = tb("ctxs", [P, DV])
            ctxT = tb("ctxT", [DV, B * G])
            ctx_rep = uf[0:DV, :, :].rearrange("p a c -> p (a c)").rearrange("p (b n) -> p b n", b=B)
            wk = tb("wk", [DV, P])
            wv = tb("wv", [DV, D])
            wq = tb("wq", [P, P])
            wqT = tb("wqT", [P, P])
            wvT = tb("wvT", [P, DV])
            w_film = tb("w_film", [P, 4 * D])
            kbd = tb("kbd", [P, B * XH * G])
            kij = tb("kij", [IM, JM, D])
            wvf = ug[0:DV, :, :].rearrange("p a c -> p (a c)")

        x2 = sb("x2", [P, B, NT * D])
        t_hi = sb("t_hi", [P, B, SEQ], F32R)
        t_lo = sb("t_lo", [P, B, SEQ], F32R)
        wT = sb("wT", [2 * NE, B, SEQ], F32R)
        g_raw = sb("g_raw", [P, HC, SEQ])
        g_hi = sb("g_hi", [P, HC, SEQ], F32R)
        g_lo = sb("g_lo", [P, HC, SEQ], F32R)
        fa = sb("fa", [P, NT, D])
        ffT = fa[:, :, :].rearrange("p j d -> p (j d)")
        stats = sb("stats", [P, NT, 6])
        mean_var = sb("mean_var", [P, NT, 2])
        var_eps = sb("var_eps", [P, NT])
        rstd = sb("rstd", [P, NT])

        experts = ExitStack()
        with experts:
            def eb(name, shape, dt=F32):
                return experts.enter_context(nc.sbuf_tensor(name, shape, dt))
            acc = eb("acc", [P, B, SEQ])
            e_raw = eb("e_raw", [P, 2 * HID])
            w_hi = eb("w_hi", [P, SLOTS, 2 * HID], F32R)
            w_lo = eb("w_lo", [P, SLOTS, 2 * HID], F32R)
            w_bc = eb("w_bc", [P, 2, SEQ])
            term = eb("term", [P, SEQ])
            eg_raw = eb("eg_raw", [P, SLOTS, SEQ])
            eg_hi = eb("eg_hi", [P, HC, SEQ], F32R)
            eg_lo = eb("eg_lo", [P, HC, SEQ], F32R)

        x_in = sb("x_in", [P, 2, NT, D])
        xT = sb("xT", [P, SEQ])
        qkv = sb("qkv", [P, NT, QKV])
        qT = sb("qT", [P, NPAIR, SEQ], BF16)
        kT = sb("kT", [P, NKV, SEQ], BF16)
        vv = sb("vv", [P, NT, NKV, 32])
        probs = sb("probs", [P, 2, PW])
        oT = sb("oT", [P, 2, SEQ])
        ry = sb("ry", [P, NT, 2])
        y_att = sb("y_att", [P, NT, D])
        yT = xT
        qs = sb("qs", [P, NT * NH, PARTS, HD], BF16)
        tmp_c = sb("tmp_c", [P, NT * QK])[:, :]
        k_parts = sb("k_parts", [P, NT * NKV, 2, PARTS, HD], BF16)
        rms_in = sb("rms_in", [P, NT * (NH + NKV)])
        rms_out = sb("rms_out", [P, NT * (NH + NKV)])
        rms_tmp = sb("rms_tmp", [P, NT * (NH + NKV)])
        rms_bits = rms_out[:, :].bitcast(I32)

        x1 = sb("x1", [P, 2, NT, D])

        x1T = sb("x1T", [P, SEQ])
        sc = sb("sc", [P, NT * XH, G])
        sc_max = sb("sc_max", [P, NT * XH])
        sc_sum = sb("sc_sum", [P, NT * XH])
        attnT = x1T
        film = sb("film", [P, NT, 4 * D])
        xn = sb("xn", [P, NT, D])
        fb = sb("fb", [P, NT, D])
        spec = sb("spec", [P, 2 * NT, D])
        xt = sb("xt", [P, NT, D])
        x2T = attnT
        gates = sb("gates", [P, NT, NE])
        gmax = sb("gmax", [P, NT])
        cmp_a, cmp_b = (fb[:, 2 * k:2 * k + 2, :].rearrange("p a (j e f) -> p (a j) e f", j=2, e=NE) for k in range(2))
        chosen = sb("chosen", [P, NT, NE])
        w_tok = sb("w_tok", [P, NT, NE])
        w_round = sb("w_round", [P, NT, NE], F32R)
        w_parts = sb("w_parts", [P, NT, 2 * NE])

        ld_attn, ld_s4, ld_vec, ld_cross, ld_dft, ld_rest, ld_wt = (
            sem(n) for n in ("ld_attn", "ld_s4", "ld_vec", "ld_cross", "ld_dft", "ld_rest", "ld_wt"))
        ld_w = sem("ld_w")
        w_split = sem("w_split")
        x_landed = sem("x_landed")
        x_used = sem("x_used")
        out_sent = sem("out_sent")
        consts_ready = sem("consts_ready")
        pro_pe = sem("pro_pe")
        pro_sb = sem("pro_sb")
        pro_arg = sem("pro_arg")
        pro_fun = sem("pro_fun")
        exponents_ready = sem("exponents_ready")
        kij_ready = sem("kij_ready")
        kij_sent = sem("kij_sent")
        kld_landed = sem("kld_landed")
        kconst_ready = sem("kconst_ready")
        wt_split = sem("wt_split")
        s_full = sem("s_full")
        s_free = sem("s_free")
        u_full = sem("u_full")
        u_free = sem("u_free")
        var_ready = sem("var_ready")
        rstd_ready = sem("rstd_ready")
        rms_ready, roped, parts_ready, v_ready = (sem(n) for n in ("rms_ready", "roped", "parts_ready", "v_ready"))
        exp_done = sem("exp_done")
        masked = sem("masked")
        pv_done = sem("pv_done")
        oT_ready = sem("oT_ready")
        y_ps = sem("y_ps")
        y_ready = sem("y_ready")
        yT_ps, yT_sb, proj_ps, x1_ready = (sem(n) for n in ("yT_ps", "yT_sb", "proj_ps", "x1_ready"))
        x1T_ps, x1T_sb, sc_ps = (sem(n) for n in ("x1T_ps", "x1T_sb", "sc_ps"))
        sc_ready, sc_exp, attn_ready, attnT_ps, attnT_sb = (sem(n) for n in (
            "sc_ready", "sc_exp", "attn_ready", "attnT_ps", "attnT_sb"))
        xn_scaled, xn_ready, xmod_ready, spec_ready, conv_ps = (sem(n) for n in (
            "xn_scaled", "xn_ready", "xmod_ready", "spec_ready", "conv_ps"))
        h_scaled, h_ready, hT_ps, hT_sb = (sem(n) for n in ("h_scaled", "h_ready", "hT_ps", "hT_sb"))
        shaped, xt_ready = sem("shaped"), sem("xt_ready")
        up_ps = sem("up_ps")
        gelu_done = sem("gelu_done")
        split_done = sem("split_done")
        down_ps, ffT_sb, ffn_tok, tok_used = (sem(n) for n in ("down_ps", "ffT_sb", "ffn_tok", "tok_used"))
        ff_scaled, sum_ready, x2_ready, x2T_ps, x2T_sb, x2_split = (sem(n) for n in (
            "ff_scaled", "sum_ready", "x2_ready", "x2T_ps", "x2T_sb", "x2_split"))
        gates_ps, gates_ready, gates_exp, wtok_ready, wT_ps, wT_sb = (sem(n) for n in (
            "gates_ps", "gates_ready", "gates_exp", "wtok_ready", "wT_ps", "wT_sb"))
        e_up, e_gelu, e_split, e_down = (sem(n) for n in ("e_up", "e_gelu", "e_split", "e_down"))
        bc_ps, bc_sb, settled, accT_ps = (sem(n) for n in ("bc_ps", "bc_sb", "settled", "accT_ps"))
        y_out_ready = sem("y_out_ready")
        acc_used = sem("acc_used")
        dve_step = sem("dve_step")
        pool_step = sem("pool_step")

        x_dram = t["x"]
        kernel_dram = nc.dram_tensor("s4d_kernel", (SEQ, D), F32, kind="Internal").ap()
        block = ctx.enter_context(nc.Block())

        @block.sync
        def _(sp):
            def load(dst, src, s):
                sp.dma_start(dst, src).then_inc(s, 16)

            def load_x(b):
                if b >= 2:
                    sp.wait_ge(x_used, b - 1)
                load(x_in[:, b % 2, :, :], x_dram[b].rearrange("(j p) d -> p j d", p=P), x_landed)

            load_x(0)
            load(ident[:, :], t["c_ident"], ld_attn)
            load(wqkv[:, 0:NH * HD], t["L0_attn_w_q"], ld_attn)
            load(wqkv[:, NH * HD:QK], t["L0_attn_w_k"], ld_attn)
            load(wqkv[:, QK:QKV], t["L0_attn_w_v"], ld_attn)
            load(rope[:, :, :, :].rearrange("p j c e -> p (j c e)"), t["c_rope"], ld_attn)
            load(wo[:, :], t["L0_attn_w_o"], ld_attn)
            load(pair_sum[:, :], t["c_pair_sum"], ld_attn)
            load(vec_rows[ROW_B1:ROW_B1 + HC, :], t["L0_xattn_b1"].rearrange("(c p) -> c p", p=P), ld_vec)
            load(vec_rows[ROW_B1 + HC:ROW_B1 + HC * (1 + NSH), :], t["L0_ffn_sb1"].rearrange("s (c p) -> (s c) p", p=P), ld_vec)
            load(vec_rows[ROW_B1 + HC * (1 + NSH):ROW_B2, :], t["L0_ffn_b1"].rearrange("s (c p) -> (s c) p", p=P), ld_vec)
            load(vec_rows[ROW_B2:ROW_B2 + 1, :], t["L0_xattn_b2"].rearrange("(c p) -> c p", p=P), ld_vec)
            load(vec_rows[ROW_B2 + 1:ROW_B2 + 1 + NSH, :], t["L0_ffn_sb2"], ld_vec)
            load(vec_rows[ROW_B2 + 1 + NSH:ROW_LDT, :], t["L0_ffn_b2"], ld_vec)
            load(vec_rows[ROW_LDT:ROWS, :], t["L0_xattn_log_dt"].rearrange("(c p) -> c p", p=P), ld_vec)
            load(ctxs[:, :], t["ctx_768"].rearrange("b g d -> (b g) d"), ld_cross)
            load(wq[:, :], t["L0_xattn_Wq"], ld_cross)
            load(wk[:, :], t["L0_xattn_Wk"], ld_cross)
            load(wv[:, :], t["L0_xattn_Wv"], ld_cross)
            load(w_film[:, 0:2 * D], t["L0_xattn_W_film_in"], ld_cross)
            load(w_film[:, 2 * D:4 * D], t["L0_xattn_W_film_out"], ld_cross)
            load(gate[:, :], t["L0_xattn_mod_gate"].partition_broadcast(P), ld_cross)
            load(film_bias[:, 0:2 * D], t["L0_xattn_b_film_in"].partition_broadcast(P), ld_cross)
            load(film_bias[:, 2 * D:4 * D], t["L0_xattn_b_film_out"].partition_broadcast(P), ld_cross)
            load(tm_rows8[:, :], t["mask_BxS_bf1"].rearrange("b (j p) -> (b j) p", p=P), ld_cross)
            load(cmask8[:, :], t["mask_BxS2_bf1"].rearrange("b g -> (b g)").partition_broadcast(P), ld_cross)
            for n, k in enumerate(("A_re", "A_im", "C_re", "C_im")):
                load(s4[:, n, :], t[f"L0_xattn_{k}"], ld_s4)
            load(index[:, :], t["c_index"].partition_broadcast(P), ld_s4)
            load(offs[:, :], t["c_offs"], ld_s4)
            load(dskip[:, :], t["L0_xattn_D_skip"].rearrange("(c p) -> c p", p=P), ld_s4)
            load_x(1)
            for m, k in ((cosm, "c_cos"), (sin_fwd, "c_sin_fwd"), (sin_inv, "c_sin_inv")):
                load(m[:, :, :], t[k].rearrange("(j p) f -> p j f", p=P), ld_dft)
            for n, k in enumerate(("g_norm_in", "b_norm_in", "g_ffn", "b_ffn", "g_norm_out", "b_norm_out")):
                load(norms[:, n, :], t[f"L0_xattn_{k}"].partition_broadcast(P), ld_rest)
            load(router_w[:, :], t["L0_ffn_rW"], ld_rest)
            load(router_b[:, :], t["L0_ffn_rb"].partition_broadcast(P), ld_rest)
            load(earlier[:, :, :].rearrange("p a b -> p (a b)"), t["c_earlier"].partition_broadcast(P), ld_rest)
            sp.wait_ge(kij_ready, 1)
            load(kernel_dram.rearrange("(i j) d -> i (j d)", i=IM), kij.rearrange("i j d -> i (j d)"), kij_sent)
            sp.wait_ge(kij_sent, 16)
            load(kld, kernel_dram.rearrange("(j p) d -> p j d", p=P), kld_landed)
            load(wt_raw[:, 0:HID], t["L0_xattn_W1"], ld_wt)
            load(wt_raw[:, HID:2 * HID].rearrange("p (c d) -> p c d", c=HC),
                 t["L0_xattn_W2"].rearrange("(c p) d -> p c d", p=P), ld_wt)
            for b in range(2, B):
                load_x(b)
            sp.wait_ge(pv_done, B * NPAIR)
            for e in range(NM):
                if e:
                    sp.wait_ge(w_split, e)
                w1, w2 = (t["L0_ffn_sW1"][e], t["L0_ffn_sW2"][e]) if e < NSH else (
                    t["L0_ffn_W1"][e - NSH], t["L0_ffn_W2"][e - NSH])
                load(e_raw[:, 0:HID], w1, ld_w)
                load(e_raw[:, HID:2 * HID].rearrange("p (c d) -> p c d", c=HC), w2.rearrange("(c p) d -> p c d", p=P), ld_w)
            for b in range(B):
                sp.wait_ge(y_out_ready, b + 1)
                sp.dma_start(out[b].rearrange("(j p) d -> p j d", p=P), x2[:, b, :].rearrange("p (j d) -> p j d", j=NT)).then_inc(out_sent, 16)
            sp.wait_ge(out_sent, 16 * B)

        @block.tensor
        def _(pe):
            mm = nc.tensor.matmul

            def tp(dst, src):
                return nc.tensor.transpose(dst, src, ident[0:src.shape[0], 0:src.shape[0]])

            def s_fill(k):
                if k >= 2:
                    pe.wait_ge(s_free, k - 1)
                return ring_s[k % 2]

            def vectors():
                pe.wait_ge(ld_vec, 16 * 7)
                tp(bank_d[:, 0:ROWS], vec_rows[:, :]).then_inc(pro_pe, 1)

            def fold1():
                pe.wait_ge(ld_cross, 16 * 11)
                tp(bank_r[:, 0:P], wq[:, :])
                tp(bank_r[0:DV, P:2 * P], ctxs[:, :])
                tp(bank_r[:, 2 * P:2 * P + DV], wv[:, :])
                pe.wait_ge(pro_sb, 1)
                tp(bank_r[:, 3 * P:3 * P + B * NT], tm_rows[:, :]).then_inc(pro_pe, 1)

            def fold2():
                pe.wait_ge(pro_sb, 2)
                mm(ring_u[0][:, 0:B * G], wk[:, :], ctxT[:, :], start=True, stop=True).then_inc(pro_pe, 1)
                mm(ring_u[1][0:DV, :], wvT[:, :], w_film[:, :], start=True, stop=True).then_inc(pro_pe, 1)

            def fold3():
                pe.wait_ge(pro_sb, 3)
                mm(bank_d[:, :], wqT[:, :], kbd[:, :], start=True, stop=True).then_inc(pro_pe, 1)

            def fold4():
                pe.wait_ge(pro_sb, 5)
                for b in range(B):
                    dst = (bank_r, ring_u[0], ring_u[1], bank_d)[b]
                    mm(dst[:, :], ctx_rep[:, b, :], wvf, start=True, stop=True).then_inc(pro_pe, 1)

            def pack():
                pe.wait_ge(pro_sb, 6)
                for n in range(4):
                    last = tp(ring_u[0][:, n * P:(n + 1) * P], packs[:, n, :])
                last.then_inc(pro_pe, 1)

            def taps(q):
                pe.wait_ge(pro_sb, 7 + q)
                for h in range(2):
                    for d in range(16):
                        last = mm(taps_ps[h][0:IM, JM * d:JM * (d + 1)], uf[:, 16 * h + d, :], pv[:, 16 * h + d, :],
                                  start=True, stop=True)
                last.then_inc(pro_pe, 1)

            def kernel_dft(f):
                if f == 0:
                    pe.wait_ge(kconst_ready, 1)
                    pe.wait_ge(ld_dft, 48)
                mat, c = (cosm, f) if f < NT else (sin_fwd, f - NT)
                for j in range(NT):
                    last = mm(ring_u[f // NT][:, P * c:P * (c + 1)], mat[:, j, P * c:P * (c + 1)],
                              kld[:, j, :], start=(j == 0), stop=(j == NT - 1))
                if f == 2 * NT - 1:
                    last.then_inc(pro_pe, 1)

            def xT_step(b):
                pe.wait_ge(x_landed, 16 * (b + 1))
                if b == 0:
                    pe.wait_ge(ld_attn, 16 * 7)
                for n in range(2):
                    bank = s_fill(fill_index(b, "xT", n=n))
                    for j in range(2):
                        last = tp(bank[:, P * j:P * (j + 1)], x_in[:, b % 2, 2 * n + j, :])
                    last.then_inc(s_full, 1)

            def qkv_step(b):
                pe.wait_ge(s_free, fill_index(b, "xT", n=1) + 1)
                for n in range(2):
                    bank = s_fill(fill_index(b, "qkv", n=n))
                    for j in range(2):
                        k = 2 * n + j
                        last = mm(bank[:, QKV * j:QKV * (j + 1)], xT[:, P * k:P * (k + 1)], wqkv[:, :],
                                  start=True, stop=True)
                    last.then_inc(s_full, 1)

            def first(b):
                if b == 0:
                    pe.wait_ge(consts_ready, 1)
                pe.wait_ge(parts_ready, b + 1)
                for n in range(6):
                    bank = s_fill(fill_index(b, "qT", n=n))[:, :].bitcast(BF16).rearrange("p (a j q) -> p a j q", a=2, j=NT)
                    for a in range(2):
                        for j in range(NT):
                            if n < 4:
                                src = qs[:, j * NH + 2 * (2 * n + a):j * NH + 2 * (2 * n + a) + 2, :, :]
                                src = src.rearrange("p n c e -> p (n c e)")
                            else:
                                src = k_parts[:, j * NKV + 2 * (n - 4) + a, :, :, :].rearrange("p n c e -> p (n c e)")
                            last = nc.tensor.transpose(bank[:, a, j, :], src, identb[:, :])
                    last.then_inc(s_full, 1)
                pe.wait_ge(s_free, fill_index(b, "qT", n=5) + 1)

            def fill(b, p, n):
                r, tiles = FILLS[n]
                bank = s_fill(fill_index(b, "sc", p, n))
                for j, c in tiles:
                    w = SEQ - P * j
                    last = mm(bank[:, c:c + w], kT[64 * r:64 * r + 64, p // 2, P * j:P * (j + 1)],
                              qT[64 * r:64 * r + 64, p, P * j:SEQ], start=True, stop=True)
                last.then_inc(s_full, 1)

            def values(pair):
                b, p = divmod(pair, NPAIR)
                pe.wait_ge(masked, pair + 1)
                if pair >= 1:
                    pe.wait_ge(oT_ready, pair)
                if p == 0:
                    pe.wait_ge(v_ready, b + 1)
                if p == 1 and b:
                    pe.wait_ge(x_used, b)
                for start in (True, False):
                    for s in range(4):
                        r, j = s % 2, ((0, 3), (1, 2))[s // 2][0 if start else 1]
                        c = COL[(r, j)]
                        last = mm(bank_o[32 * s:32 * s + 32, P * j:SEQ], vv[:, j, p // 2, :],
                                  probs[:, p % 2, c:c + SEQ - P * j], start=start, stop=not start)
                last.then_inc(pv_done, 1)

            def token_rows(pair):
                b, p = divmod(pair, NPAIR)
                pe.wait_ge(oT_ready, pair + 1)
                if pair >= 1:
                    pe.wait_ge(y_ready, pair)
                if p == 0 and b:
                    pe.wait_ge(yT_sb, b)
                for j in range(NT):
                    c = 256 * (p % 2) + 64 * j
                    last = mm(bank_m[:, c:c + 64], oT[:, p % 2, P * j:P * (j + 1)], pair_sum[:, :],
                              start=True, stop=True)
                last.then_inc(y_ps, 1)

            def close(i, p):
                pair = i * NPAIR + p - 1
                if 0 <= pair < B * NPAIR:
                    values(pair)

            def tokens(i, p):
                pair = i * NPAIR + p - 2
                if 0 <= pair < B * NPAIR:
                    token_rows(pair)

            def yT_step(b):
                pe.wait_ge(y_ready, NPAIR * (b + 1))
                for j in range(NT):
                    last = tp(bank_m[:, P * j:P * (j + 1)], y_att[:, j, :])
                last.then_inc(yT_ps, 1)

            def proj(b):
                pe.wait_ge(yT_sb, b + 1)
                pe.wait_ge(oT_ready, NPAIR * (b + 1) + (b + 1 < B))
                for j in range(NT):
                    last = mm(bank_o[:, P * j:P * (j + 1)], yT[:, P * j:P * (j + 1)], wo[:, :], start=True, stop=True)
                last.then_inc(proj_ps, 1)

            def three(bank, hi, lo, a_hi, a_lo, start, stop):
                for k, (w, a) in enumerate(((hi, a_hi), (hi, a_lo), (lo, a_hi))):
                    last = mm(bank[:, :], w, a, start=(start and k == 0), stop=(stop and k == 2))
                return last

            def x1T_step(b):
                pe.wait_ge(x1_ready, b + 1)
                if b >= 2:
                    pe.wait_ge(wT_sb, b - 1)
                for j in range(NT):
                    last = tp(bank_r[:, P * j:P * (j + 1)], x1[:, b % 2, j, :])
                last.then_inc(x1T_ps, 1)

            def scores(b):
                pe.wait_ge(x1T_sb, b + 1)
                if b:
                    pe.wait_ge(shaped, b)
                for j in range(NT):
                    last = mm(bank_d[:, P * j:P * (j + 1)], x1T[:, P * j:P * (j + 1)], xq[:, b, :], start=True, stop=True)
                last.then_inc(sc_ps, 1)

            def attnT_step(b):
                pe.wait_ge(attn_ready, b + 1)
                for j in range(NT):
                    last = tp(bank_r[:, P * j:P * (j + 1)], sc[:, XH * j:XH * (j + 1), :].rearrange("p h g -> p (h g)"))
                last.then_inc(attnT_ps, 1)

            def film_step(b, j):
                if j == 0:
                    pe.wait_ge(attnT_sb, b + 1)
                    if b:
                        pe.wait_ge(gelu_done, HC * b)
                if j >= 2:
                    pe.wait_ge(u_free, b * U_FILLS + j - 1)
                mm(ring_u[j % 2][:, :], attnT[:, P * j:P * (j + 1)], vf[:, b, :], start=True, stop=True).then_inc(u_full, 1)

            def dft(b, n):
                f, c = divmod(n, NT)
                if n == 0:
                    pe.wait_ge(xmod_ready, b + 1)
                mat = (cosm, sin_fwd)[f]
                for j in range(NT):
                    last = mm(ring_u[f][:, P * c:P * (c + 1)], mat[:, j, P * c:P * (c + 1)], xn[:, j, :],
                              start=(j == 0), stop=(j == NT - 1))
                if c == NT - 1:
                    last.then_inc(u_full, 1)

            def conv(b, n):
                if n == 0:
                    pe.wait_ge(spec_ready, b + 1)
                    if b:
                        pe.wait_ge(ffT_sb, b)
                j, half = divmod(n, 2)
                for f in range(NT * half, NT * (half + 1)):
                    mat = cosm if f < NT else sin_inv
                    last = mm(bank_d[:, P * j:P * (j + 1)], mat[:, f % NT, P * j:P * (j + 1)], spec[:, f, :],
                              start=(f == 0), stop=(f == 2 * NT - 1))
                if n == 2 * NT - 1:
                    last.then_inc(conv_ps, 1)

            def hT_step(b):
                pe.wait_ge(h_ready, b + 1)
                if b:
                    pe.wait_ge(wT_sb, b)
                if b + 1 < B:
                    pe.wait_ge(attnT_sb, b + 2)
                for j in range(NT):
                    last = tp(bank_r[:, P * j:P * (j + 1)], fa[:, j, :])
                last.then_inc(hT_ps, 1)

            def up_step(b, n):
                if n == 0:
                    pe.wait_ge(wt_split, 1)
                    pe.wait_ge(hT_sb, b + 1)
                if n == 2 and b + 1 < B:
                    pe.wait_ge(sc_ready, b + 2)
                c = slice(P * n, P * (n + 1))
                three(text_up[n], wt_hi[:, c], wt_lo[:, c], t_hi[:, b, :], t_lo[:, b, :], True, True).then_inc(up_ps, 1)

            def down_step(b, n):
                if n == 0:
                    pe.wait_ge(gelu_done, b * HC + 3)
                pe.wait_ge(split_done, b * HC + n + 1)
                c = slice(HID + P * n, HID + P * (n + 1))
                last = three(bank_d, wt_hi[:, c], wt_lo[:, c], g_hi[:, n, :], g_lo[:, n, :], n == 0, n == HC - 1)
                if n == HC - 1:
                    last.then_inc(down_ps, 1)

            def ffT_step(b):
                pe.wait_ge(ffT_sb, b + 1)
                for j in range(NT):
                    last = tp(bank_r[:, P * j:P * (j + 1)], ffT[:, P * j:P * (j + 1)])
                last.then_inc(ffn_tok, 1)

            def x2T_step(b):
                pe.wait_ge(x2_ready, b + 1)
                for j in range(NT):
                    last = tp(bank_r[:, P * j:P * (j + 1)], x2[:, b, P * j:P * (j + 1)])
                last.then_inc(x2T_ps, 1)

            def gates_step(b):
                pe.wait_ge(x2T_sb, b + 1)
                for j in range(NT):
                    last = mm(bank_r[:, NE * j:NE * (j + 1)], x2T[:, P * j:P * (j + 1)], router_w[:, :], start=True, stop=True)
                last.then_inc(gates_ps, 1)

            def wT_step(b):
                pe.wait_ge(wtok_ready, b + 1)
                for j in range(NT):
                    last = tp(bank_r[0:2 * NE, P * j:P * (j + 1)], w_parts[:, j, :])
                last.then_inc(wT_ps, 1)

            def up_ps_of(c):
                return experts_up[c % (2 if c < EARLY else HC)]

            def up(c):
                (e, b), n = PRODUCTS[c // HC], c % HC
                if c == 0:
                    pe.wait_ge(s_free, fill_index(B - 1, "sc", NPAIR - 1, NF - 1) + 1)
                if n == 0:
                    pe.wait_ge(w_split, e + 1)
                    pe.wait_ge(x2_split, b + 1)
                if e >= NSH and n == 1:
                    q = c // HC
                    pe.wait_ge(wT_sb, b + 1)
                    if c < EARLY:
                        pe.wait_ge(settled, q - 1)
                    elif ROUTED.index(q):
                        pe.wait_ge(bc_sb, ROUTED.index(q))
                    mm((down[q % 2] if c < EARLY else bank_r)[:, :], spread[:, e - NSH:e - NSH + 1].broadcast_to([2 * NE, P]), wT[:, b, :],
                       start=True, stop=True).then_inc(bc_ps, 1)
                if 2 <= c < EARLY + HC:
                    pe.wait_ge(e_gelu, min(c, EARLY + 2) - 1)
                if c >= EARLY + HC:
                    pe.wait_ge(e_gelu, c - HC + 1)
                w = slice(P * n, P * (n + 1))
                three(up_ps_of(c), w_hi[:, e % SLOTS, w], w_lo[:, e % SLOTS, w], t_hi[:, b, :], t_lo[:, b, :],
                      True, True).then_inc(e_up, 1)

            def down_product(c):
                (e, b), n = PRODUCTS[c // HC], c % HC
                q = c // HC
                if n == 0 and q >= 2:
                    pe.wait_ge(settled, q - 1)
                if n == 0 and e >= NSH and c + 1 < EARLY:
                    pe.wait_ge(bc_sb, ROUTED.index(q) + 1)
                pe.wait_ge(e_split, c + 1)
                w = slice(HID + P * n, HID + P * (n + 1))
                three(down[q % 2], w_hi[:, e % SLOTS, w], w_lo[:, e % SLOTS, w], eg_hi[:, n, :], eg_lo[:, n, :],
                      n == 0, n == HC - 1).then_inc(e_down, 1)

            def chunk(c):
                if c < CHUNKS:
                    up(c)
                if c >= LAG:
                    down_product(c - LAG)

            def final(b):
                pe.wait_ge(settled, NM * B - B + b + 1)
                if b:
                    pe.wait_ge(acc_used, b)
                for j in range(NT):
                    last = tp(bank_d[:, P * j:P * (j + 1)], acc[:, b, P * j:P * (j + 1)])
                last.then_inc(accT_ps, 1)

            def moe():
                for c in range(EARLY, CHUNKS + LAG):
                    chunk(c)
                    for b in range(B - 1):
                        if c == FINAL_AT[b]:
                            final(b)
                final(B - 1)

            iterate({"vectors": vectors, "fold1": fold1, "fold2": fold2, "fold3": fold3, "fold4": fold4, "pack": pack,
                     "taps": taps, "kernel": kernel_dft, "xT": xT_step, "qkv": qkv_step, "yT": yT_step, "proj": proj,
                     "x1T": x1T_step, "scores": scores, "attnT": attnT_step, "film": film_step, "dft": dft, "conv": conv,
                     "hT": hT_step, "up": up_step, "down": down_step, "ffT": ffT_step, "x2T": x2T_step,
                     "gates": gates_step, "wT": wT_step, "chunk": chunk}, first, fill, close, tokens)
            moe()

        @block.scalar
        def _(act):
            f = nc.scalar.activation

            def states():
                act.wait_ge(pro_arg, 1)
                f(sm[:, 2, :], sm[:, 0, :], ACT.Tanh, scale=0.5).then_inc(pro_fun, 1)
                act.wait_ge(pro_arg, 2)
                f(sm[:, 3, :], sm[:, 4, :], ACT.Sin, scale=TURN / 2)
                f(sm[:, 5, :], sm[:, 4, :], ACT.Sin, scale=TURN).then_inc(pro_fun, 1)

            def powers(q):
                if q:
                    act.wait_ge(pro_pe, 10 + q)
                act.wait_ge(pro_arg, 3 + 2 * q)
                f(pv[:, :, :], pt[:, :, :], ACT.Sin, scale=-SIN_SCALE, bias=offs[:, 2:3]).then_inc(pro_fun, 1)
                act.wait_ge(pro_arg, 4 + 2 * q)
                f(uf[:, :, :], uf[:, :, :], ACT.Sin, scale=-SIN_SCALE, bias=offs[:, 2:3])
                f(ug[:, :, :], ug[:, :, :], ACT.Sin, scale=-SIN_SCALE, bias=offs[:, 3:4]).then_inc(pro_fun, 1)
                act.wait_ge(exponents_ready, q + 1)
                f(pr[:, :, :], pr[:, :, :], ACT.Exp)
                f(ue[:, :, :], ue[:, :, :], ACT.Exp).then_inc(pro_fun, 1)

            def xT_step(b):
                for n in range(2):
                    k = fill_index(b, "xT", n=n)
                    act.wait_ge(s_full, k + 1)
                    if b >= 2:
                        act.wait_ge(proj_ps, b - 1)
                    f(xT[:, 2 * P * n:2 * P * (n + 1)], ring_s[k % 2][:, 0:2 * P], ACT.Copy).then_inc(s_free, 1)

            def qkv_step(b):
                for n in range(2):
                    k = fill_index(b, "qkv", n=n)
                    act.wait_ge(s_full, k + 1)
                    if b:
                        act.wait_ge(v_ready, b)
                    f(qkv[:, 2 * n:2 * n + 2, :].rearrange("p j c -> p (j c)"), ring_s[k % 2][:, 0:2 * QKV], ACT.Copy).then_inc(s_free, 1)

            def first(b):
                for n in range(6):
                    k = fill_index(b, "qT", n=n)
                    act.wait_ge(s_full, k + 1)
                    dst = qT[:, 2 * n:2 * n + 2, :] if n < 4 else kT[:, 2 * (n - 4):2 * (n - 4) + 2, :]
                    f(dst.rearrange("p a q -> p (a q)"), ring_s[k % 2][:, :].bitcast(BF16), ACT.Copy).then_inc(s_free, 1)

            def fill(b, p, n):
                k = fill_index(b, "sc", p, n)
                if b * NPAIR + p >= 2 and n == 0:
                    act.wait_ge(pv_done, b * NPAIR + p - 1)
                act.wait_ge(s_full, k + 1)
                f(probs[:, p % 2, BASE[n]:BASE[n] + WIDTH[n]], ring_s[k % 2][:, 0:WIDTH[n]], ACT.Tanh,
                  scale=1.0 / (CAP * float(np.sqrt(np.float32(HD))))).then_inc(s_free, 1)

            def close(i, p):
                if i < B:
                    act.wait_ge(s_free, fill_index(i, "sc", p, NF - 1) + 1)
                    f(probs[:, p % 2, :], probs[:, p % 2, :], ACT.Exp, scale=CAP).then_inc(exp_done, 1)

            def x1T_step(b):
                act.wait_ge(x1T_ps, b + 1)
                if b >= 2:
                    act.wait_ge(x2_split, b - 1)
                f(x1T[:, :], bank_r[:, :], ACT.Copy).then_inc(x1T_sb, 1)

            def cross_exp(b):
                act.wait_ge(sc_ready, b + 1)
                f(sc[:, :, :], sc[:, :, :], ACT.Exp).then_inc(sc_exp, 1)

            def attnT_step(b):
                act.wait_ge(attnT_ps, b + 1)
                f(attnT[:, :], bank_r[:, :], ACT.Copy).then_inc(attnT_sb, 1)

            def gelu(b):
                for n in range(HC):
                    act.wait_ge(up_ps, b * HC + n + 1)
                    if b:
                        act.wait_ge(split_done, HC * (b - 1) + n + 1)
                    f(g_raw[:, n, :], text_up[n][:, :], ACT.Gelu, bias=vcols[:, ROW_B1 + n:ROW_B1 + n + 1]).then_inc(gelu_done, 1)

            def ff_out(b):
                act.wait_ge(down_ps, b + 1)
                f(ffT, bank_d[:, :], ACT.Identity, bias=vcols[:, ROW_B2:ROW_B2 + 1]).then_inc(ffT_sb, 1)

            def x2T_step(b):
                act.wait_ge(x2T_ps, b + 1)
                f(x2T[:, :], bank_r[:, :], ACT.Copy).then_inc(x2T_sb, 1)

            def gates_exp_step(b):
                act.wait_ge(gates_ready, b + 1)
                f(w_tok[:, :, :], w_tok[:, :, :], ACT.Exp).then_inc(gates_exp, 1)

            def chunk(c):
                if c >= CHUNKS:
                    return
                (e, b), n = PRODUCTS[c // HC], c % HC
                if e >= NSH and n == 2:
                    q = c // HC
                    r = ROUTED.index(q)
                    act.wait_ge(bc_ps, r + 1)
                    if r >= 2:
                        act.wait_ge(settled, ROUTED[r - 2] + 1)
                    f(w_bc[:, r % 2, :], (down[q % 2] if c - 1 < EARLY else bank_r)[:, :], ACT.Copy).then_inc(bc_sb, 1)
                act.wait_ge(e_up, c + 1)
                k = ROW_B1 + HC * (1 + e) + n
                if c >= SLOTS:
                    act.wait_ge(e_split, c - SLOTS + 1)
                bank = experts_up[c % (2 if c < EARLY else HC)]
                raw = eg_raw[:, c % SLOTS, :]
                if n == HC - 1:
                    f(raw, bank[:, :], ACT.Gelu, bias=vcols[:, k:k + 1]).then_inc(e_gelu, 1)
                    return
                f(raw, bank[:, :], ACT.Gelu, bias=vcols[:, k:k + 1])
                if c >= HC:
                    act.wait_ge(e_down, c - HC + 1)
                f(eg_hi[:, n, :], bank[:, :], ACT.Gelu, bias=vcols[:, k:k + 1]).then_inc(e_gelu, 1)
            def moe():
                for c in range(EARLY, CHUNKS):
                    chunk(c)

            iterate({"functions": states, "powers": powers, "xT": xT_step, "qkv": qkv_step, "x1T": x1T_step,
                     "cross_exp": cross_exp, "attnT": attnT_step, "gelu": gelu, "ff_out": ff_out, "x2T": x2T_step,
                     "gates_exp": gates_exp_step, "chunk": chunk}, first, fill, close, lambda i, p: None)
            moe()

        @block.gpsimd
        def _(pool):
            g = nc.gpsimd
            count = [0]
            roots = [0]

            def op(ins):
                count[0] += 1
                ins.then_inc(pool_step, 1)

            def then():
                pool.wait_ge(pool_step, count[0])

            g.memset(neg_half[:, :], -0.5)
            op(g.memset(vv[:, :, :, :], 0.0))
            then()
            g.memset(vv[:, :, :, HD:HD + 1], 1.0)
            pool.wait_ge(ld_attn, 16 * 7)
            g.tensor_copy(identb[:, :], ident[:, :]).then_inc(consts_ready, 1)

            def power(*_):
                roots[0] += 1
                pool.wait_ge(var_ready, roots[0])
                g.tensor_tensor(rstd[:, :], var_eps[:, :], neg_half[:, :], ALU.pow).then_inc(rstd_ready, 1)

            def exponents(q):
                pool.wait_ge(pro_arg, 4 + 2 * q)
                for x, a, m in ((pr, pk[:, 0, :], JM), (ue, pk32[:, 0, :], IM)):
                    last = g.tensor_tensor(x[:, :, :], a[:, JM * q:JM * (q + 1)].unsqueeze(2).broadcast_to([P, JM, m]),
                                           index[:, 0:m].unsqueeze(1).broadcast_to([P, JM, m]), ALU.mult)
                last.then_inc(exponents_ready, 1)

            def rope_step(b):
                heads, half = NH + NKV, HD // 2
                r4 = lambda x: x.rearrange("p (j h e) -> p j h e", j=NT, h=heads)
                rp = lambda c, lo: rope[:, :, c:c + 1, lo:lo + half]
                pool.wait_ge(rms_ready, b + 1)
                for j in range(NT):
                    qk = qkv[:, j, 0:QK].rearrange("p (h e) -> p h e", e=HD)
                    op(g.tensor_tensor(qk, qk, rms_out[:, heads * j:heads * (j + 1)].unsqueeze(2).broadcast_to([P, heads, HD]), ALU.mult))
                then()
                x4 = qkv[:, :, 0:QK].rearrange("p j (h e) -> p j h e", h=heads)
                op(g.tensor_tensor(r4(tmp_c)[:, :, :, 0:half], x4[:, :, :, half:HD], rp(1, 0).broadcast_to([P, NT, heads, half]), ALU.mult))
                op(g.tensor_tensor(r4(tmp_c)[:, :, :, half:HD], x4[:, :, :, 0:half], rp(1, half).broadcast_to([P, NT, heads, half]), ALU.mult))
                then()
                op(g.tensor_tensor(x4, x4, rope[:, :, 0:1, :].broadcast_to([P, NT, heads, HD]), ALU.mult))
                then()
                g.tensor_tensor(qkv[:, :, 0:QK], qkv[:, :, 0:QK], tmp_c.rearrange("p (j c) -> p j c", j=NT), ALU.add).then_inc(roped, 1)

            def close(i, p):
                if i == B:
                    return
                pool.wait_ge(exp_done, i * NPAIR + p + 1)
                pr = probs[:, p % 2, :]
                for v in (pr[:, 0:4 * SEQ].rearrange("p (n w) -> p n w", w=SEQ)[:, :, 0:P],
                          pr[:, 2 * SEQ:4 * SEQ].rearrange("p (n w) -> p n w", w=SEQ)[:, :, 384:SEQ],
                          pr[:, 4 * SEQ:5 * SEQ].rearrange("p (n w) -> p n w", w=256)[:, :, 0:P]):
                    last = g.affine_select(out=v, in_=v, compare_op=ALU.is_ge, fill=0.0, base=0,
                                           pattern=[[0, v.shape[1]], [1, P]], channel_multiplier=-1)
                last.then_inc(masked, 1)

            def affine(x, n):
                op(g.tensor_tensor(x[:, :, :], x[:, :, :], norms[:, n:n + 1, :].broadcast_to([P, NT, D]), ALU.mult))
                then()
                return g.tensor_tensor(x[:, :, :], x[:, :, :], norms[:, n + 1:n + 2, :].broadcast_to([P, NT, D]), ALU.add)

            def xn_step(b):
                if b == 0:
                    pool.wait_ge(ld_rest, 16 * 9)
                pool.wait_ge(xn_scaled, b + 1)
                affine(xn, 0).then_inc(xn_ready, 1)

            def shape_out(b):
                pool.wait_ge(shaped, b + 1)
                op(g.tensor_tensor(fa[:, :, :], fa[:, :, :], film[:, :, 3 * D:4 * D], ALU.add))
                then()
                g.tensor_tensor(xt[:, :, :], fa[:, :, :], x1[:, b % 2, :, :], ALU.add).then_inc(xt_ready, 1)

            def h_step(b):
                pool.wait_ge(h_scaled, b + 1)
                affine(fa, 2).then_inc(h_ready, 1)

            def ff_norm(b):
                pool.wait_ge(ff_scaled, b + 1)
                op(affine(fa, 4))
                then()
                g.tensor_tensor(fa[:, :, :], fa[:, :, :], x1[:, b % 2, :, :], ALU.add).then_inc(sum_ready, 1)

            def gates_step(b):
                pool.wait_ge(x2T_sb, b + 1)
                op(g.tensor_copy(t_hi[:, b, :], x2T[:, :]))
                then()
                g.tensor_tensor(t_lo[:, b, :], x2T[:, :], t_hi[:, b, :].bitcast(F32), ALU.subtract).then_inc(x2_split, 1)

            def nothing(*_):
                pass

            def args(q):
                if q < D // JM:
                    exponents(q)

            iterate({"args": args, "rope": rope_step, "proj": power, "x_norm": power, "xn": xn_step, "shape_out": shape_out,
                     "h_norm": power, "h": h_step, "ffT": power, "ff_norm": ff_norm, "x2_norm": power,
                     "gates": gates_step}, nothing, nothing, close, nothing)
            for b in range(B):
                power()

        @block.vector
        def _(dve):
            v = nc.vector
            count = [0]
            roots = [0]

            def op(ins):
                count[0] += 1
                ins.then_inc(dve_step, 1)

            def then():
                dve.wait_ge(dve_step, count[0])

            def one(ins):
                op(ins)
                then()

            def s(k):
                return sm[:, k, :]

            tt, ts, stt = v.tensor_tensor, v.tensor_scalar, v.scalar_tensor_tensor

            def fl(x):
                return x[:, :, :].rearrange("p d m -> p (d m)")

            def vectors():
                dve.wait_ge(ld_cross, 16 * 11)
                v.tensor_copy(tm_rows[:, :], tm_rows8[:, :]).then_inc(pro_sb, 1)
                op(v.tensor_copy(cmask[:, :], cmask8[:, :]))
                op(ts(gate4[:, :], gate[:, :], 0.25, None, ALU.mult))
                one(ts(film_bias[:, :], film_bias[:, :], gate[:, 0:1], None, ALU.mult))
                op(ts(cmask[:, :], cmask[:, :], 1.0, 3e38, ALU.subtract, ALU.mult))
                for n in range(2):
                    op(ts(film_bias[:, 2 * D * n:2 * D * n + D], film_bias[:, 2 * D * n:2 * D * n + D], 1.0, None, ALU.add))
                then()
                for h in range(XH):
                    op(ts(ctx_bias[:, :, h, :], cmask[:, :].rearrange("p (b g) -> p b g", b=B), 10.0, None, ALU.mult))
                op(tt(spread[:, :], ident[0:2 * NE, 0:NE], ident[0:2 * NE, NE:2 * NE], ALU.add))
                dve.wait_ge(pro_pe, 1)
                one(v.tensor_copy(vcols[:, :], bank_d[:, 0:ROWS]))
                one(tt(b2_shared[:, :], vcols[:, ROW_B2 + 1:ROW_B2 + 2], vcols[:, ROW_B2 + 2:ROW_B2 + 3], ALU.add))
                op(ts(b2_shared[:, :], b2_shared[:, :], 0.5, None, ALU.mult))
                one(v.memset(kbd[:, :], 0.0))

            def fold1():
                dve.wait_ge(pro_pe, 2)
                op(v.tensor_copy(wqT[:, :], bank_r[:, 0:P]))
                op(v.tensor_copy(tmask[:, :], bank_r[:, 3 * P:3 * P + B * NT]))
                one(v.tensor_copy(ctxT[:, :], bank_r[0:DV, P:2 * P]))
                v.tensor_copy(wvT[:, :], bank_r[:, 2 * P:2 * P + DV]).then_inc(pro_sb, 1)
                for h in range(XH):
                    op(v.tensor_copy(ctx_rep.rearrange("p b (h g) -> p b h g", h=XH)[:, :, h, :],
                                     ctxT[:, :].rearrange("p (b g) -> p b g", b=B)))

            def fold2():
                dve.wait_ge(pro_pe, 3)
                for h in range(XH):
                    last = v.tensor_copy(kbd[:, :].rearrange("p (b h g) -> p b h g", b=B, h=XH)[32 * h:32 * h + 32, :, h, :],
                                         ring_u[0][32 * h:32 * h + 32, 0:B * G].rearrange("p (b g) -> p b g", b=B))
                last.then_inc(pro_sb, 1)
                then()
                dve.wait_ge(pro_pe, 4)
                v.tensor_copy(wvf, ring_u[1][0:DV, :]).then_inc(pro_sb, 1)

            def fold3():
                dve.wait_ge(pro_pe, 5)
                v.tensor_copy(xq[:, :, :].rearrange("p b g -> p (b g)"), bank_d[:, :]).then_inc(pro_sb, 1)

            def fold4():
                for b in range(B):
                    dve.wait_ge(pro_pe, 6 + b)
                    op(ts(vf[:, b, :], (bank_r, ring_u[0], ring_u[1], bank_d)[b][:, :], gate4[:, 0:1], None, ALU.mult))

            def step_sizes():
                ldt = vcols[:, ROW_LDT:ROW_LDT + 1]
                c = lambda k: dtc[:, k:k + 1]
                dve.wait_ge(ld_s4, 16 * 7)
                one(ts(c(0), ldt, 1.4426950408889634, MAGIC, ALU.mult, ALU.add))
                one(ts(c(0), c(0), MAGIC, None, ALU.subtract))
                op(ts(c(4), c(0), 127.0, None, ALU.add))
                one(stt(out=c(1), in0=c(0), scalar=-LN2_HI, in1=ldt, op0=ALU.mult, op1=ALU.add))
                op(v.tensor_copy(dti[:, 0:1], c(4)))
                one(stt(out=c(2), in0=c(0), scalar=-LN2_LO, in1=c(1), op0=ALU.mult, op1=ALU.add))
                one(ts(dti[:, 1:2], dti[:, 0:1], 23, None, ALU.logical_shift_left))
                one(ts(c(3), c(2), 1.0 / 5040, 1.0 / 720, ALU.mult, ALU.add))
                for k in (1.0 / 120, 1.0 / 24, 1.0 / 6, 0.5, 1.0, 1.0):
                    one(ts(c(3), c(3), c(2), k, ALU.mult, ALU.add))
                one(tt(c(5), c(3), dti[:, 1:2].bitcast(F32), ALU.mult))
                op(ts(s(0), s4[:, 0, :], c(5), None, ALU.mult))
                one(ts(s(1), s4[:, 1, :], c(5), 1.0 / TWO_PI, ALU.mult, ALU.mult))
                one(ts(s(4), s(1), MAGIC, MAGIC, ALU.add, ALU.subtract))
                v.tensor_copy(packs[:, 0, 0:NS], s(0)).then_inc(pro_arg, 1)
                tt(s(4), s(1), s(4), ALU.subtract).then_inc(pro_arg, 1)

            def states():
                dve.wait_ge(pro_arg, 2)
                op(v.tensor_copy(packs[:, 0, NS:P], s(0)))
                op(v.tensor_copy(packs[:, 1, 0:NS], s(4)))
                op(v.tensor_copy(packs[:, 1, NS:P], s(4)))
                op(tt(s(9), s4[:, 0, :], s4[:, 0, :], ALU.mult))
                op(tt(s(10), s4[:, 1, :], s4[:, 1, :], ALU.mult))
                dve.wait_ge(pro_fun, 1)
                one(ts(s(6), s(2), -1.0, 1.0, ALU.mult, ALU.add))
                op(tt(s(9), s(9), s(10), ALU.add))
                one(v.reciprocal(s(6), s(6)))
                op(v.reciprocal(s(9), s(9)))
                one(tt(s(6), s(6), s(2), ALU.mult))
                one(ts(s(6), s(6), 2.0, None, ALU.mult))
                dve.wait_ge(pro_fun, 2)
                one(tt(s(3), s(3), s(3), ALU.mult))
                one(ts(s(3), s(3), -2.0, None, ALU.mult))
                op(ts(s(7), s(3), 1.0, None, ALU.add))
                one(ts(s(8), s(6), 1.0, None, ALU.add))
                op(tt(s(7), s(7), s(6), ALU.mult))
                one(tt(s(8), s(8), s(5), ALU.mult))
                one(tt(s(7), s(7), s(3), ALU.add))
                op(tt(s(0), s4[:, 2, :], s(7), ALU.mult))
                op(tt(s(1), s4[:, 3, :], s(8), ALU.mult))
                op(tt(s(2), s4[:, 2, :], s(8), ALU.mult))
                one(tt(s(3), s4[:, 3, :], s(7), ALU.mult))
                op(tt(s(0), s(0), s(1), ALU.subtract))
                one(tt(s(2), s(2), s(3), ALU.add))
                op(tt(s(5), s(0), s4[:, 0, :], ALU.mult))
                op(tt(s(6), s(2), s4[:, 1, :], ALU.mult))
                op(tt(s(7), s(2), s4[:, 0, :], ALU.mult))
                one(tt(s(8), s(0), s4[:, 1, :], ALU.mult))
                op(tt(s(5), s(5), s(6), ALU.add))
                one(tt(s(7), s(8), s(7), ALU.subtract))
                op(tt(packs[:, 2, 0:NS], s(5), s(9), ALU.mult))
                one(tt(packs[:, 3, 0:NS], s(7), s(9), ALU.mult))
                op(ts(packs[:, 2, NS:P], packs[:, 2, 0:NS], -1.0, None, ALU.mult))
                v.tensor_copy(packs[:, 3, NS:P], packs[:, 3, 0:NS]).then_inc(pro_sb, 1)

            def pack():
                dve.wait_ge(pro_pe, 10)
                one(v.tensor_copy(pk[:, :, :].rearrange("p n d -> p (n d)"), ring_u[0][:, :]))
                op(ts(pk32[:, 0, :], pk[:, 0, :], float(JM), None, ALU.mult))
                one(ts(pk32[:, 1, :], pk[:, 1, :], float(JM), None, ALU.mult))
                one(ts(pk32[:, 2, :], pk32[:, 1, :], MAGIC, MAGIC, ALU.add, ALU.subtract))
                one(tt(pk32[:, 1, :], pk32[:, 1, :], pk32[:, 2, :], ALU.subtract))

            def bc(x, q, m):
                return x[:, JM * q:JM * (q + 1)].unsqueeze(2).broadcast_to([P, JM, m])

            def ix(m):
                return index[:, 0:m].unsqueeze(1).broadcast_to([P, JM, m])

            def evacuate(q, h):
                d0 = JM * q + 16 * h
                return ts(kij[:, :, d0:d0 + 16].rearrange("i j d -> i d j"),
                          taps_ps[h][0:IM, :].rearrange("i (d j) -> i d j", j=JM), 2.0, None, ALU.mult)

            def args(q):
                if q < D // JM:
                    one(tt(pr[:, :, :], bc(pk[:, 1, :], q, JM), ix(JM), ALU.mult))
                    one(ts(fl(pt), fl(pr), offs[:, 0:1], MAGIC, ALU.add, ALU.add))
                    stt(out=fl(pt), in0=fl(pt), scalar=MAGIC, in1=fl(pr), op0=ALU.subtract, op1=ALU.subtract).then_inc(pro_arg, 1)
                    one(tt(ue[:, :, :], bc(pk32[:, 1, :], q, IM), ix(IM), ALU.mult))
                    one(ts(fl(ug), fl(ue), offs[:, 1:2], MAGIC, ALU.add, ALU.add))
                    op(stt(out=fl(ug), in0=fl(ug), scalar=MAGIC, in1=fl(ue), op0=ALU.subtract, op1=ALU.subtract))
                if q:
                    dve.wait_ge(pro_pe, 10 + q)
                if q < D // JM:
                    one(ts(fl(uf), fl(ue), offs[:, 0:1], MAGIC, ALU.add, ALU.add))
                    stt(out=fl(uf), in0=fl(uf), scalar=MAGIC, in1=fl(ue), op0=ALU.subtract, op1=ALU.subtract).then_inc(pro_arg, 1)
                if q:
                    op(evacuate(q - 1, 0))
                    last = evacuate(q - 1, 1)
                    if q == D // JM:
                        last.then_inc(kij_ready, 1)
                    else:
                        op(last)

            def powers(q):
                dve.wait_ge(pro_fun, 4 + 3 * q)
                op(tt(uf[:, :, :], uf[:, :, :], bc(pk[:, 2, :], q, IM), ALU.mult))
                one(tt(ug[:, :, :], ug[:, :, :], bc(pk[:, 3, :], q, IM), ALU.mult))
                one(tt(fl(uf), fl(uf), fl(ug), ALU.add))
                dve.wait_ge(pro_fun, 5 + 3 * q)
                op(tt(fl(pv), fl(pv), fl(pr), ALU.mult))
                tt(fl(uf), fl(uf), fl(ue), ALU.mult).then_inc(pro_sb, 1)

            def first_tap():
                dve.wait_ge(kld_landed, 16)
                tt(kld[0:1, 0, :], kld[0:1, 0, :], dskip[:, :], ALU.add).then_inc(kconst_ready, 1)

            def spectra():
                dve.wait_ge(pro_pe, 15)
                op(ts(fl(kc), ring_u[0][:, :], 2.0 / (2 * SEQ), None, ALU.mult))
                op(ts(fl(ks), ring_u[1][:, :], 2.0 / (2 * SEQ), None, ALU.mult))
                one(ts(fl(kcn), ring_u[0][:, :], 2.0 / (2 * SEQ), None, ALU.mult))
                op(ts(kc[0:1, 0, :], kc[0:1, 0, :], 0.5, None, ALU.mult))
                one(ts(kcn[0:1, 0, :], ks[0:1, 0, :], 0.5, None, ALU.mult))
                one(v.memset(ks[0:1, 0, :], 0.0))

            def text_weights():
                dve.wait_ge(ld_wt, 32)
                halves(wt_hi[:, :], wt_lo[:, :], wt_raw).then_inc(wt_split, 1)

            def norm_begin(src):
                for j in range(NT):
                    op(v.bn_stats(stats[:, j, :], src[:, j, :]))
                then()
                for j in range(NT):
                    op(v.bn_aggr(mean_var[:, j, :], stats[:, j, :]))
                then()
                ts(var_eps[:, :], mean_var[:, :, 1], EPS, None, ALU.add).then_inc(var_ready, 1)

            def norm_end(src, dst):
                roots[0] += 1
                dve.wait_ge(rstd_ready, roots[0])
                for j in range(NT):
                    last = ts(dst[:, j, :], src[:, j, :], mean_var[:, j, 0:1], rstd[:, j:j + 1], ALU.subtract, ALU.mult)
                    if j < NT - 1:
                        op(last)
                return last

            def norm(src, dst):
                norm_begin(src)
                return norm_end(src, dst)

            def halves(hi, lo, src):
                one(v.tensor_copy(hi, src))
                return tt(lo, src, hi.bitcast(F32), ALU.subtract)

            def rms(b):
                dve.wait_ge(s_free, fill_index(b, "qkv", n=1) + 1)
                qk = qkv[:, :, 0:QK]
                one(tt(tmp_c.rearrange("p (j c) -> p j c", j=NT), qk, qk, ALU.mult))
                one(v.tensor_reduce(rms_in[:, :], tmp_c.rearrange("p (n e) -> p n e", e=HD), AX, ALU.add))
                one(ts(rms_in[:, :], rms_in[:, :], 1.0 / HD, EPS, ALU.mult, ALU.add))
                one(ts(rms_bits, rms_in[:, :].bitcast(I32), 1, None, ALU.logical_shift_right))
                op(ts(rms_in[:, :], rms_in[:, :], -0.5, None, ALU.mult))
                one(v.tensor_copy(rms_tmp[:, :], rms_bits))
                one(ts(rms_tmp[:, :], rms_tmp[:, :], -1.0, float(0x5F3759DF), ALU.mult, ALU.add))
                one(v.tensor_copy(rms_bits, rms_tmp[:, :]))
                y = rms_out[:, :]
                for k in range(4):
                    one(tt(rms_tmp[:, :], y, y, ALU.mult))
                    one(tt(rms_tmp[:, :], rms_tmp[:, :], rms_in[:, :], ALU.mult))
                    last = stt(out=rms_out[:, :], in0=rms_tmp[:, :], scalar=1.5, in1=y, op0=ALU.add, op1=ALU.mult)
                    if k < 3:
                        one(last)
                last.then_inc(rms_ready, 1)

            def parts_step(b):
                heads = NH + NKV
                dve.wait_ge(roped, b + 1)
                if b:
                    dve.wait_ge(s_full, fill_index(b - 1, "qT", n=5) + 1)
                qk = qkv[:, :, 0:QK].rearrange("p j (h e) -> p j h e", h=heads)
                q4, k4 = qk[:, :, 0:NH, :], qk[:, :, NH:heads, :]
                qp = lambda c: qs[:, :, c, :].rearrange("p (j h) e -> p j h e", j=NT)
                kp = lambda c: k_parts[:, :, 0, c, :].rearrange("p (j h) e -> p j h e", j=NT)
                op(v.tensor_copy(qp(0), q4))
                one(v.tensor_copy(kp(0), k4))
                op(tt(q4, q4, qp(0), ALU.subtract))
                one(tt(k4, k4, kp(0), ALU.subtract))
                op(v.tensor_copy(qp(3), q4))
                one(v.tensor_copy(kp(1), k4))
                op(tt(qp(6), q4, qp(3), ALU.subtract))
                one(tt(kp(2), k4, kp(1), ALU.subtract))
                for src, dsts in ((0, (1, 2)), (3, (4, 5)), (6, (7,))):
                    op(v.tensor_copy(qs[:, :, dsts[0]:dsts[-1] + 1, :],
                                     qs[:, :, src:src + 1, :].broadcast_to([P, NT * NH, len(dsts), HD])))
                for src, dsts in ((0, (3, 6)), (1, (4, 7)), (2, (5,))):
                    for d in dsts:
                        op(v.tensor_copy(k_parts[:, :, 0, d, :], k_parts[:, :, 0, src, :]))
                then()
                v.tensor_copy(k_parts[:, :, 1, :, :].rearrange("p n c e -> p n (c e)"),
                              k_parts[:, :, 0, :, :].rearrange("p n c e -> p n (c e)")).then_inc(parts_ready, 1)

            def close(i, p):
                pair = i * NPAIR + p - 1
                if 0 <= pair < B * NPAIR:
                    dve.wait_ge(pv_done, pair + 1)
                    if pair >= 2:
                        dve.wait_ge(y_ps, pair - 1)
                    op(v.tensor_copy(oT[0:64, pair % 2, :], bank_o[0:64, :]))
                    v.tensor_copy(oT[64:P, pair % 2, P:SEQ], bank_o[64:P, P:SEQ]).then_inc(oT_ready, 1)
                if p == 0 and i < B:
                    dve.wait_ge(consts_ready, 1)
                    v.tensor_copy(vv[:, :, :, 0:HD], qkv[:, :, QK:QKV].rearrange("p j (g e) -> p j g e", g=NKV)).then_inc(v_ready, 1)

            def tokens(i, p):
                pair = i * NPAIR + p - 2
                if 0 <= pair < B * NPAIR:
                    q = pair % NPAIR
                    dve.wait_ge(y_ps, pair + 1)
                    ys = bank_m[:, 256 * (q % 2):256 * (q % 2 + 1)].rearrange("p (j h e) -> p j h e", j=NT, h=2)
                    one(v.reciprocal(ry[:, :, :], ys[:, :, :, HD]))
                    tt(y_att[:, :, 2 * HD * q:2 * HD * (q + 1)].rearrange("p j (h e) -> p j h e", h=2), ys[:, :, :, 0:HD],
                       ry[:, :, :].unsqueeze(3).broadcast_to([P, NT, 2, HD]), ALU.mult).then_inc(y_ready, 1)

            def yT_step(b):
                dve.wait_ge(yT_ps, b + 1)
                v.tensor_copy(yT[:, :], bank_m[:, :]).then_inc(yT_sb, 1)

            def proj(b):
                dve.wait_ge(proj_ps, b + 1)
                tt(fl(xt), bank_o[:, :], x_in[:, b % 2, :, :].rearrange("p j d -> p (j d)"), ALU.add).then_inc(x_used, 1)
                dve.wait_ge(x_used, b + 1)
                norm_begin(xt)

            def x1_step(b):
                norm_end(xt, x1[:, b % 2, :, :]).then_inc(x1_ready, 1)

            def scores(b):
                dve.wait_ge(sc_ps, b + 1)
                d4 = bank_d[:, :].rearrange("p (j c) -> p j c", j=NT)
                s4v = fl(sc).rearrange("p (j c) -> p j c", j=NT)
                one(stt(out=s4v, in0=d4, scalar=1.0 / float(np.sqrt(np.float32(XD))),
                        in1=ctx_bias[:, b:b + 1].rearrange("p b h g -> p b (h g)").broadcast_to([P, NT, XH * G]),
                        op0=ALU.mult, op1=ALU.add))
                one(v.tensor_reduce(sc_max[:, :], sc[:, :, :], AX, ALU.max))
                tt(sc[:, :, :], sc[:, :, :], sc_max[:, :].unsqueeze(2).broadcast_to([P, NT * XH, G]), ALU.subtract).then_inc(sc_ready, 1)

            def x_norm(b):
                dve.wait_ge(x1_ready, b + 1)
                norm_begin(x1[:, b % 2, :, :])

            def xn_step(b):
                norm_end(x1[:, b % 2, :, :], xn).then_inc(xn_scaled, 1)

            def soften(b):
                dve.wait_ge(sc_exp, b + 1)
                one(v.tensor_reduce(sc_sum[:, :], sc[:, :, :], AX, ALU.add))
                one(v.reciprocal(sc_sum[:, :], sc_sum[:, :]))
                one(tt(sc_sum[:, :].rearrange("p (j h) -> p j h", j=NT), sc_sum[:, :].rearrange("p (j h) -> p j h", j=NT),
                       tmask[:, NT * b:NT * (b + 1)].unsqueeze(2).broadcast_to([P, NT, XH]), ALU.mult))
                tt(sc[:, :, :], sc[:, :, :], sc_sum[:, :].unsqueeze(2).broadcast_to([P, NT * XH, G]), ALU.mult).then_inc(attn_ready, 1)

            def film_step(b, j):
                dve.wait_ge(u_full, b * U_FILLS + U_FILM + j + 1)
                tt(film[:, j, :], ring_u[j % 2][:, :], film_bias[:, :], ALU.add).then_inc(u_free, 1)

            def modulate(b):
                dve.wait_ge(u_free, b * U_FILLS + NT)
                dve.wait_ge(xn_ready, b + 1)
                one(tt(xn[:, :, :], xn[:, :, :], film[:, :, 0:D], ALU.mult))
                tt(xn[:, :, :], xn[:, :, :], film[:, :, D:2 * D], ALU.add).then_inc(xmod_ready, 1)

            def spectrum(b):
                dve.wait_ge(u_full, b * U_FILLS + U_DFT + 2)
                re, im = ring_u[0][:, :], ring_u[1][:, :]
                lo = spec[:, 0:NT, :].rearrange("p n d -> p (n d)")
                hi = spec[:, NT:2 * NT, :].rearrange("p n d -> p (n d)")
                op(tt(lo, re, fl(kc), ALU.mult))
                op(tt(fl(xn), im, fl(ks), ALU.mult))
                tt(hi, re, fl(ks), ALU.mult).then_inc(u_free, 1)
                tt(fl(fb), im, fl(kcn), ALU.mult).then_inc(u_free, 1)
                then()
                dve.wait_ge(u_free, U_FILLS * (b + 1))
                one(tt(lo, lo, fl(xn), ALU.subtract))
                tt(hi, hi, fl(fb), ALU.add).then_inc(spec_ready, 1)

            def shape_out(b):
                dve.wait_ge(conv_ps, b + 1)
                tt(fa[:, :, :], bank_d[:, :].rearrange("p (j d) -> p j d", j=NT), film[:, :, 2 * D:3 * D], ALU.mult).then_inc(shaped, 1)

            def h_norm(b):
                dve.wait_ge(xt_ready, b + 1)
                norm_begin(xt)

            def h_step(b):
                norm_end(xt, fa).then_inc(h_scaled, 1)

            def hT_step(b):
                dve.wait_ge(hT_ps, b + 1)
                halves(t_hi[:, b, :], t_lo[:, b, :], bank_r[:, :]).then_inc(hT_sb, 1)

            def split_hidden(b):
                for n in range(HC):
                    dve.wait_ge(gelu_done, b * HC + n + 1)
                    halves(g_hi[:, n, :], g_lo[:, n, :], g_raw[:, n, :]).then_inc(split_done, 1)

            def ffT_step(b):
                dve.wait_ge(ffn_tok, b + 1)
                tt(fl(xt), bank_r[:, :], fl(xt), ALU.add).then_inc(tok_used, 1)
                dve.wait_ge(tok_used, b + 1)
                norm_begin(xt)

            def ff_norm(b):
                norm_end(xt, fa).then_inc(ff_scaled, 1)

            def x2_norm(b):
                dve.wait_ge(sum_ready, b + 1)
                norm_begin(fa)

            def x2_step(b):
                norm_end(fa, x2[:, b, :].rearrange("p (j d) -> p j d", j=NT)).then_inc(x2_ready, 1)

            def gates_step(b):
                dve.wait_ge(gates_ps, b + 1)
                one(tt(gates[:, :, :], bank_r[:, 0:NT * NE].rearrange("p (j e) -> p j e", j=NT),
                       router_b[:, :].unsqueeze(1).broadcast_to([P, NT, NE]), ALU.add))
                one(v.tensor_reduce(gmax[:, :], gates[:, :, :], AX, ALU.max))
                tt(w_tok[:, :, :], gates[:, :, :], gmax[:, :].unsqueeze(2).broadcast_to([P, NT, NE]), ALU.subtract).then_inc(gates_ready, 1)

            def route(b):
                other = gates[:, :, :].unsqueeze(2).broadcast_to([P, NT, NE, NE])
                own = gates[:, :, :].unsqueeze(3).broadcast_to([P, NT, NE, NE])
                op(tt(cmp_a[:, :, :, :], other, own, ALU.is_gt))
                one(tt(cmp_b[:, :, :, :], other, own, ALU.is_equal))
                one(tt(cmp_b[:, :, :, :], cmp_b[:, :, :, :], earlier[:, :, :].unsqueeze(1).broadcast_to([P, NT, NE, NE]), ALU.mult))
                one(tt(cmp_a[:, :, :, :], cmp_a[:, :, :, :], cmp_b[:, :, :, :], ALU.add))
                one(v.tensor_reduce(chosen[:, :, :], cmp_a[:, :, :, :], AX, ALU.add))
                one(ts(chosen[:, :, :], chosen[:, :, :], 2.0, None, ALU.is_lt))
                dve.wait_ge(gates_exp, b + 1)
                one(tt(w_tok[:, :, :], w_tok[:, :, :], chosen[:, :, :], ALU.mult))
                one(v.tensor_reduce(gmax[:, :], w_tok[:, :, :], AX, ALU.add))
                one(v.reciprocal(gmax[:, :], gmax[:, :]))
                one(tt(w_tok[:, :, :], w_tok[:, :, :], gmax[:, :].unsqueeze(2).broadcast_to([P, NT, NE]), ALU.mult))
                one(v.tensor_copy(w_round[:, :, :], w_tok[:, :, :]))
                op(v.tensor_copy(w_parts[:, :, 0:NE], w_round[:, :, :].bitcast(F32)))
                tt(w_parts[:, :, NE:2 * NE], w_tok[:, :, :], w_round[:, :, :].bitcast(F32), ALU.subtract).then_inc(wtok_ready, 1)

            def wT_step(b):
                dve.wait_ge(wT_ps, b + 1)
                v.tensor_copy(wT[:, b, :], bank_r[0:2 * NE, :]).then_inc(wT_sb, 1)

            def settle(q):
                e, b = PRODUCTS[q]
                dve.wait_ge(e_down, HC * (q + 1))
                if q >= 1:
                    dve.wait_ge(settled, q)
                bank = down[q % 2][:, :]
                if e == 0:
                    ts(acc[:, b, :], bank, 1.0 / NSH, b2_shared[:, 0:1], ALU.mult, ALU.add).then_inc(settled, 1)
                elif e < NSH:
                    stt(out=acc[:, b, :], in0=bank, scalar=1.0 / NSH, in1=acc[:, b, :], op0=ALU.mult, op1=ALU.add).then_inc(settled, 1)
                else:
                    r, k = ROUTED.index(q), ROW_B2 + 1 + e
                    dve.wait_ge(bc_sb, r + 1)
                    one(stt(out=term[:, :], in0=bank, scalar=vcols[:, k:k + 1], in1=w_bc[:, r % 2, :], op0=ALU.add, op1=ALU.mult))
                    tt(acc[:, b, :], acc[:, b, :], term[:, :], ALU.add).then_inc(settled, 1)

            def split_weights(e):
                dve.wait_ge(ld_w, 32 * (e + 1))
                halves(w_hi[:, e % SLOTS, :], w_lo[:, e % SLOTS, :], e_raw[:, :]).then_inc(w_split, 1)

            def chunk(c):
                if c >= CHUNKS:
                    return
                (e, b), n = PRODUCTS[c // HC], c % HC
                q = c // HC
                if c == 0:
                    split_weights(0)
                dve.wait_ge(e_gelu, c + 1)
                if c >= HC:
                    dve.wait_ge(e_down, c - HC + 1)
                if n == HC - 1:
                    one(v.tensor_copy(eg_hi[:, n, :], eg_raw[:, c % SLOTS, :]))
                tt(eg_lo[:, n, :], eg_raw[:, c % SLOTS, :], eg_hi[:, n, :].bitcast(F32), ALU.subtract).then_inc(e_split, 1)
                if n == LAG and q:
                    settle(q - 1)
                for k, at in SPLIT_BEHIND.items():
                    if c == at:
                        split_weights(k)

            def final(b):
                dve.wait_ge(accT_ps, b + 1)
                tt(fl(fa), bank_d[:, :], x2[:, b, :], ALU.add).then_inc(acc_used, 1)
                dve.wait_ge(acc_used, b + 1)
                norm(fa, x2[:, b, :].rearrange("p (j d) -> p j d", j=NT)).then_inc(y_out_ready, 1)

            def moe():
                for c in range(EARLY, CHUNKS + 1):
                    chunk(c)
                    for b in range(B - 1):
                        if c == FINAL_AT[b]:
                            final(b)
                settle(NM * B - 1)
                final(B - 1)

            def nothing(*_):
                pass

            op(v.memset(oT[64:P, :, 0:P], 0.0))
            iterate({"vectors": vectors, "fold1": fold1, "fold2": fold2, "fold3": fold3, "vf": fold4,
                     "steps": step_sizes, "states": states, "pack": pack, "args": args, "powers": powers, "first_tap": first_tap,
                     "spectra": spectra, "text_weights": text_weights, "rms": rms, "parts": parts_step, "yT": yT_step,
                     "proj": proj, "scores": scores, "x_norm": x_norm, "soften": soften, "film": film_step,
                     "modulate": modulate, "spectrum": spectrum, "shape_out": shape_out, "hT": hT_step,
                     "gelu": split_hidden, "ffT": ffT_step, "ff_norm": ff_norm, "x2": x2_step, "gates": gates_step,
                     "route": route, "wT": wT_step, "chunk": chunk, "x1": x1_step, "xn": xn_step,
                     "h_norm": h_norm, "h": h_step, "x2_norm": x2_norm}, nothing, nothing, close, tokens)
            moe()


_INS = ["x", "ctx_768", "mask_BxS_bf1", "mask_BxS2_bf1", "L0_attn_w_q", "L0_attn_w_k", "L0_attn_w_v", "L0_attn_w_o",
        "L0_xattn_Wq", "L0_xattn_Wk", "L0_xattn_Wv", "L0_xattn_W_film_in", "L0_xattn_b_film_in", "L0_xattn_W_film_out",
        "L0_xattn_b_film_out", "L0_xattn_g_norm_in", "L0_xattn_b_norm_in", "L0_xattn_g_norm_out",
        "L0_xattn_b_norm_out", "L0_xattn_g_ffn", "L0_xattn_b_ffn", "L0_xattn_W1", "L0_xattn_b1", "L0_xattn_W2",
        "L0_xattn_b2", "L0_xattn_log_dt", "L0_xattn_A_re", "L0_xattn_A_im", "L0_xattn_C_re", "L0_xattn_C_im",
        "L0_xattn_D_skip", "L0_xattn_mod_gate", "L0_ffn_rW", "L0_ffn_rb", "L0_ffn_W1", "L0_ffn_b1", "L0_ffn_W2",
        "L0_ffn_b2", "L0_ffn_sW1", "L0_ffn_sb1", "L0_ffn_sW2", "L0_ffn_sb2"]


def constants():
    n = np.arange(SEQ)
    turn = 2 * np.pi * np.outer(n, n) / (2 * SEQ)
    alternate = (-1.0) ** n
    sin_fwd, sin_inv = np.sin(turn), np.sin(turn)
    sin_fwd[:, 0] = alternate
    sin_inv[0, :] = alternate
    freq = 1.0 / 10000.0 ** (np.arange(0, HD, 2, dtype=np.float32) / np.float32(HD))
    angle = (n.astype(np.float32)[:, None] * freq.astype(np.float32)[None, :]).astype(np.float64)
    c, s = np.cos(angle), np.sin(angle)
    rope = np.stack([np.concatenate([c, c], 1), np.concatenate([-s, s], 1)], 1)
    rope = rope.reshape(NT, P, 2, HD).transpose(1, 0, 2, 3).reshape(P, -1)
    offs = np.zeros((P, 4))
    offs[:NS, 0], offs[NS:, 1] = 0.25, 0.25
    offs[:, 2:4] = offs[:, 0:2] * SIN_SCALE
    pair_sum = np.tile(np.eye(64), (2, 1))
    earlier = (np.arange(NE)[None, :] < np.arange(NE)[:, None]).astype(np.float32).reshape(-1)
    tables = dict(c_cos=np.cos(turn), c_sin_fwd=sin_fwd, c_sin_inv=sin_inv, c_rope=rope, c_offs=offs,
                  c_pair_sum=pair_sum, c_earlier=earlier, c_ident=np.eye(P), c_index=np.arange(JM))
    return {k: np.ascontiguousarray(v, dtype=np.float32) for k, v in tables.items()}


def kernel(**inputs):
    import numpy as _np
    import concourse.bacc as _bacc
    from concourse import mybir as _mybir
    from concourse.bass_utils import run_bass_kernel_spmd as _run

    nc = _bacc.Bacc("TRN2", target_bir_lowering=False, num_devices=1)
    arrays, args = {}, {}
    for name in _INS:
        a = _np.ascontiguousarray(inputs[name])
        if a.ndim == 0:
            a = a.reshape(1)
        arrays[f"in_{name}"] = a
    for name, a in constants().items():
        arrays[f"in_{name}"] = a
    for name, a in arrays.items():
        args[name[3:]] = nc.dram_tensor(name, a.shape, _mybir.dt.from_np(a.dtype), kind="ExternalInput").ap()
    out = nc.dram_tensor("out_0", (B, SEQ, D), F32, kind="ExternalOutput").ap()
    build(nc, args, out)
    r = _run(nc, [arrays], core_ids=[0])
    return r.results[0]["out_0"]
```
